# Optimizing a Trainium2 kernel written in Bass

```python
import numpy as np
import jax
import jax.numpy as jnp

def _softmax(x, axis=-1):
    return jax.nn.softmax(x, axis=axis)

def _gelu(x):
    return jax.nn.gelu(x, approximate=True)

def _silu(x):
    return jax.nn.silu(x)

def _sigmoid(x):
    return jax.nn.sigmoid(x)

def _layernorm(x, axis=-1, eps=1e-05):
    m = jnp.mean(x, axis=axis, keepdims=True)
    v = jnp.var(x, axis=axis, keepdims=True)
    return (x - m) / jnp.sqrt(v + eps)

def _scatter_add(tgt, idx, src, axis=0):
    return tgt.at[idx].add(src)

def _segment_sum(src, seg, n):
    return jax.ops.segment_sum(src, seg, n)
kernel_name = 'mk_sandwich_d4_jaxref_r8_8e1ae6'

def setup_inputs(seed: int=0):
    np.random.seed(seed)
    _w = jnp.asarray

    def _L0_attn_setup():
        import jax, jax.numpy as jnp
        import numpy as np
        N_HEAD = 16
        FUTURE_DIM = 4

        def _layernorm(x, g, b, eps=1e-05):
            mu = jnp.mean(x, axis=-1, keepdims=True)
            var = jnp.mean(jnp.square(x - mu), axis=-1, keepdims=True)
            return (x - mu) * jax.lax.rsqrt(var + eps) * g + b

        def _future_attn_head(h, W_qkvf, W_conv, W_proj):
            B, T, D = h.shape
            H, hs, F = (N_HEAD, D // N_HEAD, FUTURE_DIM)
            NEG = jnp.float32(-jnp.inf)
            qkvf = h @ W_qkvf.T
            q, k, v, f = jnp.split(qkvf, 4, axis=-1)
            to_h = lambda t: t.reshape(B, T, H, hs).transpose(0, 2, 1, 3)
            q, k, v, f = (to_h(q), to_h(k), to_h(v), to_h(f))
            attn = jnp.einsum('bhtd,bhsd->bhts', q, k) * hs ** (-0.5)
            rows = jnp.arange(T)[:, None]
            causal_mask = jnp.arange(T)[None, :] <= rows
            causal_attn = jnp.where(causal_mask, attn, 0.0)
            padded_causal = jnp.pad(causal_attn, ((0, 0), (0, 0), (0, 0), (0, F)))
            up_future = jnp.einsum('bhtc,cdf->btfhd', f, W_conv).reshape(B, T, F, D)
            k_future = jnp.einsum('btfc,dc->btfd', up_future, W_qkvf[D:2 * D])
            k_future = k_future.reshape(B, T, F, H, hs).transpose(0, 3, 1, 2, 4)
            future_attention = jnp.einsum('bhtd,bhtfd->bhtf', q, k_future)
            cols_f = rows + 1 + jnp.arange(F)[None, :]
            full_attn = padded_causal.at[:, :, rows, cols_f].set(future_attention)
            full_mask = jnp.arange(T + F)[None, :] <= rows + F
            full_attn = jnp.where(full_mask, full_attn, NEG)
            sm = jax.nn.softmax(full_attn, axis=-1)
            sm_causal = jnp.where(causal_mask, sm[..., :T], 0.0)
            unpadded_future = sm[:, :, rows, cols_f]
            v_future = jnp.einsum('btfc,dc->btfd', up_future, W_qkvf[2 * D:3 * D])
            v_future = v_future.reshape(B, T, F, H, hs).transpose(0, 3, 1, 2, 4)
            future_x = jnp.einsum('bhtf,bhtfd->bhtd', unpadded_future, v_future)
            causal_x = jnp.einsum('bhts,bhsd->bhtd', sm_causal, v)
            new_x = (causal_x + future_x).transpose(0, 2, 1, 3).reshape(B, T, D)
            return new_x @ W_proj.T
        key = jax.random.key(seed)
        ks = jax.random.split(key, 7)
        B, T, D, H, F = (2, 128, 128, N_HEAD, FUTURE_DIM)
        hs = D // H
        s = 0.02
        return {'x': jax.random.normal(ks[0], (B, T, D), jnp.float32), 'W_qkvf': jax.random.normal(ks[1], (4 * D, D), jnp.float32) * s, 'W_conv': jax.random.normal(ks[2], (hs, hs, F), jnp.float32) * s, 'W_proj': jax.random.normal(ks[3], (D, D), jnp.float32) * s, 'W_ff1': jax.random.normal(ks[4], (D, 4 * D), jnp.float32) * s, 'W_ff2': jax.random.normal(ks[5], (4 * D, D), jnp.float32) * s, 'ln1_g': jnp.ones((D,), jnp.float32), 'ln1_b': jnp.zeros((D,), jnp.float32), 'ln2_g': jnp.ones((D,), jnp.float32), 'ln2_b': jnp.zeros((D,), jnp.float32)}
    _L0_attn_in = _L0_attn_setup()

    def _L0_ffn_setup():
        import jax, jax.numpy as jnp
        import numpy as np
        DIM = 128
        DEPTH = 2
        HEADS = 8
        DIM_HEAD = 64
        WINDOW = 64
        INNER = HEADS * DIM_HEAD
        HID = int(DIM * 4 * 2 / 3)
        B, N = (2, 1024)
        QK_SCALE = 8.0

        def shift_token(t):
            t1, t2 = jnp.split(t, 2, axis=-1)
            t2 = jnp.pad(t2, ((0, 0), (1, 0), (0, 0)))[:, :-1]
            return jnp.concatenate([t1, t2], axis=-1)

        def l2norm(t):
            return t / jnp.clip(jnp.linalg.norm(t, axis=-1, keepdims=True), 1e-12)

        def rotate_half(x):
            x1, x2 = jnp.split(x, 2, axis=-1)
            return jnp.concatenate([-x2, x1], axis=-1)

        def rotary_xpos(q, k):
            n = q.shape[-2]
            half_idx = jnp.arange(0, DIM_HEAD, 2, dtype=jnp.float32)
            inv_freq = 1.0 / 10000.0 ** (half_idx / DIM_HEAD)
            t = jnp.arange(n, dtype=jnp.float32)
            freqs = t[:, None] * inv_freq[None, :]
            freqs = jnp.concatenate([freqs, freqs], axis=-1)
            base = (half_idx + 0.4 * DIM_HEAD) / (1.4 * DIM_HEAD)
            power = (t - n // 2) / float(WINDOW // 2)
            scale = base[None, :] ** power[:, None]
            scale = jnp.concatenate([scale, scale], axis=-1)
            cos, sin = (jnp.cos(freqs), jnp.sin(freqs))
            q = q * cos * scale + rotate_half(q) * sin * scale
            k = k * cos / scale + rotate_half(k) * sin / scale
            return (q, k)

        def local_attention(q, k, v):
            b, h, n, d = q.shape
            w = n // WINDOW
            bq = q.reshape(b, h, w, WINDOW, d) * QK_SCALE
            bk = k.reshape(b, h, w, WINDOW, d)
            bv = v.reshape(b, h, w, WINDOW, d)

            def look_around(t):
                p = jnp.pad(t, ((0, 0), (0, 0), (1, 0), (0, 0), (0, 0)))
                return jnp.concatenate([p[:, :, :w], p[:, :, 1:]], axis=3)
            bk, bv = (look_around(bk), look_around(bv))
            bt = jnp.arange(n).reshape(w, WINDOW)
            btp = jnp.pad(bt, ((1, 0), (0, 0)), constant_values=-1)
            btk = jnp.concatenate([btp[:w], btp[1:]], axis=1)
            sim = jnp.einsum('bhwid,bhwjd->bhwij', bq, bk)
            i = bt[:, :, None]
            j = btk[:, None, :]
            mask = (i < j) | (i > j + WINDOW) | (j == -1)
            sim = jnp.where(mask, -jnp.finfo(sim.dtype).max, sim)
            attn = jax.nn.softmax(sim, axis=-1)
            out = jnp.einsum('bhwij,bhwjd->bhwid', attn, bv)
            return out.reshape(b, h, n, d)

        def _layer(x, wqkv, qs, ksc, wo, lg, lb, w1, b1, w2, b2):
            b, n, _ = x.shape
            h = shift_token(x)
            qkv = h @ wqkv
            q, k, v = jnp.split(qkv, 3, axis=-1)
            to_heads = lambda t: t.reshape(b, n, HEADS, DIM_HEAD).transpose(0, 2, 1, 3)
            q, k, v = (to_heads(q), to_heads(k), to_heads(v))
            q = l2norm(q) * qs
            k = l2norm(k) * ksc
            q, k = rotary_xpos(q, k)
            o = local_attention(q, k, v)
            o = o.transpose(0, 2, 1, 3).reshape(b, n, INNER)
            x = x + o @ wo
            h = shift_token(x)
            mu = h.mean(-1, keepdims=True)
            var = h.var(-1, keepdims=True)
            h = (h - mu) / jnp.sqrt(var + 1e-05) * lg + lb
            h = h @ w1 + b1
            a, g = jnp.split(h, 2, axis=-1)
            h = a * jax.nn.gelu(g, approximate=False)
            x = x + h @ w2 + b2
            return x
        key = jax.random.key(seed)
        ks = jax.random.split(key, 6)
        return {'x': jax.random.normal(ks[0], (B, N, DIM), jnp.float32), 'wqkv': jax.random.normal(ks[1], (DEPTH, DIM, 3 * INNER), jnp.float32) * 0.02, 'q_scale': jnp.ones((DEPTH, DIM_HEAD), jnp.float32), 'k_scale': jnp.ones((DEPTH, DIM_HEAD), jnp.float32), 'wo': jax.random.normal(ks[2], (DEPTH, INNER, DIM), jnp.float32) * 0.02, 'ln_g': jnp.ones((DEPTH, DIM), jnp.float32), 'ln_b': jnp.zeros((DEPTH, DIM), jnp.float32), 'w1': jax.random.normal(ks[3], (DEPTH, DIM, 2 * HID), jnp.float32) * 0.02, 'b1': jnp.zeros((DEPTH, 2 * HID), jnp.float32), 'w2': jax.random.normal(ks[4], (DEPTH, HID, DIM), jnp.float32) * 0.02, 'b2': jnp.zeros((DEPTH, DIM), jnp.float32)}
    _L0_ffn_in = _L0_ffn_setup()

    def _L1_attn_setup():
        import math
        import jax, jax.numpy as jnp
        import numpy as np
        B, S, E, H = (4, 256, 128, 16)
        HD = E // H
        key = jax.random.key(seed)
        ks = jax.random.split(key, 7)
        scale = 1.0 / math.sqrt(E)
        return {'x': jax.random.normal(ks[0], (B, S, E), dtype=jnp.float32), 'Wq': jax.random.normal(ks[1], (H, HD, E), dtype=jnp.float32) * scale, 'bq': jax.random.normal(ks[2], (H, HD), dtype=jnp.float32) * 0.01, 'Wk': jax.random.normal(ks[3], (H, HD, E), dtype=jnp.float32) * scale, 'bk': jax.random.normal(ks[4], (H, HD), dtype=jnp.float32) * 0.01, 'Wv': jax.random.normal(ks[5], (H, HD, E), dtype=jnp.float32) * scale, 'bv': jax.random.normal(ks[6], (H, HD), dtype=jnp.float32) * 0.01}
    _L1_attn_in = _L1_attn_setup()

    def _L1_ffn_setup():
        import jax, jax.numpy as jnp
        import numpy as np
        D_IN, D_HID = (128, 512)

        def _ternary(key, shape):
            return jax.random.randint(key, shape, -1, 2).astype(jnp.float32)

        def _tlin(x, w, s):
            return jnp.einsum('bsi,oi->bso', x, w) * s
        key = jax.random.key(seed)
        ks = jax.random.split(key, 12)
        inv = lambda fan: 1.0 / np.sqrt(fan).astype(np.float32)
        return {'x': jax.random.normal(ks[0], (4, 256, D_IN), dtype=jnp.float32), 'w1_w': _ternary(ks[1], (D_HID, D_IN)), 'w1_s': jax.random.uniform(ks[2], (D_HID,), dtype=jnp.float32) * inv(D_IN), 'w2_w': _ternary(ks[3], (D_HID, D_IN)), 'w2_s': jax.random.uniform(ks[4], (D_HID,), dtype=jnp.float32) * inv(D_IN), 'h1_w': _ternary(ks[5], (D_HID, D_HID)), 'h1_s': jax.random.uniform(ks[6], (D_HID,), dtype=jnp.float32) * inv(D_HID), 'h2_w': _ternary(ks[7], (D_HID, D_HID)), 'h2_s': jax.random.uniform(ks[8], (D_HID,), dtype=jnp.float32) * inv(D_HID), 'w3_w': _ternary(ks[9], (D_IN, D_HID)), 'w3_s': jax.random.uniform(ks[10], (D_IN,), dtype=jnp.float32) * inv(D_HID)}
    _L1_ffn_in = _L1_ffn_setup()

    def _L2_attn_setup():
        import jax, jax.numpy as jnp
        import numpy as np
        B, S, H, NH = (4, 128, 128, 16)
        HD = H // NH
        CAUSAL_HEADS = 4
        META_HEADS = NH // 4
        CAUSAL_W = 0.7
        META_W = (0.9 - 0.8) / 0.2 * 0.3

        def _mha(xq, xkv, Win, bi, Wout, bout, nh):
            b, sq, h = xq.shape
            sk = xkv.shape[1]
            hd = h // nh
            q = (xq @ Win[:, :h] + bi[:h]).reshape(b, sq, nh, hd).transpose(0, 2, 1, 3)
            k = (xkv @ Win[:, h:2 * h] + bi[h:2 * h]).reshape(b, sk, nh, hd).transpose(0, 2, 1, 3)
            v = (xkv @ Win[:, 2 * h:] + bi[2 * h:]).reshape(b, sk, nh, hd).transpose(0, 2, 1, 3)
            scores = jnp.einsum('bhqd,bhkd->bhqk', q, k) / jnp.sqrt(jnp.asarray(hd, q.dtype))
            probs = jax.nn.softmax(scores, axis=-1)
            ctx = jnp.einsum('bhqk,bhkd->bhqd', probs, v)
            return ctx.transpose(0, 2, 1, 3).reshape(b, sq, h) @ Wout + bout

        def _forward(hidden_states, cons_vec, Wq, bq, Wk, bk, Wv, bv, cg_W, cg_b, am_W, am_b, ca_Win, ca_bin, ca_Wout, ca_bout, mc_Win, mc_bin, mc_Wout, mc_bout, Wo, bo):
            b, s, h = hidden_states.shape
            q = (hidden_states @ Wq + bq).reshape(b, s, NH, HD).transpose(0, 2, 1, 3)
            k = (hidden_states @ Wk + bk).reshape(b, s, NH, HD).transpose(0, 2, 1, 3)
            v = (hidden_states @ Wv + bv).reshape(b, s, NH, HD).transpose(0, 2, 1, 3)
            scores = jnp.einsum('bhqd,bhkd->bhqk', q, k) / jnp.sqrt(jnp.asarray(HD, q.dtype))
            mod = jax.nn.sigmoid(hidden_states @ cg_W + cg_b + (cons_vec @ am_W + am_b))
            scores = scores * mod.transpose(0, 2, 1)[..., None]
            probs = jax.nn.softmax(scores, axis=-1)
            ctx = jnp.einsum('bhqk,bhkd->bhqd', probs, v).transpose(0, 2, 1, 3).reshape(b, s, h)
            causal_ctx = _mha(hidden_states, hidden_states, ca_Win, ca_bin, ca_Wout, ca_bout, CAUSAL_HEADS)
            ctx = ctx * (1.0 - CAUSAL_W) + causal_ctx * CAUSAL_W
            meta_ctx = _mha(ctx, ctx, mc_Win, mc_bin, mc_Wout, mc_bout, META_HEADS)
            ctx = ctx * (1.0 - META_W) + meta_ctx * META_W
            return ctx @ Wo + bo
        key = jax.random.key(seed)
        ks = jax.random.split(key, 16)
        sc = 0.02
        d = {'hidden_states': jax.random.normal(ks[0], (B, S, H), jnp.float32), 'cons_vec': jax.random.uniform(ks[1], (16,), jnp.float32), 'Wq': jax.random.normal(ks[2], (H, H), jnp.float32) * sc, 'bq': jnp.zeros((H,), jnp.float32), 'Wk': jax.random.normal(ks[3], (H, H), jnp.float32) * sc, 'bk': jnp.zeros((H,), jnp.float32), 'Wv': jax.random.normal(ks[4], (H, H), jnp.float32) * sc, 'bv': jnp.zeros((H,), jnp.float32), 'cg_W': jax.random.normal(ks[5], (H, NH), jnp.float32) * sc, 'cg_b': jnp.zeros((NH,), jnp.float32), 'am_W': jax.random.normal(ks[6], (16, NH), jnp.float32) * sc, 'am_b': jnp.zeros((NH,), jnp.float32), 'ca_Win': jax.random.normal(ks[7], (H, 3 * H), jnp.float32) * sc, 'ca_bin': jnp.zeros((3 * H,), jnp.float32), 'ca_Wout': jax.random.normal(ks[8], (H, H), jnp.float32) * sc, 'ca_bout': jnp.zeros((H,), jnp.float32), 'mc_Win': jax.random.normal(ks[9], (H, 3 * H), jnp.float32) * sc, 'mc_bin': jnp.zeros((3 * H,), jnp.float32), 'mc_Wout': jax.random.normal(ks[10], (H, H), jnp.float32) * sc, 'mc_bout': jnp.zeros((H,), jnp.float32), 'Wo': jax.random.normal(ks[11], (H, H), jnp.float32) * sc, 'bo': jnp.zeros((H,), jnp.float32)}
        return d
    _L2_attn_in = _L2_attn_setup()

    def _L2_ffn_setup():
        import jax, jax.numpy as jnp
        import numpy as np
        D = 128
        H = 4
        DF = 512
        E = 8
        EPS = 1e-05

        def _layer_norm(x, g, b):
            mu = jnp.mean(x, axis=-1, keepdims=True)
            var = jnp.mean(jnp.square(x - mu), axis=-1, keepdims=True)
            return (x - mu) * jax.lax.rsqrt(var + EPS) * g + b

        def _mha(x, Wqkv, bqkv, Wo, bo):
            S, B, _ = x.shape
            hd = D // H
            qkv = x @ Wqkv.T + bqkv
            q, k, v = jnp.split(qkv, 3, axis=-1)
            to_heads = lambda t: t.reshape(S, B, H, hd).transpose(1, 2, 0, 3)
            q, k, v = (to_heads(q), to_heads(k), to_heads(v))
            scores = jnp.einsum('bhqd,bhkd->bhqk', q, k) * (1.0 / np.sqrt(hd))
            att = jax.nn.softmax(scores, axis=-1)
            o = jnp.einsum('bhqk,bhkd->bhqd', att, v)
            o = o.transpose(2, 0, 1, 3).reshape(S, B, D)
            return o @ Wo.T + bo

        def _moe(x, Wg, W1, b1, W2, b2):
            S, B, _ = x.shape
            xf = x.reshape(S * B, D)
            logits = xf @ Wg.T
            idx = jnp.argmax(logits, axis=-1)
            out = jnp.zeros_like(xf)
            for e in range(E):
                m = (idx == e)[:, None].astype(xf.dtype)
                h = jax.nn.relu(xf @ W1[e] + b1[e])
                out = out + m * (h @ W2[e] + b2[e])
            return out.reshape(S, B, D)
        key = jax.random.key(seed)
        ks = jax.random.split(key, 16)
        S, B = (64, 8)
        s = lambda k, shape, fan: jax.random.normal(k, shape, jnp.float32) * (1.0 / np.sqrt(fan))
        return {'x': jax.random.normal(ks[0], (S, B, D), jnp.float32), 'Wqkv': s(ks[1], (3 * D, D), D), 'bqkv': jnp.zeros((3 * D,), jnp.float32), 'Wo': s(ks[2], (D, D), D), 'bo': jnp.zeros((D,), jnp.float32), 'g1': jnp.ones((D,), jnp.float32), 'be1': jnp.zeros((D,), jnp.float32), 'g2': jnp.ones((D,), jnp.float32), 'be2': jnp.zeros((D,), jnp.float32), 'Wg': s(ks[3], (E, D), D), 'W1': s(ks[4], (E, D, DF), D), 'b1': jnp.zeros((E, DF), jnp.float32), 'W2': s(ks[5], (E, DF, D), DF), 'b2': jnp.zeros((E, D), jnp.float32)}
    _L2_ffn_in = _L2_ffn_setup()

    def _L3_attn_setup():
        import jax, jax.numpy as jnp
        import numpy as np
        DIM = 128
        H = 16
        HD = DIM // H
        EPS_DENOM = 1e-06
        EPS_LN = 1e-05
        key = jax.random.key(seed)
        ks = jax.random.split(key, 8)
        B, N = (4, 512)
        s = 1.0 / np.sqrt(DIM)
        return {'x': jax.random.normal(ks[0], (B, N, DIM), dtype=jnp.float32), 'Wq': jax.random.normal(ks[1], (DIM, DIM), dtype=jnp.float32) * s, 'bq': jnp.zeros((DIM,), dtype=jnp.float32), 'Wk': jax.random.normal(ks[2], (DIM, DIM), dtype=jnp.float32) * s, 'bk': jnp.zeros((DIM,), dtype=jnp.float32), 'Wv': jax.random.normal(ks[3], (DIM, DIM), dtype=jnp.float32) * s, 'bv': jnp.zeros((DIM,), dtype=jnp.float32), 'gamma': jnp.ones((DIM,), dtype=jnp.float32), 'beta': jnp.zeros((DIM,), dtype=jnp.float32)}
    _L3_attn_in = _L3_attn_setup()

    def _L3_ffn_setup():
        import jax, jax.numpy as jnp
        import numpy as np
        B, S, H, I, E, K = (2, 256, 128, 256, 8, 2)
        key = jax.random.key(seed)
        k1, k2, k3, k4, k5 = jax.random.split(key, 5)
        scale_h = 1.0 / np.sqrt(H)
        scale_i = 1.0 / np.sqrt(I)
        return {'x': jax.random.normal(k1, (B, S, H), dtype=jnp.float32), 'Wg': jax.random.normal(k2, (H, E), dtype=jnp.float32) * scale_h, 'W11': jax.random.normal(k3, (E, H, I), dtype=jnp.float32) * scale_h, 'W12': jax.random.normal(k4, (E, H, I), dtype=jnp.float32) * scale_h, 'W2': jax.random.normal(k5, (E, I, H), dtype=jnp.float32) * scale_i}
    _L3_ffn_in = _L3_ffn_setup()
    _d = {'L0_attn_x': _L0_attn_in['x'], 'L0_attn_W_qkvf': _L0_attn_in['W_qkvf'], 'L0_attn_W_conv': _L0_attn_in['W_conv'], 'L0_attn_W_proj': _L0_attn_in['W_proj'], 'L0_attn_W_ff1': _L0_attn_in['W_ff1'], 'L0_attn_W_ff2': _L0_attn_in['W_ff2'], 'L0_attn_ln1_g': _L0_attn_in['ln1_g'], 'L0_attn_ln1_b': _L0_attn_in['ln1_b'], 'L0_attn_ln2_g': _L0_attn_in['ln2_g'], 'L0_attn_ln2_b': _L0_attn_in['ln2_b'], 'L0_ffn_wqkv': _L0_ffn_in['wqkv'], 'L0_ffn_q_scale': _L0_ffn_in['q_scale'], 'L0_ffn_k_scale': _L0_ffn_in['k_scale'], 'L0_ffn_wo': _L0_ffn_in['wo'], 'L0_ffn_ln_g': _L0_ffn_in['ln_g'], 'L0_ffn_ln_b': _L0_ffn_in['ln_b'], 'L0_ffn_w1': _L0_ffn_in['w1'], 'L0_ffn_b1': _L0_ffn_in['b1'], 'L0_ffn_w2': _L0_ffn_in['w2'], 'L0_ffn_b2': _L0_ffn_in['b2'], 'L1_attn_Wq': _L1_attn_in['Wq'], 'L1_attn_bq': _L1_attn_in['bq'], 'L1_attn_Wk': _L1_attn_in['Wk'], 'L1_attn_bk': _L1_attn_in['bk'], 'L1_attn_Wv': _L1_attn_in['Wv'], 'L1_attn_bv': _L1_attn_in['bv'], 'L1_ffn_w1_w': _L1_ffn_in['w1_w'], 'L1_ffn_w1_s': _L1_ffn_in['w1_s'], 'L1_ffn_w2_w': _L1_ffn_in['w2_w'], 'L1_ffn_w2_s': _L1_ffn_in['w2_s'], 'L1_ffn_h1_w': _L1_ffn_in['h1_w'], 'L1_ffn_h1_s': _L1_ffn_in['h1_s'], 'L1_ffn_h2_w': _L1_ffn_in['h2_w'], 'L1_ffn_h2_s': _L1_ffn_in['h2_s'], 'L1_ffn_w3_w': _L1_ffn_in['w3_w'], 'L1_ffn_w3_s': _L1_ffn_in['w3_s'], 'L2_attn_cons_vec': _L2_attn_in['cons_vec'], 'L2_attn_Wq': _L2_attn_in['Wq'], 'L2_attn_bq': _L2_attn_in['bq'], 'L2_attn_Wk': _L2_attn_in['Wk'], 'L2_attn_bk': _L2_attn_in['bk'], 'L2_attn_Wv': _L2_attn_in['Wv'], 'L2_attn_bv': _L2_attn_in['bv'], 'L2_attn_cg_W': _L2_attn_in['cg_W'], 'L2_attn_cg_b': _L2_attn_in['cg_b'], 'L2_attn_am_W': _L2_attn_in['am_W'], 'L2_attn_am_b': _L2_attn_in['am_b'], 'L2_attn_ca_Win': _L2_attn_in['ca_Win'], 'L2_attn_ca_bin': _L2_attn_in['ca_bin'], 'L2_attn_ca_Wout': _L2_attn_in['ca_Wout'], 'L2_attn_ca_bout': _L2_attn_in['ca_bout'], 'L2_attn_mc_Win': _L2_attn_in['mc_Win'], 'L2_attn_mc_bin': _L2_attn_in['mc_bin'], 'L2_attn_mc_Wout': _L2_attn_in['mc_Wout'], 'L2_attn_mc_bout': _L2_attn_in['mc_bout'], 'L2_attn_Wo': _L2_attn_in['Wo'], 'L2_attn_bo': _L2_attn_in['bo'], 'L2_ffn_Wqkv': _L2_ffn_in['Wqkv'], 'L2_ffn_bqkv': _L2_ffn_in['bqkv'], 'L2_ffn_Wo': _L2_ffn_in['Wo'], 'L2_ffn_bo': _L2_ffn_in['bo'], 'L2_ffn_g1': _L2_ffn_in['g1'], 'L2_ffn_be1': _L2_ffn_in['be1'], 'L2_ffn_g2': _L2_ffn_in['g2'], 'L2_ffn_be2': _L2_ffn_in['be2'], 'L2_ffn_Wg': _L2_ffn_in['Wg'], 'L2_ffn_W1': _L2_ffn_in['W1'], 'L2_ffn_b1': _L2_ffn_in['b1'], 'L2_ffn_W2': _L2_ffn_in['W2'], 'L2_ffn_b2': _L2_ffn_in['b2'], 'L3_attn_Wq': _L3_attn_in['Wq'], 'L3_attn_bq': _L3_attn_in['bq'], 'L3_attn_Wk': _L3_attn_in['Wk'], 'L3_attn_bk': _L3_attn_in['bk'], 'L3_attn_Wv': _L3_attn_in['Wv'], 'L3_attn_bv': _L3_attn_in['bv'], 'L3_attn_gamma': _L3_attn_in['gamma'], 'L3_attn_beta': _L3_attn_in['beta'], 'L3_ffn_Wg': _L3_ffn_in['Wg'], 'L3_ffn_W11': _L3_ffn_in['W11'], 'L3_ffn_W12': _L3_ffn_in['W12'], 'L3_ffn_W2': _L3_ffn_in['W2']}
    _x0 = _d['L0_attn_x']
    _d['L0_attn_x'] = jax.random.normal(jax.random.fold_in(jax.random.key(seed), 1), (8, 512, 128), dtype=_x0.dtype)
    del _x0
    return _d

def reference(L0_attn_x, L0_attn_W_qkvf, L0_attn_W_conv, L0_attn_W_proj, L0_attn_W_ff1, L0_attn_W_ff2, L0_attn_ln1_g, L0_attn_ln1_b, L0_attn_ln2_g, L0_attn_ln2_b, L0_ffn_wqkv, L0_ffn_q_scale, L0_ffn_k_scale, L0_ffn_wo, L0_ffn_ln_g, L0_ffn_ln_b, L0_ffn_w1, L0_ffn_b1, L0_ffn_w2, L0_ffn_b2, L1_attn_Wq, L1_attn_bq, L1_attn_Wk, L1_attn_bk, L1_attn_Wv, L1_attn_bv, L1_ffn_w1_w, L1_ffn_w1_s, L1_ffn_w2_w, L1_ffn_w2_s, L1_ffn_h1_w, L1_ffn_h1_s, L1_ffn_h2_w, L1_ffn_h2_s, L1_ffn_w3_w, L1_ffn_w3_s, L2_attn_cons_vec, L2_attn_Wq, L2_attn_bq, L2_attn_Wk, L2_attn_bk, L2_attn_Wv, L2_attn_bv, L2_attn_cg_W, L2_attn_cg_b, L2_attn_am_W, L2_attn_am_b, L2_attn_ca_Win, L2_attn_ca_bin, L2_attn_ca_Wout, L2_attn_ca_bout, L2_attn_mc_Win, L2_attn_mc_bin, L2_attn_mc_Wout, L2_attn_mc_bout, L2_attn_Wo, L2_attn_bo, L2_ffn_Wqkv, L2_ffn_bqkv, L2_ffn_Wo, L2_ffn_bo, L2_ffn_g1, L2_ffn_be1, L2_ffn_g2, L2_ffn_be2, L2_ffn_Wg, L2_ffn_W1, L2_ffn_b1, L2_ffn_W2, L2_ffn_b2, L3_attn_Wq, L3_attn_bq, L3_attn_Wk, L3_attn_bk, L3_attn_Wv, L3_attn_bv, L3_attn_gamma, L3_attn_beta, L3_ffn_Wg, L3_ffn_W11, L3_ffn_W12, L3_ffn_W2):

    def _L0_attn_ref(x, W_qkvf, W_conv, W_proj, W_ff1, W_ff2, ln1_g, ln1_b, ln2_g, ln2_b):
        import jax, jax.numpy as jnp
        import numpy as np
        N_HEAD = 16
        FUTURE_DIM = 4

        def _layernorm(x, g, b, eps=1e-05):
            mu = jnp.mean(x, axis=-1, keepdims=True)
            var = jnp.mean(jnp.square(x - mu), axis=-1, keepdims=True)
            return (x - mu) * jax.lax.rsqrt(var + eps) * g + b

        def _future_attn_head(h, W_qkvf, W_conv, W_proj):
            B, T, D = h.shape
            H, hs, F = (N_HEAD, D // N_HEAD, FUTURE_DIM)
            NEG = jnp.float32(-jnp.inf)
            qkvf = h @ W_qkvf.T
            q, k, v, f = jnp.split(qkvf, 4, axis=-1)
            to_h = lambda t: t.reshape(B, T, H, hs).transpose(0, 2, 1, 3)
            q, k, v, f = (to_h(q), to_h(k), to_h(v), to_h(f))
            attn = jnp.einsum('bhtd,bhsd->bhts', q, k) * hs ** (-0.5)
            rows = jnp.arange(T)[:, None]
            causal_mask = jnp.arange(T)[None, :] <= rows
            causal_attn = jnp.where(causal_mask, attn, 0.0)
            padded_causal = jnp.pad(causal_attn, ((0, 0), (0, 0), (0, 0), (0, F)))
            up_future = jnp.einsum('bhtc,cdf->btfhd', f, W_conv).reshape(B, T, F, D)
            k_future = jnp.einsum('btfc,dc->btfd', up_future, W_qkvf[D:2 * D])
            k_future = k_future.reshape(B, T, F, H, hs).transpose(0, 3, 1, 2, 4)
            future_attention = jnp.einsum('bhtd,bhtfd->bhtf', q, k_future)
            cols_f = rows + 1 + jnp.arange(F)[None, :]
            full_attn = padded_causal.at[:, :, rows, cols_f].set(future_attention)
            full_mask = jnp.arange(T + F)[None, :] <= rows + F
            full_attn = jnp.where(full_mask, full_attn, NEG)
            sm = jax.nn.softmax(full_attn, axis=-1)
            sm_causal = jnp.where(causal_mask, sm[..., :T], 0.0)
            unpadded_future = sm[:, :, rows, cols_f]
            v_future = jnp.einsum('btfc,dc->btfd', up_future, W_qkvf[2 * D:3 * D])
            v_future = v_future.reshape(B, T, F, H, hs).transpose(0, 3, 1, 2, 4)
            future_x = jnp.einsum('bhtf,bhtfd->bhtd', unpadded_future, v_future)
            causal_x = jnp.einsum('bhts,bhsd->bhtd', sm_causal, v)
            new_x = (causal_x + future_x).transpose(0, 2, 1, 3).reshape(B, T, D)
            return new_x @ W_proj.T
        x = x + _future_attn_head(_layernorm(x, ln1_g, ln1_b), W_qkvf, W_conv, W_proj)
        h = _layernorm(x, ln2_g, ln2_b)
        x = x + jax.nn.gelu(h @ W_ff1, approximate=False) @ W_ff2
        return x

    def _L0_ffn_ref(x, wqkv, q_scale, k_scale, wo, ln_g, ln_b, w1, b1, w2, b2):
        import jax, jax.numpy as jnp
        import numpy as np
        DIM = 128
        DEPTH = 2
        HEADS = 8
        DIM_HEAD = 64
        WINDOW = 64
        INNER = HEADS * DIM_HEAD
        HID = int(DIM * 4 * 2 / 3)
        B, N = (2, 1024)
        QK_SCALE = 8.0

        def shift_token(t):
            t1, t2 = jnp.split(t, 2, axis=-1)
            t2 = jnp.pad(t2, ((0, 0), (1, 0), (0, 0)))[:, :-1]
            return jnp.concatenate([t1, t2], axis=-1)

        def l2norm(t):
            return t / jnp.clip(jnp.linalg.norm(t, axis=-1, keepdims=True), 1e-12)

        def rotate_half(x):
            x1, x2 = jnp.split(x, 2, axis=-1)
            return jnp.concatenate([-x2, x1], axis=-1)

        def rotary_xpos(q, k):
            n = q.shape[-2]
            half_idx = jnp.arange(0, DIM_HEAD, 2, dtype=jnp.float32)
            inv_freq = 1.0 / 10000.0 ** (half_idx / DIM_HEAD)
            t = jnp.arange(n, dtype=jnp.float32)
            freqs = t[:, None] * inv_freq[None, :]
            freqs = jnp.concatenate([freqs, freqs], axis=-1)
            base = (half_idx + 0.4 * DIM_HEAD) / (1.4 * DIM_HEAD)
            power = (t - n // 2) / float(WINDOW // 2)
            scale = base[None, :] ** power[:, None]
            scale = jnp.concatenate([scale, scale], axis=-1)
            cos, sin = (jnp.cos(freqs), jnp.sin(freqs))
            q = q * cos * scale + rotate_half(q) * sin * scale
            k = k * cos / scale + rotate_half(k) * sin / scale
            return (q, k)

        def local_attention(q, k, v):
            b, h, n, d = q.shape
            w = n // WINDOW
            bq = q.reshape(b, h, w, WINDOW, d) * QK_SCALE
            bk = k.reshape(b, h, w, WINDOW, d)
            bv = v.reshape(b, h, w, WINDOW, d)

            def look_around(t):
                p = jnp.pad(t, ((0, 0), (0, 0), (1, 0), (0, 0), (0, 0)))
                return jnp.concatenate([p[:, :, :w], p[:, :, 1:]], axis=3)
            bk, bv = (look_around(bk), look_around(bv))
            bt = jnp.arange(n).reshape(w, WINDOW)
            btp = jnp.pad(bt, ((1, 0), (0, 0)), constant_values=-1)
            btk = jnp.concatenate([btp[:w], btp[1:]], axis=1)
            sim = jnp.einsum('bhwid,bhwjd->bhwij', bq, bk)
            i = bt[:, :, None]
            j = btk[:, None, :]
            mask = (i < j) | (i > j + WINDOW) | (j == -1)
            sim = jnp.where(mask, -jnp.finfo(sim.dtype).max, sim)
            attn = jax.nn.softmax(sim, axis=-1)
            out = jnp.einsum('bhwij,bhwjd->bhwid', attn, bv)
            return out.reshape(b, h, n, d)

        def _layer(x, wqkv, qs, ksc, wo, lg, lb, w1, b1, w2, b2):
            b, n, _ = x.shape
            h = shift_token(x)
            qkv = h @ wqkv
            q, k, v = jnp.split(qkv, 3, axis=-1)
            to_heads = lambda t: t.reshape(b, n, HEADS, DIM_HEAD).transpose(0, 2, 1, 3)
            q, k, v = (to_heads(q), to_heads(k), to_heads(v))
            q = l2norm(q) * qs
            k = l2norm(k) * ksc
            q, k = rotary_xpos(q, k)
            o = local_attention(q, k, v)
            o = o.transpose(0, 2, 1, 3).reshape(b, n, INNER)
            x = x + o @ wo
            h = shift_token(x)
            mu = h.mean(-1, keepdims=True)
            var = h.var(-1, keepdims=True)
            h = (h - mu) / jnp.sqrt(var + 1e-05) * lg + lb
            h = h @ w1 + b1
            a, g = jnp.split(h, 2, axis=-1)
            h = a * jax.nn.gelu(g, approximate=False)
            x = x + h @ w2 + b2
            return x
        for l in range(DEPTH):
            x = _layer(x, wqkv[l], q_scale[l], k_scale[l], wo[l], ln_g[l], ln_b[l], w1[l], b1[l], w2[l], b2[l])
        return x

    def _L1_attn_ref(x, Wq, bq, Wk, bk, Wv, bv):
        import math
        import jax, jax.numpy as jnp
        import numpy as np
        B, S, E, H = (4, 256, 128, 16)
        HD = E // H
        b, s, e = x.shape
        h, hd, _ = Wq.shape
        inv_scale = 1.0 / math.sqrt(hd)
        q = jnp.einsum('bse,hde->bshd', x, Wq) + bq
        k = jnp.einsum('bse,hde->bshd', x, Wk) + bk
        v = jnp.einsum('bse,hde->bshd', x, Wv) + bv
        mask = jnp.triu(jnp.full((s, s), -jnp.inf, dtype=x.dtype), k=1)
        scores = (jnp.einsum('bqhd,bkhd->bhqk', q, k) + mask) * inv_scale
        attn = jax.nn.softmax(scores, axis=-1)
        out = jnp.einsum('bhqk,bkhd->bqhd', attn, v)
        return out.reshape(b, s, h * hd)

    def _L1_ffn_ref(x, w1_w, w1_s, w2_w, w2_s, h1_w, h1_s, h2_w, h2_s, w3_w, w3_s):
        import jax, jax.numpy as jnp
        import numpy as np
        D_IN, D_HID = (128, 512)

        def _ternary(key, shape):
            return jax.random.randint(key, shape, -1, 2).astype(jnp.float32)

        def _tlin(x, w, s):
            return jnp.einsum('bsi,oi->bso', x, w) * s
        h = jax.nn.silu(_tlin(x, w1_w, w1_s)) * _tlin(x, w2_w, w2_s)
        h = jax.nn.gelu(_tlin(h, h1_w, h1_s), approximate=False)
        h = jax.nn.gelu(_tlin(h, h2_w, h2_s), approximate=False)
        return _tlin(h, w3_w, w3_s)

    def _L2_attn_ref(hidden_states, cons_vec, Wq, bq, Wk, bk, Wv, bv, cg_W, cg_b, am_W, am_b, ca_Win, ca_bin, ca_Wout, ca_bout, mc_Win, mc_bin, mc_Wout, mc_bout, Wo, bo):
        import jax, jax.numpy as jnp
        import numpy as np
        B, S, H, NH = (4, 128, 128, 16)
        HD = H // NH
        CAUSAL_HEADS = 4
        META_HEADS = NH // 4
        CAUSAL_W = 0.7
        META_W = (0.9 - 0.8) / 0.2 * 0.3

        def _mha(xq, xkv, Win, bi, Wout, bout, nh):
            b, sq, h = xq.shape
            sk = xkv.shape[1]
            hd = h // nh
            q = (xq @ Win[:, :h] + bi[:h]).reshape(b, sq, nh, hd).transpose(0, 2, 1, 3)
            k = (xkv @ Win[:, h:2 * h] + bi[h:2 * h]).reshape(b, sk, nh, hd).transpose(0, 2, 1, 3)
            v = (xkv @ Win[:, 2 * h:] + bi[2 * h:]).reshape(b, sk, nh, hd).transpose(0, 2, 1, 3)
            scores = jnp.einsum('bhqd,bhkd->bhqk', q, k) / jnp.sqrt(jnp.asarray(hd, q.dtype))
            probs = jax.nn.softmax(scores, axis=-1)
            ctx = jnp.einsum('bhqk,bhkd->bhqd', probs, v)
            return ctx.transpose(0, 2, 1, 3).reshape(b, sq, h) @ Wout + bout

        def _forward(hidden_states, cons_vec, Wq, bq, Wk, bk, Wv, bv, cg_W, cg_b, am_W, am_b, ca_Win, ca_bin, ca_Wout, ca_bout, mc_Win, mc_bin, mc_Wout, mc_bout, Wo, bo):
            b, s, h = hidden_states.shape
            q = (hidden_states @ Wq + bq).reshape(b, s, NH, HD).transpose(0, 2, 1, 3)
            k = (hidden_states @ Wk + bk).reshape(b, s, NH, HD).transpose(0, 2, 1, 3)
            v = (hidden_states @ Wv + bv).reshape(b, s, NH, HD).transpose(0, 2, 1, 3)
            scores = jnp.einsum('bhqd,bhkd->bhqk', q, k) / jnp.sqrt(jnp.asarray(HD, q.dtype))
            mod = jax.nn.sigmoid(hidden_states @ cg_W + cg_b + (cons_vec @ am_W + am_b))
            scores = scores * mod.transpose(0, 2, 1)[..., None]
            probs = jax.nn.softmax(scores, axis=-1)
            ctx = jnp.einsum('bhqk,bhkd->bhqd', probs, v).transpose(0, 2, 1, 3).reshape(b, s, h)
            causal_ctx = _mha(hidden_states, hidden_states, ca_Win, ca_bin, ca_Wout, ca_bout, CAUSAL_HEADS)
            ctx = ctx * (1.0 - CAUSAL_W) + causal_ctx * CAUSAL_W
            meta_ctx = _mha(ctx, ctx, mc_Win, mc_bin, mc_Wout, mc_bout, META_HEADS)
            ctx = ctx * (1.0 - META_W) + meta_ctx * META_W
            return ctx @ Wo + bo
        return _forward(hidden_states, cons_vec, Wq, bq, Wk, bk, Wv, bv, cg_W, cg_b, am_W, am_b, ca_Win, ca_bin, ca_Wout, ca_bout, mc_Win, mc_bin, mc_Wout, mc_bout, Wo, bo)

    def _L2_ffn_ref(x, Wqkv, bqkv, Wo, bo, g1, be1, g2, be2, Wg, W1, b1, W2, b2):
        import jax, jax.numpy as jnp
        import numpy as np
        D = 128
        H = 4
        DF = 512
        E = 8
        EPS = 1e-05

        def _layer_norm(x, g, b):
            mu = jnp.mean(x, axis=-1, keepdims=True)
            var = jnp.mean(jnp.square(x - mu), axis=-1, keepdims=True)
            return (x - mu) * jax.lax.rsqrt(var + EPS) * g + b

        def _mha(x, Wqkv, bqkv, Wo, bo):
            S, B, _ = x.shape
            hd = D // H
            qkv = x @ Wqkv.T + bqkv
            q, k, v = jnp.split(qkv, 3, axis=-1)
            to_heads = lambda t: t.reshape(S, B, H, hd).transpose(1, 2, 0, 3)
            q, k, v = (to_heads(q), to_heads(k), to_heads(v))
            scores = jnp.einsum('bhqd,bhkd->bhqk', q, k) * (1.0 / np.sqrt(hd))
            att = jax.nn.softmax(scores, axis=-1)
            o = jnp.einsum('bhqk,bhkd->bhqd', att, v)
            o = o.transpose(2, 0, 1, 3).reshape(S, B, D)
            return o @ Wo.T + bo

        def _moe(x, Wg, W1, b1, W2, b2):
            S, B, _ = x.shape
            xf = x.reshape(S * B, D)
            logits = xf @ Wg.T
            idx = jnp.argmax(logits, axis=-1)
            out = jnp.zeros_like(xf)
            for e in range(E):
                m = (idx == e)[:, None].astype(xf.dtype)
                h = jax.nn.relu(xf @ W1[e] + b1[e])
                out = out + m * (h @ W2[e] + b2[e])
            return out.reshape(S, B, D)
        y = _layer_norm(x + _mha(x, Wqkv, bqkv, Wo, bo), g1, be1)
        z = _layer_norm(y + _moe(y, Wg, W1, b1, W2, b2), g2, be2)
        return z

    def _L3_attn_ref(x, Wq, bq, Wk, bk, Wv, bv, gamma, beta):
        import jax, jax.numpy as jnp
        import numpy as np
        DIM = 128
        H = 16
        HD = DIM // H
        EPS_DENOM = 1e-06
        EPS_LN = 1e-05
        B, N, C = x.shape
        q = (x @ Wq.T + bq).reshape(B, N, H, HD)
        k = (x @ Wk.T + bk).reshape(B, N, H, HD)
        v = (x @ Wv.T + bv).reshape(B, N, H, HD)
        q = jax.nn.relu(q)
        k = jax.nn.relu(k)
        kv = jnp.einsum('bnhd,bnhp->bhdp', k, v)
        k_sum = k.sum(axis=1)
        denom = jnp.einsum('bnhd,bhd->bnh', q, k_sum)
        denom = jnp.maximum(denom, EPS_DENOM)[..., None]
        ctx = jnp.einsum('bnhd,bhdp->bnhp', q, kv)
        out = (ctx / denom).reshape(B, N, C)
        y = out + x
        mu = y.mean(axis=-1, keepdims=True)
        var = y.var(axis=-1, keepdims=True)
        return (y - mu) / jnp.sqrt(var + EPS_LN) * gamma + beta

    def _L3_ffn_ref(x, Wg, W11, W12, W2):
        import jax, jax.numpy as jnp
        import numpy as np
        B, S, H, I, E, K = (2, 256, 128, 256, 8, 2)
        gate_scores = jax.nn.softmax(x @ Wg, axis=-1)
        topk_scores, topk_idx = jax.lax.top_k(gate_scores, K)
        topk_scores = topk_scores / (topk_scores.sum(-1, keepdims=True) + 1e-08)
        gate = jnp.einsum('bsh,ehi->bsei', x, W11)
        value = jnp.einsum('bsh,ehi->bsei', x, W12)
        fused = gate * jax.nn.sigmoid(gate) * value
        expert_out = jnp.einsum('bsei,eih->bseh', fused, W2)
        gathered = jnp.take_along_axis(expert_out, topk_idx[..., None], axis=2)
        out = jnp.sum(topk_scores[..., None] * gathered, axis=2)
        return out
    x = L0_attn_x
    x = x + _layernorm(_L0_attn_ref(_layernorm(x, axis=-1), L0_attn_W_qkvf, L0_attn_W_conv, L0_attn_W_proj, L0_attn_W_ff1, L0_attn_W_ff2, L0_attn_ln1_g, L0_attn_ln1_b, L0_attn_ln2_g, L0_attn_ln2_b), axis=-1)
    x = x + _layernorm(_L0_ffn_ref(_layernorm(x, axis=-1), L0_ffn_wqkv, L0_ffn_q_scale, L0_ffn_k_scale, L0_ffn_wo, L0_ffn_ln_g, L0_ffn_ln_b, L0_ffn_w1, L0_ffn_b1, L0_ffn_w2, L0_ffn_b2), axis=-1)
    x = x + _layernorm(_L1_attn_ref(_layernorm(x, axis=-1), L1_attn_Wq, L1_attn_bq, L1_attn_Wk, L1_attn_bk, L1_attn_Wv, L1_attn_bv), axis=-1)
    x = x + _layernorm(_L1_ffn_ref(_layernorm(x, axis=-1), L1_ffn_w1_w, L1_ffn_w1_s, L1_ffn_w2_w, L1_ffn_w2_s, L1_ffn_h1_w, L1_ffn_h1_s, L1_ffn_h2_w, L1_ffn_h2_s, L1_ffn_w3_w, L1_ffn_w3_s), axis=-1)
    x = x + _layernorm(_L2_attn_ref(_layernorm(x, axis=-1), L2_attn_cons_vec, L2_attn_Wq, L2_attn_bq, L2_attn_Wk, L2_attn_bk, L2_attn_Wv, L2_attn_bv, L2_attn_cg_W, L2_attn_cg_b, L2_attn_am_W, L2_attn_am_b, L2_attn_ca_Win, L2_attn_ca_bin, L2_attn_ca_Wout, L2_attn_ca_bout, L2_attn_mc_Win, L2_attn_mc_bin, L2_attn_mc_Wout, L2_attn_mc_bout, L2_attn_Wo, L2_attn_bo), axis=-1)
    x = x + _layernorm(_L2_ffn_ref(_layernorm(x, axis=-1), L2_ffn_Wqkv, L2_ffn_bqkv, L2_ffn_Wo, L2_ffn_bo, L2_ffn_g1, L2_ffn_be1, L2_ffn_g2, L2_ffn_be2, L2_ffn_Wg, L2_ffn_W1, L2_ffn_b1, L2_ffn_W2, L2_ffn_b2), axis=-1)
    x = x + _layernorm(_L3_attn_ref(_layernorm(x, axis=-1), L3_attn_Wq, L3_attn_bq, L3_attn_Wk, L3_attn_bk, L3_attn_Wv, L3_attn_bv, L3_attn_gamma, L3_attn_beta), axis=-1)
    x = x + _layernorm(_L3_ffn_ref(_layernorm(x, axis=-1), L3_ffn_Wg, L3_ffn_W11, L3_ffn_W12, L3_ffn_W2), axis=-1)
    return x

_drawn_inputs = setup_inputs


def setup_inputs(seed=0):
    import zlib

    import numpy as np

    out = dict(_drawn_inputs(seed))
    spreads = {'L0_attn_ln1_g': (1.0, 0.6),
     'L0_attn_ln1_b': (0.0, 0.409),
     'L0_attn_ln2_g': (1.0, 0.6),
     'L0_attn_ln2_b': (0.0, 0.297),
     'L0_ffn_q_scale': (1.0, 0.6),
     'L0_ffn_k_scale': (1.0, 0.6),
     'L0_ffn_ln_g': (1.0, 0.6),
     'L0_ffn_ln_b': (0.0, 0.8),
     'L0_ffn_b1': (0.0, 0.49),
     'L0_ffn_b2': (0.0, 0.1),
     'L2_attn_bq': (0.0, 0.8),
     'L2_attn_bk': (0.0, 2.0),
     'L2_attn_bv': (0.0, 0.1),
     'L2_attn_cg_b': (0.0, 0.8),
     'L2_attn_am_b': (0.0, 2.0),
     'L2_attn_ca_bin': (0.0, 0.344),
     'L2_attn_ca_bout': (0.0, 0.1),
     'L2_attn_mc_bin': (0.0, 0.8),
     'L2_attn_mc_bout': (0.0, 0.308),
     'L2_attn_bo': (0.0, 0.1),
     'L2_ffn_bqkv': (0.0, 0.1),
     'L2_ffn_bo': (0.0, 0.1),
     'L2_ffn_g1': (1.0, 0.2),
     'L2_ffn_be1': (0.0, 0.1),
     'L2_ffn_g2': (1.0, 0.2),
     'L2_ffn_be2': (0.0, 0.1),
     'L2_ffn_b1': (0.0, 0.36),
     'L2_ffn_b2': (0.0, 0.281),
     'L3_attn_bq': (0.0, 2.0),
     'L3_attn_bk': (0.0, 2.0),
     'L3_attn_bv': (0.0, 0.268),
     'L3_attn_gamma': (1.0, 0.2),
     'L3_attn_beta': (0.0, 0.287)}
    factors = {'L0_attn_W_qkvf': 2.817,
     'L0_attn_W_conv': 8.0,
     'L0_attn_W_proj': 3.015,
     'L0_ffn_w1': 3.152,
     'L0_ffn_w2': 3.262,
     'L1_attn_bq': 4.937,
     'L1_attn_bk': 64.0,
     'L2_attn_cons_vec': 8.0,
     'L2_attn_Wq': 8.0,
     'L2_attn_Wk': 8.0,
     'L2_attn_Wv': 3.342,
     'L2_attn_cg_W': 8.0,
     'L2_attn_am_W': 8.0,
     'L2_attn_ca_Win': 4.627,
     'L2_attn_ca_Wout': 3.024,
     'L2_attn_mc_Win': 8.0,
     'L2_attn_mc_Wout': 4.911,
     'L3_attn_Wq': 2.688}
    for name, (base, spread) in spreads.items():
        noise = np.random.default_rng([zlib.crc32(name.encode()), seed]).standard_normal(out[name].shape)
        drawn = base * np.exp(spread * noise) if base else spread * noise
        out[name] = jnp.asarray(drawn.astype(out[name].dtype))
    for name, factor in factors.items():
        out[name] = (out[name] * factor).astype(out[name].dtype)
    return out
```

```python
from contextlib import ExitStack, contextmanager

import numpy as np

import concourse.bass as bass
from concourse import mybir

F32 = mybir.dt.float32
F32R = mybir.dt.float32r
BF16 = mybir.dt.bfloat16
ALU = mybir.AluOpType
ACT = mybir.ActivationFunctionType
AX = mybir.AxisListType

P = 128
B, T, D = 8, 512, 128
NT = T // P
TILES = B * NT
EPS = 1e-5
MASKED = -1e30
H2 = D // 2
NQ = 4


class Signal:

    def __init__(self, sem, per):
        self.sem, self.per, self.n = sem, per, 0

    def at(self, turn, n=0):
        return turn.times(self.per) + (n + 1)

    def one(self):
        self.n += 1
        return 1

    def turn_done(self):
        assert self.n == self.per, (self.sem, self.n, self.per)


class Turn:

    def __init__(self, eng, i):
        self.eng, self.i, self.products = eng, i, {1: i}

    def times(self, per):
        if per not in self.products:
            self.products[per] = self.eng.snap(self.i * per)
        return self.products[per]

    def tiles(self, t):
        return t[:, bass.ds(self.times(NT), NT), :]

    def tile(self, t, j):
        return t[:, bass.ds(self.times(NT) + j, 1), :]


@contextmanager
def turns(eng, n):
    with eng.Fori(0, n) as i:
        yield Turn(eng, i)


class Phase:

    def __init__(self, nc, name):
        self.nc, self.name, self.made, self.signals, self.ctx = nc, name, [], [], ExitStack()

    def flag(self, what, per=1):
        sem = self.nc.alloc_semaphore(f"{self.name}_{what}")
        self.made.append(sem)
        self.signals.append(Signal(sem, per))
        return self.signals[-1]

    def sb(self, what, shape, dt=F32):
        return self.ctx.enter_context(self.nc.sbuf_tensor(f"{self.name}_{what}", shape, dt))

    def block(self):
        for s in self.signals:
            if s.per:
                self.nc.sync.sem_inc(s.sem, 1)
        self.nc.all_engine_barrier()
        return self.ctx.enter_context(self.nc.Block())

    def close(self):
        self.ctx.close()
        self.nc.clear_and_free_semaphores(self.made)
        self.nc.all_engine_barrier()


class Chip:
    pass


def tiles_of(t, i):
    return i.tiles(t)


def tile_of(t, i, j):
    return i.tile(t, j)



class Norm:
    def __init__(self, ph, per):
        self.variance, self.eps_added, self.rstd_ready = (ph.flag(s, per) for s in ("variance", "eps_added", "rstd_ready"))
        self.bn = ph.sb("bn", [P, NT, 6])
        self.mv = ph.sb("mv", [P, NT, 2])
        self.veps = ph.sb("veps", [P, NT])
        self.rstd = ph.sb("rstd", [P, NT])

    def on_gpsimd(self, nc, pool, c, i):
        pool.wait_ge(self.variance.sem, self.variance.at(i, self.rstd_ready.n + 1))
        nc.gpsimd.tensor_tensor(self.veps[:, :], self.mv[:, :, 1], c.eps[:, :], ALU.add).then_inc(self.eps_added.sem, self.eps_added.one())
        n = self.eps_added.n
        pool.wait_ge(self.eps_added.sem, self.eps_added.at(i, n))
        nc.gpsimd.tensor_tensor(self.rstd[:, :], self.veps[:, :], c.minus_half[:, :], ALU.pow).then_inc(self.rstd_ready.sem, self.rstd_ready.one())

    def on_vector(self, nc, dve, c, i, src, dst, step):
        for j in range(NT):
            ins = nc.vector.bn_stats(self.bn[:, j, :], src(j))
        dve.drain()
        for j in range(NT):
            ins = nc.vector.bn_aggr(self.mv[:, j, :], self.bn[:, j, :])
        ins.then_inc(self.variance.sem, self.variance.one())
        n = self.variance.n
        dve.wait_ge(self.rstd_ready.sem, self.rstd_ready.at(i, n))
        for j in range(NT):
            ins = nc.vector.tensor_scalar(dst(j), src(j), self.mv[:, j, 0:1], self.rstd[:, j:j + 1], ALU.subtract, ALU.mult)
        return ins


def wide(row):
    return row.unsqueeze(1).to_broadcast([P, NT, row.shape[-1]])


def turn_done(*signals):
    for s in signals:
        s.turn_done()



def attention_phase(nc, c, name, w, heads, scale, causal=False, bias=False, source=None, affine=False, grouped=False,
                    future=False, modulated=False, out_steps=(), finish="residual_norm"):
    ph = Phase(nc, name)
    hd = D // heads
    rows = NQ * hd
    in_group = P // rows
    G = heads // in_group
    E = hd + 1
    half = heads // 2
    R = half * E
    units = heads * NT
    W_USES = 1 + 2 * G + 1 + 1 + 2 + (9 if future else 0) + (G if modulated else 0) + 2 * len(out_steps)
    norms = {None: 1, "given": 0}[source] + affine + (finish == "residual_norm") + ("mixed" in out_steps)

    src = ph.sb("src", [P, NT, D])
    hsrc = ph.sb("hsrc", [P, NT, D]) if affine else src
    uT = ph.sb("uT", [P, T])
    high = ph.sb("high", [P, 2, T], F32R)
    lowpart = ph.sb("lowpart", [P, 2, T])
    qs = ph.sb("qs", [P, G, T], F32R)
    ks = ph.sb("ks", [P, G, T], F32R)
    vx = ph.sb("vx", [P, NT, heads, R + E])
    vx_flat = vx[:, :, :, :].rearrange("p j h m -> p j (h m)")
    sums = ph.sb("sums", [R, 2, T])
    sums_tok = ph.sb("sums_tok", [P, 2, NT, half, E])
    negmax = ph.sb("negmax", [P, NT, heads])
    mrow = ph.sb("mrow", [heads, T])
    mT = ph.sb("mT", [48, T], F32R)
    pT = ph.sb("pT", [P, 2, NT, T])
    rden = ph.sb("rden", [P, 2, NT, half])
    ctxt = ph.sb("ctx", [P, NT, D])
    tmp = ph.sb("tmp", [P, NT, D])
    stepT = uT
    stepo = ph.sb("stepo", [P, NT, D]) if out_steps else None
    if modulated:
        modT = ph.sb("modT", [P, G, T])
        mod_bias = ph.sb("mod_bias", [P, G])
        scaled = ph.sb("scaled", [P, 2, T])
    sb_scaled = ph.sb("biases", [P, 4 * G]) if bias else None
    if future:
        qtok = ph.sb("qtok", [P, NT, D])
        kf = c.ctx[:, 0:4 * NT, :].rearrange("p (f j) d -> p f j d", f=4)
        vf = c.ctx[:, 4 * NT:8 * NT, :].rearrange("p (f j) d -> p f j d", f=4)
        afT = kf[:, 0, :, :]
        wkf, wvf = (ph.sb(n, [P, 4, P]) for n in ("wkf", "wvf"))
        fut = ph.sb("fut", [P, 4, NT, heads])
        futmax = ph.sb("futmax", [P, NT, heads])
        pf = ph.sb("pf", [P, 4, NT, heads])
        futden = ph.sb("futden", [P, NT, heads])

    w0, w1 = c.bank[0], c.bank[1]
    wbank = (w0, w1)
    abank = (c.bank[2], c.bank[3])
    bbank = (c.bank[4], c.bank[5])
    obank = (c.bank[6], c.bank[7])

    S = ph.flag
    prepared, mod_added = S("prepared", 0), S("mod_added", 0)
    src_ready = S("src_ready")
    w_filled, w_emptied = S("w_filled", W_USES), S("w_emptied", W_USES)
    parts_ready, stacked = S("parts_ready", G), S("stacked", 2 * G)
    scored_a, maxed = S("scored_a", units), S("maxed", units)
    m_copied = S("m_copied", 2)
    m_final = S("m_final")
    scored_b, exped = S("scored_b", units), S("exped", units)
    head_done = S("head_done", heads)
    sums_copied = S("sums_copied", 2)
    ctx_ready = S("ctx_ready")
    step_taken = S("step_taken", max(len(out_steps), 1))
    mod_scaled = S("mod_scaled", G)
    norm = Norm(ph, max(norms, 1))
    step = S("dve_step", affine + 13 * future + sum({"causal_out": 1, "meta_out": 1, "mixed": 3}.get(s, 0) for s in out_steps)
             + (finish == "residual_norm") * (1 + (not out_steps)) + (finish == "context") + 1 - future)
    fut_asked, fut_exped = S("fut_asked"), S("fut_exped")

    def keys_of(q):
        return (q * P if grouped else 0), ((q + 1) * P if causal or grouped else T)

    def queries_of(k):
        return (k * P if causal or grouped else 0), ((k + 1) * P if grouped else T)

    masked = causal or grouped
    mask_a, mask_b = (c.other_groups, c.other_groups) if grouped else (c.later_keys, c.earlier_queries)
    block = ph.block()
    use_v = 1 + 2 * G + (G if modulated else 0)

    @block.sync
    def _(sp):
        load_next(sp, c)

    @block.tensor
    def _(pe):
        wait_weights(pe, c, w)
        if future:
            for f in range(4):
                ins = nc.tensor.matmul(w0[:, f * P:(f + 1) * P], w["bd"](f), w["wf"], start=True, stop=True)
            ins.then_inc(prepared.sem, prepared.one())
            pe.wait_ge(prepared.sem, 2)
            for which, bank in (("wkT", w1), ("wvT", w0)):
                for f in range(4):
                    ins = nc.tensor.matmul(bank[:, f * P:(f + 1) * P], afT[:, f, :], w[which], start=True, stop=True)
            ins.then_inc(prepared.sem, prepared.one())
            pe.wait_ge(prepared.sem, 5)
        if modulated:
            for g in range(G):
                ins = nc.tensor.matmul(w0[:, g:g + 1], w["am"](g), w["cons"], start=True, stop=True)
            ins.then_inc(prepared.sem, prepared.one())
        with turns(pe, B) as i:
            use = [0]

            def fill(emit):
                n = use[0]
                pe.wait_ge(w_emptied.sem, w_emptied.at(i, max(n - 1, 0)))
                emit(wbank[n % 2]).then_inc(w_filled.sem, w_filled.one())
                use[0] += 1

            def turn(s):
                def emit(bank):
                    for j in range(NT):
                        ins = nc.tensor.transpose(bank[:, j * P:(j + 1) * P], s[:, j, :], c.ident[:, :])
                    return ins
                return emit

            def tokens(sT, weights, b=None):
                def emit(bank):
                    for j in range(NT):
                        ins = nc.tensor.matmul(bank[:, j * P:(j + 1) * P], sT[:, j * P:(j + 1) * P], weights, start=True, stop=b is None)
                        if b is not None:
                            ins = nc.tensor.matmul(bank[:, j * P:(j + 1) * P], c.ones[0:1, :], b, start=False, stop=True)
                    return ins
                return emit

            pe.wait_ge(src_ready.sem, src_ready.at(i, 1))
            fill(turn(hsrc))
            pe.wait_ge(w_emptied.sem, w_emptied.at(i, 1))
            if modulated:
                for g in range(G):
                    fill(lambda bank: nc.tensor.matmul(bank[:, :], w["mod"](g), uT[:, :], start=True, stop=True))
            for g in range(2 * G):
                fill(lambda bank: nc.tensor.matmul(bank[:, :], w["qk"](g), uT[:, :], start=True, stop=True))
            fill(tokens(uT, w["v"], w.get("bv")))
            if future:
                fill(tokens(uT, w["q"]))
                for f in range(4):
                    fill(tokens(uT, wkf[:, f, :]))
                    fill(tokens(uT, wvf[:, f, :]))
            pe.wait_ge(stacked.sem, stacked.at(i, 2 * G))
            for h in range(heads):
                g, at = h // in_group, (h % in_group) * rows
                for q in range(NT):
                    n = h * NT + q
                    pe.wait_ge(maxed.sem, maxed.at(i, max(n - 1, 0)))
                    lo, hi = keys_of(q)
                    bank = abank[n % 2]
                    ins = nc.tensor.matmul(bank[:, lo:hi], qs[at:at + rows, g, q * P:(q + 1) * P], ks[at:at + rows, g, lo:hi], start=True, stop=not masked)
                    if masked:
                        ins = nc.tensor.matmul(bank[:, q * P:hi], c.ident_bf[:, :], mask_a[:, :], start=False, stop=True)
                    ins.then_inc(scored_a.sem, scored_a.one())
            if future:
                pe.wait_ge(m_final.sem, m_final.at(i, 1))
            else:
                pe.wait_ge(maxed.sem, maxed.at(i, units))
            n = use[0]
            pe.wait_ge(w_emptied.sem, w_emptied.at(i, n - 1))
            for q in range(NT):
                ins = nc.tensor.transpose(wbank[n % 2][0:heads, q * P:(q + 1) * P], negmax[:, q, :], c.ident[:, :])
            ins.then_inc(w_filled.sem, w_filled.one())
            use[0] += 1
            pe.wait_ge(m_copied.sem, m_copied.at(i, 2))

            def scores_b(h):
                g, at = h // in_group, (h % in_group) * rows
                for k in range(NT):
                    n = h * NT + k
                    pe.wait_ge(exped.sem, exped.at(i, max(n - 1, 0)))
                    lo, hi = queries_of(k)
                    bank = bbank[n % 2]
                    nc.tensor.matmul(bank[:, lo:hi], ks[at:at + rows, g, k * P:(k + 1) * P], qs[at:at + rows, g, lo:hi], start=True, stop=False)
                    ins = nc.tensor.matmul(bank[:, lo:hi], c.pick[0:48, h, :], mT[:, lo:hi], start=False, stop=not masked)
                    if masked:
                        ins = nc.tensor.matmul(bank[:, lo:lo + P], c.ident_bf[:, :], mask_b[:, :], start=False, stop=True)
                    ins.then_inc(scored_b.sem, scored_b.one())

            def values(h):
                pe.wait_ge(exped.sem, exped.at(i, NT * (h + 1)))
                if h == 0:
                    pe.wait_ge(w_emptied.sem, w_emptied.at(i, use_v + 1))
                    pe.wait_ge(sums_copied.sem, sums_copied.at(i, 0))
                side, b = h // half, h % half
                col = side * half * (R + E) + b * R
                for k in range(NT):
                    lo, hi = queries_of(k)
                    ins = nc.tensor.matmul(obank[side][0:R, lo:hi], vx_flat[:, k, col:col + R], pT[:, h % 2, k, lo:hi],
                                           start=b == 0 and k == 0, stop=b == half - 1 and k == NT - 1, skip_group_check=True)
                ins.then_inc(head_done.sem, head_done.one())

            scores_b(0)
            for h in range(heads):
                if h + 1 < heads:
                    scores_b(h + 1)
                values(h)
            for side in range(2):
                pe.wait_ge(sums_copied.sem, sums_copied.at(i, side + 1))

                def turn_sums(bank):
                    for q in range(NT):
                        ins = nc.tensor.transpose(bank[:, q * R:(q + 1) * R], sums[:, side, q * P:(q + 1) * P], c.ident[0:R, 0:R])
                    return ins
                fill(turn_sums)
            for s in range(len(out_steps)):
                if s > 0:
                    pe.wait_ge(step_taken.sem, step_taken.at(i, s))
                else:
                    pe.wait_ge(ctx_ready.sem, ctx_ready.at(i, 1))
                fill(turn(ctxt))
                pe.wait_ge(w_emptied.sem, w_emptied.at(i, use[0]))
                fill(tokens(stepT, w[out_steps[s]], w.get(out_steps[s] + "_b")))
            assert use[0] == W_USES
            turn_done(w_filled, scored_a, scored_b, head_done)

    @block.scalar
    def _(act):
        if future:
            act.wait_ge(prepared.sem, 1)
            nc.scalar.copy(afT[:, :, :], w0[:, :].rearrange("p (f n) -> p f n", f=4)).then_inc(prepared.sem, prepared.one())
            act.wait_ge(prepared.sem, 3)
            nc.scalar.copy(wkf[:, :, :], w1[:, :].rearrange("p (f n) -> p f n", f=4)).then_inc(prepared.sem, prepared.one())
            nc.scalar.copy(wvf[:, :, :], w0[:, :].rearrange("p (f n) -> p f n", f=4)).then_inc(prepared.sem, prepared.one())
        if bias or affine:
            wait_weights(act, c, w)
        if bias:
            act.wait_ge(prepared.sem, 2 if modulated else 1)
        with turns(act, B) as i:
            use = [0]

            def empty(emit):
                n = use[0]
                act.wait_ge(w_filled.sem, w_filled.at(i, n + 1))
                emit(wbank[n % 2]).then_inc(w_emptied.sem, w_emptied.one())
                use[0] += 1

            def tokens_to(dst):
                return lambda bank: nc.scalar.copy(dst, bank[:, :].rearrange("p (j d) -> p j d", j=NT))

            if affine:
                empty(lambda bank: nc.scalar.activation(uT[:, :], bank[:, :], ACT.Identity, bias=w["shift"], scale=w["gain"]))
            else:
                empty(lambda bank: nc.scalar.copy(uT[:, :], bank[:, :]))
            if modulated:
                for g in range(G):
                    if g == 0:
                        act.wait_ge(mod_scaled.sem, mod_scaled.at(i, 0))
                    empty(lambda bank: nc.scalar.activation(modT[:, g, :], bank[:, :], ACT.Sigmoid, bias=mod_bias[:, g:g + 1]))
            for g in range(2 * G):
                q_side = g < G
                k2 = g % 2
                act.wait_ge(stacked.sem, stacked.at(i, max(g - 1, 0)))
                m = w["maskq"] if q_side else w["maskk"]
                isc = scale if q_side else 1.0
                if modulated and q_side:
                    n = use[0]
                    act.wait_ge(w_filled.sem, w_filled.at(i, n + 1))
                    nc.scalar.activation(scaled[:, k2, :], wbank[n % 2][:, :], ACT.Identity, bias=sb_scaled[:, g:g + 1], scale=isc).then_inc(w_emptied.sem, w_emptied.one())
                    use[0] += 1
                    act.wait_ge(mod_scaled.sem, mod_scaled.at(i, g + 1))
                    nc.scalar.copy(high[:, k2, :], scaled[:, k2, :])
                    nc.scalar.mul(lowpart[:, k2, :], scaled[:, k2, :], m[1]).then_inc(parts_ready.sem, parts_ready.one())
                    continue

                n = use[0]
                act.wait_ge(w_filled.sem, w_filled.at(i, n + 1))
                bank = wbank[n % 2]
                nc.scalar.activation(high[:, k2, :], bank[:, :], ACT.Identity, bias=sb_scaled[:, g:g + 1] if bias else 0.0, scale=isc)
                nc.scalar.activation(lowpart[:, k2, :], bank[:, :], ACT.Identity, bias=sb_scaled[:, 2 * G + g:2 * G + g + 1] if bias else 0.0, scale=w["maskq_scaled"] if q_side else m[1]).then_inc(w_emptied.sem, w_emptied.one())
                use[0] += 1
            act.wait_ge(head_done.sem, head_done.at(i, 0))
            empty(lambda bank: nc.scalar.copy(vx[:, :, :, 0:hd], bank[:, :].rearrange("p (j h e) -> p j h e", j=NT, h=heads)))
            if future:
                act.wait_ge(ctx_ready.sem, ctx_ready.at(i, 0))
                empty(tokens_to(qtok[:, :, :]))
                for f in range(4):
                    empty(tokens_to(kf[:, f, :, :]))
                    empty(tokens_to(vf[:, f, :, :]))
            act.wait_ge(m_copied.sem, m_copied.at(i, 0))
            empty(lambda bank: nc.scalar.copy(mrow[:, :], bank[0:heads, :]))
            if future:
                act.wait_ge(fut_asked.sem, fut_asked.at(i, 1))
                nc.scalar.activation(pf[:, :, :, :], fut[:, :, :, :], ACT.Exp).then_inc(fut_exped.sem, fut_exped.one())
            for h in range(heads):
                act.wait_ge(head_done.sem, head_done.at(i, max(h - 1, 0)))
                for k in range(NT):
                    lo, hi = queries_of(k)
                    n = h * NT + k
                    act.wait_ge(scored_b.sem, scored_b.at(i, n + 1))
                    nc.scalar.activation(pT[:, h % 2, k, lo:hi], bbank[n % 2][:, lo:hi], ACT.Exp).then_inc(exped.sem, exped.one())
            for side in range(2):
                act.wait_ge(head_done.sem, head_done.at(i, (side + 1) * half))
                nc.scalar.copy(sums[:, side, :], obank[side][0:R, :]).then_inc(sums_copied.sem, sums_copied.one())
            for side in range(2):
                if side == 0:
                    act.wait_ge(ctx_ready.sem, ctx_ready.at(i, 0))
                empty(lambda bank: nc.scalar.copy(sums_tok[:, side, :, :, :], bank[:, 0:NT * R].rearrange("p (j b e) -> p j b e", j=NT, e=E)))
            for s in range(len(out_steps)):
                empty(lambda bank: nc.scalar.copy(stepT[:, :], bank[:, :]))
                act.wait_ge(step_taken.sem, step_taken.at(i, s))
                empty(tokens_to(stepo[:, :, :]))
            assert use[0] == W_USES

    @block.gpsimd
    def _(pool):
        with turns(pool, B) as i:
            for _ in range(norms):
                norm.on_gpsimd(nc, pool, c, i)

    @block.vector
    def _(dve):
        wait_weights(dve, c, w)
        nc.vector.memset(vx[:, :, :, :], 0.0)
        dve.drain()
        nc.vector.memset(vx[:, :, :, hd:E], 1.0)
        nc.vector.memset(mT[:, :].bitcast(F32), 0.0)
        if bias:
            nc.vector.tensor_scalar(sb_scaled[:, 0:G], w["bqk"][:, 0:G], scale, None, ALU.mult)
            nc.vector.tensor_copy(sb_scaled[:, G:2 * G], w["bqk"][:, G:2 * G])
            nc.vector.tensor_scalar(sb_scaled[:, 2 * G:3 * G], w["bqk"][:, 0:G], w["maskq"][1], scale, ALU.mult, ALU.mult)
            ins = nc.vector.tensor_scalar(sb_scaled[:, 3 * G:4 * G], w["bqk"][:, G:2 * G], w["maskk"][1], None, ALU.mult)
            if modulated:
                dve.wait_ge(prepared.sem, 1)
                nc.vector.tensor_tensor(mod_bias[:, :], w0[:, 0:G], w["cg_am_bias"][:, 0:G], ALU.add).then_inc(mod_added.sem, mod_added.one())
                dve.wait_ge(mod_added.sem, 1)
                ins = nc.vector.tensor_tensor(mod_bias[:, :], mod_bias[:, :], w["cg_am_bias"][:, G:2 * G], ALU.add)
            ins.then_inc(prepared.sem, prepared.one())
        with turns(dve, B) as i:
            def then(ins):
                ins.then_inc(step.sem, step.one())
                dve.wait_ge(step.sem, step.at(i, step.n))

            if source is None:
                dve.wait_ge(w_filled.sem, w_filled.at(i, 0))
                ins = norm.on_vector(nc, dve, c, i, lambda j: tile_of(c.x, i, j), lambda j: src[:, j, :], step)
                if affine:
                    then(ins)
                    ins = norm.on_vector(nc, dve, c, i, lambda j: src[:, j, :], lambda j: hsrc[:, j, :], step)
                ins.then_inc(src_ready.sem, src_ready.one())
            else:
                dve.wait_ge(w_filled.sem, w_filled.at(i, 0))
                nc.vector.tensor_copy(src[:, :, :], tiles_of(c.ctx, i)).then_inc(src_ready.sem, src_ready.one())
            use_q = 1 + (G if modulated else 0)
            for g in range(2 * G):
                q_side = g < G
                if modulated and q_side:
                    dve.wait_ge(w_emptied.sem, w_emptied.at(i, use_q + g + 1))
                    nc.vector.tensor_tensor(scaled[:, g % 2, :], scaled[:, g % 2, :], modT[:, g, :], ALU.mult).then_inc(mod_scaled.sem, mod_scaled.one())
                    dve.wait_ge(parts_ready.sem, parts_ready.at(i, g + 1))
                elif modulated:
                    dve.wait_ge(w_emptied.sem, w_emptied.at(i, use_q + g + 1))
                else:
                    dve.wait_ge(w_emptied.sem, w_emptied.at(i, use_q + g + 1))
                if g == 0:
                    dve.wait_ge(head_done.sem, head_done.at(i, 0))
                m = w["maskq"] if q_side else w["maskk"]
                dst = qs[:, g, :] if q_side else ks[:, g - G, :]
                nc.vector.scalar_tensor_tensor(out=dst, in0=high[:, g % 2, :].bitcast(F32), scalar=m[0], in1=lowpart[:, g % 2, :], op0=ALU.mult, op1=ALU.add).then_inc(stacked.sem, stacked.one())
            if future:
                base = use_v + 1
                for f in range(4):
                    dve.wait_ge(w_emptied.sem, w_emptied.at(i, base + 2 + 2 * f))
                    then(nc.vector.tensor_tensor(kf[:, f, :, :], kf[:, f, :, :], qtok[:, :, :], ALU.mult))
                    ins = nc.vector.tensor_reduce(fut[:, f, :, :], kf[:, f, :, :].rearrange("p j (h e) -> p j h e", h=heads), AX.X, ALU.add)
                then(ins)
                then(nc.vector.tensor_reduce(futmax[:, :, :], fut[:, :, :, :].rearrange("p f j h -> p j h f"), AX.X, ALU.max, negate=True))
            dve.wait_ge(w_filled.sem, w_filled.at(i, 0))
            for n in range(units):
                h, q = n // NT, n % NT
                dve.wait_ge(scored_a.sem, scored_a.at(i, n + 1))
                nc.vector.tensor_reduce(negmax[:, q, h:h + 1], abank[n % 2][:, keys_of(q)[0]:keys_of(q)[1]], AX.X, ALU.max, negate=True).then_inc(maxed.sem, maxed.one())
                ins = maxed.n
            dve.wait_ge(maxed.sem, maxed.at(i, units))
            if future:
                nc.vector.tensor_tensor(negmax[:, :, :], negmax[:, :, :], futmax[:, :, :], ALU.min).then_inc(m_final.sem, m_final.one())
                dve.wait_ge(m_final.sem, m_final.at(i, 1))
                nc.vector.tensor_tensor(fut[:, :, :, :], fut[:, :, :, :], negmax[:, :, :].unsqueeze(1).to_broadcast([P, 4, NT, heads]), ALU.add).then_inc(fut_asked.sem, fut_asked.one())
            use_m = use_v + 1 + (9 if future else 0)
            dve.wait_ge(w_emptied.sem, w_emptied.at(i, use_m + 1))
            dve.wait_ge(head_done.sem, head_done.at(i, 0))
            nc.vector.tensor_copy(mT[0:heads, :], mrow[:, :]).then_inc(m_copied.sem, m_copied.one())
            n = m_copied.n
            dve.wait_ge(m_copied.sem, m_copied.at(i, n))
            nc.vector.tensor_tensor(mT[32:32 + heads, :], mrow[:, :], mT[0:heads, :].bitcast(F32), ALU.subtract).then_inc(m_copied.sem, m_copied.one())
            if future:
                dve.wait_ge(fut_exped.sem, fut_exped.at(i, 1))
                for f in range(4):
                    ins = nc.vector.tensor_tensor(vf[:, f, :, :].rearrange("p j (h e) -> p (j h) e", h=heads), vf[:, f, :, :].rearrange("p j (h e) -> p (j h) e", h=heads),
                                                  pf[:, f, :, :].rearrange("p j h -> p (j h)").unsqueeze(2).to_broadcast([P, NT * heads, hd]), ALU.mult)
                nc.vector.tensor_reduce(futden[:, :, :], pf[:, :, :, :].rearrange("p f j h -> p j h f"), AX.X, ALU.add)
                then(ins)
                then(nc.vector.tensor_tensor(vf[:, 0:2, :, :], vf[:, 0:2, :, :], vf[:, 2:4, :, :], ALU.add))
                then(nc.vector.tensor_tensor(tmp[:, :, :], vf[:, 0, :, :], vf[:, 1, :, :], ALU.add))
            dve.wait_ge(w_emptied.sem, w_emptied.at(i, use_m + 3))
            if future:
                then(nc.vector.tensor_tensor(rden[:, :, :, :], sums_tok[:, :, :, :, hd], futden[:, :, :].rearrange("p j (s b) -> p s j b", s=2), ALU.add))
                then(nc.vector.reciprocal(rden[:, :, :, :], rden[:, :, :, :]))
            else:
                then(nc.vector.reciprocal(rden[:, :, :, :], sums_tok[:, :, :, :, hd]))
            for side in range(2):
                den = rden[:, side, :, :].unsqueeze(3).to_broadcast([P, NT, half, hd])
                part = slice(side * half * hd, (side + 1) * half * hd)
                dst = ctxt[:, :, part].rearrange("p j (b e) -> p j b e", b=half)
                if future:
                    more = tmp[:, :, part].rearrange("p j (b e) -> p j b e", b=half)
                    then(nc.vector.tensor_tensor(more, more, sums_tok[:, side, :, :, 0:hd], ALU.add))
                    ins = nc.vector.tensor_tensor(dst, more, den, ALU.mult)
                else:
                    ins = nc.vector.tensor_tensor(dst, sums_tok[:, side, :, :, 0:hd], den, ALU.mult)
            ins.then_inc(ctx_ready.sem, ctx_ready.one())
            dve.wait_ge(ctx_ready.sem, ctx_ready.at(i, 1))
            result = ctxt
            for s in range(len(out_steps)):
                kind = out_steps[s]
                dve.wait_ge(w_emptied.sem, w_emptied.at(i, use_m + 3 + 2 * (s + 1)))
                if kind == "mixed":
                    nc.vector.tensor_tensor(tmp[:, :, :], stepo[:, :, :], src[:, :, :], ALU.add).then_inc(step_taken.sem, step_taken.one())
                    dve.wait_ge(step_taken.sem, step_taken.at(i, s + 1))
                    then(norm.on_vector(nc, dve, c, i, lambda j: tmp[:, j, :], lambda j: ctxt[:, j, :], step))
                    then(nc.vector.tensor_tensor(ctxt[:, :, :], ctxt[:, :, :], wide(w["g1"]), ALU.mult))
                    then(nc.vector.tensor_tensor(tiles_of(c.y, i), ctxt[:, :, :], wide(w["be1"]), ALU.add))
                elif kind == "proj":
                    nc.vector.tensor_tensor(tiles_of(c.y, i), stepo[:, :, :], src[:, :, :], ALU.add).then_inc(step_taken.sem, step_taken.one())
                elif kind == "causal_out":
                    then(nc.vector.tensor_scalar(stepo[:, :, :], stepo[:, :, :], w["mix"][1], None, ALU.mult))
                    nc.vector.scalar_tensor_tensor(out=tiles_of(c.ctx, i), in0=tiles_of(c.ctx, i), scalar=w["mix"][0], in1=stepo[:, :, :], op0=ALU.mult, op1=ALU.add).then_inc(step_taken.sem, step_taken.one())
                elif kind == "meta_out":
                    then(nc.vector.tensor_scalar(stepo[:, :, :], stepo[:, :, :], w["mix"][1], None, ALU.mult))
                    nc.vector.scalar_tensor_tensor(out=ctxt[:, :, :], in0=src[:, :, :], scalar=w["mix"][0], in1=stepo[:, :, :], op0=ALU.mult, op1=ALU.add).then_inc(step_taken.sem, step_taken.one())
                else:
                    result = stepo
            if finish == "residual_norm":
                then(norm.on_vector(nc, dve, c, i, lambda j: result[:, j, :], lambda j: tmp[:, j, :], step))
                ins = nc.vector.tensor_tensor(tiles_of(c.x, i), tiles_of(c.x, i), tmp[:, :, :], ALU.add)
                if result is stepo:
                    ins.then_inc(step_taken.sem, step_taken.one())
                    dve.wait_ge(step_taken.sem, step_taken.at(i, len(out_steps)))
                else:
                    then(ins)
            elif finish == "context":
                then(nc.vector.tensor_copy(tiles_of(c.ctx, i), ctxt[:, :, :]))
            turn_done(step, stacked, maxed, m_copied, ctx_ready)
    ph.close()



class Layer:

    def __init__(self, kb, mb, W, func, scale=None, bias=None, V=None, v_op=None, v_arg=None):
        self.kb, self.mb, self.W, self.func, self.scale, self.bias = kb, mb, W, func, scale, bias
        self.V, self.v_op, self.v_arg = V, v_op, v_arg


def mlp_phase(nc, c, name, w, layers, final, experts=1, source="x", affine=False, shifted=False, gate=None,
              out_scale=False, add_y=False, tail_gain=False, finish="residual_norm"):
    ph = Phase(nc, name)
    S = ph.flag
    L = layers(0)
    gated = any(l.V is not None for l in L)
    moe = experts > 1
    top1 = gate == "top1"
    NA = 1 + experts * sum(l.mb for l in L) + top1
    NB = shifted + moe + experts * (1 + sum(l.mb for l in L if l.V is not None)) + top1
    widest = max(l.mb for l in L)
    norms = (source == "x" or affine or shifted) + (finish == "residual_norm") + tail_gain
    src = ph.sb("src", [P, NT, D])
    uT = ph.sb("uT", [P, T])
    hidden = [ph.sb(f"hidden{k}", [P, widest, T]) for k in range(2)]
    gates = ph.sb("gates", [P, 2, T]) if gated else None
    acc = ph.sb("acc", [P, NT, D])
    tmp = ph.sb("tmp", [P, NT, D])
    if moe:
        logit = ph.sb("logit", [P, NT, 8])
        chosen = ph.sb("chosen", [P, NT, 8])
        second = ph.sb("second", [P, NT, 8])
        small = ph.sb("small", [P, 4, NT])
        chosenT = ph.sb("chosenT", [8, T])
    ring_a, ring_b = c.bank[0:4], c.bank[4:8]
    a_filled, a_emptied, b_filled, b_emptied = S("a_filled", NA), S("a_emptied", NA), S("b_filled", NB), S("b_emptied", NB)
    src_ready, expected, exped = S("src_ready"), S("exp_asked"), S("gate_exped")
    chosen_ready = S("chosen_ready")
    steps = {"residual_norm": 2}.get(finish, 0) + 3 * tail_gain + {None: 0, "top1": 4, "top2": 18}[gate]
    step = S("dve_step", steps)
    norm = Norm(ph, max(norms, 1))
    block = ph.block()

    @block.sync
    def _(sp):
        load_next(sp, c)

    def order():
        out = []
        for e in range(experts):
            out.append(("up", e))
            if e == 0 and top1:
                out.append(("chosen", 0))
            if e > 0:
                out.append(("down", e - 1))
        return out + [("down", experts - 1)]

    @block.tensor
    def _(pe):
        wait_weights(pe, c, w)
        with turns(pe, B) as i:
            na, nb = [0], [0]

            def fill(ring, n, filled, emptied, emit):
                pe.wait_ge(emptied.sem, emptied.at(i, max(n[0] - 3, 0)))
                emit(ring[n[0] % 4]).then_inc(filled.sem, filled.one())
                n[0] += 1

            fill_a = lambda emit: fill(ring_a, na, a_filled, a_emptied, emit)
            fill_b = lambda emit: fill(ring_b, nb, b_filled, b_emptied, emit)
            if shifted:
                def shift_tokens(bank):
                    for j in range(NT):
                        dst = bank[:, j * H2:(j + 1) * H2]
                        ins = nc.tensor.matmul(dst, c.shift[:, 0, :], i.tile(c.y, j)[:, :, H2:D], start=True, stop=j == 0)
                        if j > 0:
                            ins = nc.tensor.matmul(dst, c.shift[:, 1, :], i.tile(c.y, j - 1)[:, :, H2:D], start=False, stop=True)
                    return ins
                fill_b(shift_tokens)
            pe.wait_ge(src_ready.sem, src_ready.at(i, 1))

            def turn(bank):
                for j in range(NT):
                    ins = nc.tensor.transpose(bank[:, j * P:(j + 1) * P], src[:, j, :], c.ident[:, :])
                return ins
            fill_a(turn)
            pe.wait_ge(a_emptied.sem, a_emptied.at(i, 1))
            if moe:
                def logits(bank):
                    for j in range(NT):
                        ins = nc.tensor.matmul(bank[:, j * 8:(j + 1) * 8], uT[:, j * P:(j + 1) * P], w["gate"], start=True, stop=True)
                    return ins
                fill_b(logits)
            ready = {}

            def product(bank, W, m, kb, src_of):
                for k in range(kb):
                    ins = nc.tensor.matmul(bank[:, :], W(k, m), src_of(k), start=k == 0, stop=k == kb - 1)
                return ins

            for what, e in order():
                if what == "up":
                    src_of = lambda k: uT[:, :]
                    for l, layer in enumerate(layers(e)):
                        for m in range(layer.mb):
                            fill_a(lambda bank: product(bank, layer.W, m, layer.kb, src_of))
                            if layer.V is not None:
                                fill_b(lambda bank: product(bank, layer.V, m, layer.kb, src_of))
                        buf = hidden[(e + l) % 2]
                        ready[e] = (b_emptied, nb[0]) if layer.V is not None else (a_emptied, na[0])
                        src_of = (lambda b: lambda k: b[:, k, :])(buf)
                        if l + 1 < len(layers(e)):
                            pe.wait_ge(ready[e][0].sem, ready[e][0].at(i, ready[e][1]))
                elif what == "chosen":
                    pe.wait_ge(chosen_ready.sem, chosen_ready.at(i, 1))

                    def turn_chosen(bank):
                        for j in range(NT):
                            ins = nc.tensor.transpose(bank[0:8, j * P:(j + 1) * P], chosen[:, j, :], c.ident[:, :])
                        return ins
                    fill_a(turn_chosen)
                    pe.wait_ge(a_emptied.sem, a_emptied.at(i, na[0]))

                    def chosen_bias(bank):
                        for j in range(NT):
                            ins = nc.tensor.matmul(bank[:, j * P:(j + 1) * P], chosenT[:, j * P:(j + 1) * P], w["expert_bias"], start=True, stop=True)
                        return ins
                    fill_b(chosen_bias)
                else:
                    pe.wait_ge(ready[e][0].sem, ready[e][0].at(i, ready[e][1]))
                    kb, W = final(e)
                    buf = hidden[(e + len(L) - 1) % 2]

                    def down(bank):
                        for j in range(NT):
                            for k in range(kb):
                                ins = nc.tensor.matmul(bank[:, j * P:(j + 1) * P], buf[:, k, j * P:(j + 1) * P], W(k), start=k == 0, stop=k == kb - 1 and "final_b" not in w)
                            if "final_b" in w:
                                ins = nc.tensor.matmul(bank[:, j * P:(j + 1) * P], c.ones[0:1, :], w["final_b"], start=False, stop=True)
                        return ins
                    fill_b(down)
            turn_done(a_filled, b_filled)

    @block.scalar
    def _(act):
        wait_weights(act, c, w)
        with turns(act, B) as i:
            na, nb = [0], [shifted + moe]

            def empty(emit):
                act.wait_ge(a_filled.sem, a_filled.at(i, na[0] + 1))
                emit(ring_a[na[0] % 4]).then_inc(a_emptied.sem, a_emptied.one())
                na[0] += 1
            if affine:
                empty(lambda bank: nc.scalar.activation(uT[:, :], bank[:, :], ACT.Identity, bias=w["shift"], scale=w["gain"]))
            else:
                empty(lambda bank: nc.scalar.copy(uT[:, :], bank[:, :]))
            if gate == "top2":
                act.wait_ge(expected.sem, expected.at(i, 1))
                nc.scalar.activation(logit[:, :, :], logit[:, :, :], ACT.Exp).then_inc(exped.sem, exped.one())
            for what, e in order():
                if what == "up":
                    for l, layer in enumerate(layers(e)):
                        for m in range(layer.mb):
                            if layer.V is not None:
                                k = nb[0]
                                act.wait_ge(b_emptied.sem, b_emptied.at(i, max(k - 1, 0)))
                                dst = gates[:, nb[0] % 2, :]
                                nb[0] += 1
                            else:
                                dst = hidden[(e + l) % 2][:, m, :]
                            kw = {}
                            if layer.scale is not None:
                                kw["scale"] = layer.scale(m)
                            if layer.bias is not None:
                                kw["bias"] = layer.bias(m)
                            empty(lambda bank: nc.scalar.activation(dst, bank[:, :], layer.func, **kw))
                elif what == "chosen":
                    empty(lambda bank: nc.scalar.copy(chosenT[:, :], bank[0:8, :]))
                    nb[0] += 1
                else:
                    nb[0] += 1
            turn_done(a_emptied)

    @block.gpsimd
    def _(pool):
        with turns(pool, B) as i:
            for _ in range(norms):
                norm.on_gpsimd(nc, pool, c, i)

    @block.vector
    def _(dve):
        wait_weights(dve, c, w)
        with turns(dve, B) as i:
            na, nb = [1], [0]

            def then(ins):
                ins.then_inc(step.sem, step.one())
                dve.wait_ge(step.sem, step.at(i, step.n))

            def emptyb(emit):
                dve.wait_ge(b_filled.sem, b_filled.at(i, nb[0] + 1))
                ins = emit(ring_b[nb[0] % 4])
                ins.then_inc(b_emptied.sem, b_emptied.one())
                n = b_emptied.n
                nb[0] += 1
                return n
            dve.wait_ge(a_filled.sem, a_filled.at(i, 0))
            whole = c.x if source == "x" else c.y
            if shifted:
                def take_shifted(bank):
                    nc.vector.tensor_copy(src[:, :, 0:H2], tiles_of(c.y, i)[:, :, 0:H2])
                    return nc.vector.tensor_copy(src[:, :, H2:D], bank[:, 0:NT * H2].rearrange("p (j d) -> p j d", j=NT))
                n = emptyb(take_shifted)
                dve.wait_ge(b_emptied.sem, b_emptied.at(i, n))
                norm.on_vector(nc, dve, c, i, lambda j: src[:, j, :], lambda j: src[:, j, :], step).then_inc(src_ready.sem, src_ready.one())
            elif source == "x" or affine:
                ins = norm.on_vector(nc, dve, c, i, lambda j: tile_of(whole, i, j), lambda j: src[:, j, :], step)
                ins.then_inc(src_ready.sem, src_ready.one())
            else:
                nc.vector.tensor_copy(src[:, :, :], tiles_of(whole, i)).then_inc(src_ready.sem, src_ready.one())
            if moe:
                bc = lambda a: a.unsqueeze(2).to_broadcast([P, NT, 8])
                down8 = c.down8[:, :].unsqueeze(1).to_broadcast([P, NT, 8])
                if gate == "top2":
                    dve.wait_ge(b_emptied.sem, b_emptied.at(i, 0))
                n = emptyb(lambda bank: nc.vector.tensor_copy(logit[:, :, :], bank[:, 0:8 * NT].rearrange("p (j e) -> p j e", e=8)))
                dve.wait_ge(b_emptied.sem, b_emptied.at(i, n))

                def first_of(values, largest, dst):
                    then(nc.vector.tensor_tensor(dst, values, bc(largest), ALU.is_ge))
                    then(nc.vector.tensor_tensor(dst, dst, down8, ALU.mult))
                    then(nc.vector.tensor_reduce(small[:, 3, :], dst, AX.X, ALU.max))
                    return nc.vector.tensor_tensor(dst, dst, bc(small[:, 3, :]), ALU.is_equal)

                then(nc.vector.tensor_reduce(small[:, 0, :], logit[:, :, :], AX.X, ALU.max))
                if gate == "top1":
                    first_of(logit[:, :, :], small[:, 0, :], chosen[:, :, :]).then_inc(chosen_ready.sem, chosen_ready.one())
                    dve.wait_ge(chosen_ready.sem, chosen_ready.at(i, 1))
                else:
                    nc.vector.tensor_tensor(logit[:, :, :], logit[:, :, :], bc(small[:, 0, :]), ALU.subtract).then_inc(expected.sem, expected.one())
                    dve.wait_ge(exped.sem, exped.at(i, 1))
                    then(nc.vector.tensor_reduce(small[:, 0, :], logit[:, :, :], AX.X, ALU.add))
                    then(nc.vector.reciprocal(small[:, 0, :], small[:, 0, :]))
                    then(nc.vector.tensor_tensor(logit[:, :, :], logit[:, :, :], bc(small[:, 0, :]), ALU.mult))
                    then(nc.vector.tensor_reduce(small[:, 0, :], logit[:, :, :], AX.X, ALU.max))
                    then(first_of(logit[:, :, :], small[:, 0, :], chosen[:, :, :]))
                    then(nc.vector.scalar_tensor_tensor(out=second[:, :, :], in0=chosen[:, :, :], scalar=-2.0, in1=logit[:, :, :], op0=ALU.mult, op1=ALU.add))
                    then(nc.vector.tensor_reduce(small[:, 1, :], second[:, :, :], AX.X, ALU.max))
                    nc.vector.tensor_tensor(small[:, 2, :], small[:, 0, :], small[:, 1, :], ALU.add)
                    then(first_of(second[:, :, :], small[:, 1, :], second[:, :, :]))
                    nc.vector.tensor_tensor(chosen[:, :, :], chosen[:, :, :], second[:, :, :], ALU.add)
                    then(nc.vector.tensor_scalar(small[:, 2, :], small[:, 2, :], 1e-8, None, ALU.add))
                    nc.vector.tensor_tensor(chosen[:, :, :], chosen[:, :, :], logit[:, :, :], ALU.mult)
                    then(nc.vector.reciprocal(small[:, 2, :], small[:, 2, :]))
                    then(nc.vector.tensor_tensor(chosen[:, :, :], chosen[:, :, :], bc(small[:, 2, :]), ALU.mult))
            for what, e in order():
                if what == "up":
                    for l, layer in enumerate(layers(e)):
                        for m in range(layer.mb):
                            na[0] += 1
                            if layer.V is not None:
                                dve.wait_ge(a_emptied.sem, a_emptied.at(i, na[0]))
                                g = gates[:, nb[0] % 2, :]
                                arg = layer.v_arg(m) if layer.v_arg is not None else 1.0
                                emptyb(lambda bank: nc.vector.scalar_tensor_tensor(out=hidden[(e + l) % 2][:, m, :], in0=bank[:, :], scalar=arg, in1=g, op0=layer.v_op or ALU.mult, op1=ALU.mult))
                elif what == "chosen":
                    na[0] += 1
                    n = emptyb(lambda bank: nc.vector.tensor_tensor(acc[:, :, :], bank[:, :].rearrange("p (j d) -> p j d", j=NT), src[:, :, :], ALU.add))
                    dve.wait_ge(b_emptied.sem, b_emptied.at(i, n))
                elif moe:
                    def add(bank):
                        for j in range(NT):
                            part = bank[:, j * P:(j + 1) * P]
                            if e == 0 and not top1:
                                ins = nc.vector.tensor_scalar(acc[:, j, :], part, chosen[:, j, e:e + 1], None, ALU.mult)
                            else:
                                ins = nc.vector.scalar_tensor_tensor(out=acc[:, j, :], in0=part, scalar=chosen[:, j, e:e + 1], in1=acc[:, j, :], op0=ALU.mult, op1=ALU.add)
                        return ins
                    n = emptyb(add)
                    dve.wait_ge(b_emptied.sem, b_emptied.at(i, n))
                else:
                    def take(bank):
                        part = bank[:, :].rearrange("p (j d) -> p j d", j=NT)
                        if out_scale:
                            return nc.vector.tensor_tensor(acc[:, :, :], part, wide(w["out_scale"]), ALU.mult)
                        dst = tiles_of(c.y, i) if finish == "y" else acc[:, :, :]
                        return nc.vector.tensor_tensor(dst, part, tiles_of(c.y, i), ALU.add)
                    n = emptyb(take)
                    dve.wait_ge(b_emptied.sem, b_emptied.at(i, n))
            if tail_gain:
                then(norm.on_vector(nc, dve, c, i, lambda j: acc[:, j, :], lambda j: tmp[:, j, :], step))
                then(nc.vector.tensor_tensor(tmp[:, :, :], tmp[:, :, :], wide(w["g2"]), ALU.mult))
                then(nc.vector.tensor_tensor(acc[:, :, :], tmp[:, :, :], wide(w["be2"]), ALU.add))
            if finish == "residual_norm":
                then(norm.on_vector(nc, dve, c, i, lambda j: acc[:, j, :], lambda j: tmp[:, j, :], step))
                then(nc.vector.tensor_tensor(tiles_of(c.x, i), tiles_of(c.x, i), tmp[:, :, :], ALU.add))
            turn_done(b_emptied, step)
    ph.close()



def local_attention_phase(nc, c, name, w, first):
    heads, hd = 8, 64
    E = hd + 1
    inner = heads * hd
    BLK = inner // P
    SPAN = P + hd
    units = NT * heads
    ph = Phase(nc, name)
    S = ph.flag
    W_USES = 1 + 3 * NT + 2 * NT + 1 + NT + 1
    src = ph.sb("src", [P, NT, D])
    uT = ph.sb("uT", [P, T])
    raw = ph.sb("raw", [P, 2, 2, heads, hd])
    square = ph.sb("square", [P, 2, heads, hd])
    turned = ph.sb("turned", [P, 2, 2, heads, hd])
    inv = ph.sb("inv", [P, 2, 2 * heads])
    cosines = ph.sb("cosines", [P, NT, 2, hd])
    sines = ph.sb("sines", [P, NT, 2, hd])
    qT = ph.sb("qT", [P, BLK, T])
    kT = ph.sb("kT", [P, BLK, T])
    vx = ph.sb("vx", [P, NT, heads, E])
    negmax = ph.sb("negmax", [P, NT, heads])
    mrow = ph.sb("mrow", [heads, T])
    mT = ph.sb("mT", [P, T], F32R)
    pT = ph.sb("pT", [P, 2, heads, SPAN])
    rden = ph.sb("rden", [P, 2, heads])
    stepo = ph.sb("stepo", [P, NT, D])
    ctxt = c.ctx[:, 0:NT * BLK, :].rearrange("p (j b) d -> p j (b d)", j=NT)
    ctxT = c.ctx[:, NT * BLK:2 * NT * BLK, :].rearrange("p (b j) d -> p b (j d)", b=BLK)

    wbank = (c.bank[0], c.bank[1])
    sbank = (c.bank[2], c.bank[3])
    obank = ((c.bank[4], c.bank[5]), (c.bank[6], c.bank[7]))
    tables = S("tables", 0)
    src_ready = S("src_ready")
    w_filled, w_emptied = S("w_filled", W_USES), S("w_emptied", W_USES)
    squared, summed, inverted = S("squared", 2 * NT), S("summed", 2 * NT), S("inverted", 2 * NT)
    floored = S("floored", NT)
    sines_done, rotated = S("sines_done", NT), S("rotated", NT)
    scored_a, maxed = S("scored_a", units), S("maxed", units)
    m_copied = S("m_copied", 2)
    scored_b, exped = S("scored_b", units), S("exped", units)
    tile_done, o_taken = S("tile_done", NT), S("o_taken", NT)
    step = S("dve_step", 3 * NT)
    stored = S("stored")
    norm = Norm(ph, 1)
    block = ph.block()

    def keys_of(q):
        return max(q * P - hd, 0), (q + 1) * P

    def queries_of(k):
        return k * P, min(k * P + SPAN, T)

    def order():
        out = [("qkv", 0)]
        for j in range(1, NT):
            out += [("qkv", j), ("turn", j - 1)]
        return out + [("turn", NT - 1)]

    @block.sync
    def _(sp):
        load_next(sp, c)

    @block.tensor
    def _(pe):
        wait_weights(pe, c, w)
        with turns(pe, B) as i:
            use = [0]

            def fill(emit):
                n = use[0]
                pe.wait_ge(w_emptied.sem, w_emptied.at(i, max(n - 1, 0)))
                emit(wbank[n % 2]).then_inc(w_filled.sem, w_filled.one())
                use[0] += 1

            def turn(tiles, width=P):
                def emit(bank):
                    for k, t in enumerate(tiles):
                        ins = nc.tensor.transpose(bank[0:width, k * P:(k + 1) * P], t, c.ident[:, :])
                    return ins
                return emit

            pe.wait_ge(src_ready.sem, src_ready.at(i, 1))
            fill(turn([src[:, j, :] for j in range(NT)]))
            pe.wait_ge(w_emptied.sem, w_emptied.at(i, 1))
            for what, j in order():
                if what == "qkv":
                    for part in range(3):
                        fill(lambda bank: nc.tensor.matmul(bank[:, :], uT[:, j * P:(j + 1) * P], w["qkv"][:, part * inner:(part + 1) * inner], start=True, stop=True))
                else:
                    pe.wait_ge(rotated.sem, rotated.at(i, j + 1))
                    for side in range(2):
                        flat = turned[:, j % 2, side, :, :].rearrange("p h d -> p (h d)")
                        fill(turn([flat[:, b * P:(b + 1) * P] for b in range(BLK)]))
            pe.wait_ge(w_emptied.sem, w_emptied.at(i, use[0]))
            pe.wait_ge(exped.sem, exped.at(i, 0))
            for q in range(NT):
                lo, hi = keys_of(q)
                for h in range(heads):
                    n, at = q * heads + h, h % 2 * hd
                    pe.wait_ge(maxed.sem, maxed.at(i, max(n - 1, 0)))
                    bank = sbank[n % 2]
                    nc.tensor.matmul(bank[:, 0:hi - lo], qT[at:at + hd, h // 2, q * P:(q + 1) * P], kT[at:at + hd, h // 2, lo:hi], start=True, stop=False)
                    nc.tensor.matmul(bank[:, 0:hi - lo], c.ident_bf[:, :], c.far_keys[:, SPAN - (hi - lo):SPAN], start=False, stop=True).then_inc(scored_a.sem, scored_a.one())
            pe.wait_ge(maxed.sem, maxed.at(i, units))
            fill(turn([negmax[:, q, :] for q in range(NT)], heads))
            pe.wait_ge(m_copied.sem, m_copied.at(i, 2))

            def scores_b(k, h):
                n, at = k * heads + h, h % 2 * hd
                lo, hi = queries_of(k)
                pe.wait_ge(exped.sem, exped.at(i, max(n - 1, 0)))
                bank = sbank[n % 2]
                nc.tensor.matmul(bank[:, 0:hi - lo], kT[at:at + hd, h // 2, k * P:(k + 1) * P], qT[at:at + hd, h // 2, lo:hi], start=True, stop=False)
                nc.tensor.matmul(bank[:, 0:hi - lo], c.pick[:, h, :], mT[:, lo:hi], start=False, stop=False)
                nc.tensor.matmul(bank[:, 0:hi - lo], c.ident_bf[:, :], c.far_queries[:, 0:hi - lo], start=False, stop=True).then_inc(scored_b.sem, scored_b.one())

            def values(q, h):
                pe.wait_ge(exped.sem, exped.at(i, q * heads + h + 1))
                if h == 0:
                    pe.wait_ge(o_taken.sem, o_taken.at(i, max(q - 1, 0)))
                dst = obank[q % 2][h // 4][:, h % 4 * E:(h % 4 + 1) * E]
                ins = nc.tensor.matmul(dst, pT[:, q % 2, h, 0:P], vx[:, q, h, :], start=True, stop=True)
                if q > 0:
                    ins = nc.tensor.matmul(dst[0:hd, :], pT[:, (q - 1) % 2, h, P:SPAN], vx[:, q - 1, h, :], start=False, stop=True, skip_group_check=True)
                if h == heads - 1:
                    ins.then_inc(tile_done.sem, tile_done.one())

            for k in range(NT):
                for h in range(heads):
                    scores_b(k, h)
                    if h >= 2:
                        values(k, h - 2)
                values(k, heads - 2)
                values(k, heads - 1)
            for j in range(NT):
                pe.wait_ge(o_taken.sem, o_taken.at(i, j + 1))
                fill(turn([ctxt[:, j, b * P:(b + 1) * P] for b in range(BLK)]))
            pe.wait_ge(w_emptied.sem, w_emptied.at(i, use[0]))

            def out(bank):
                for j in range(NT):
                    for b in range(BLK):
                        ins = nc.tensor.matmul(bank[:, j * P:(j + 1) * P], ctxT[:, b, j * P:(j + 1) * P], w["wo"][:, b * P:(b + 1) * P], start=b == 0, stop=b == BLK - 1)
                return ins
            fill(out)
            assert use[0] == W_USES
            turn_done(w_filled, scored_a, scored_b, tile_done)

    @block.scalar
    def _(act):
        with turns(act, B) as i:
            use = [0]

            def empty(emit):
                n = use[0]
                act.wait_ge(w_filled.sem, w_filled.at(i, n + 1))
                emit(wbank[n % 2]).then_inc(w_emptied.sem, w_emptied.one())
                use[0] += 1

            def take_shifted(bank):
                nc.scalar.copy(uT[0:H2, :], bank[0:H2, :])
                return nc.scalar.copy(uT[H2:P, 1:T], bank[H2:P, 0:T - 1])
            if True:
                act.wait_ge(tables.sem, 3)
            empty(take_shifted)
            for what, j in order():
                if what == "qkv":
                    for side in range(2):
                        n = use[0]
                        if side == 0:
                            act.wait_ge(rotated.sem, rotated.at(i, max(j - 1, 0)))
                        act.wait_ge(w_filled.sem, w_filled.at(i, n + 1))
                        nc.scalar.copy(raw[:, j % 2, side, :, :], wbank[n % 2][:, :].rearrange("p (h d) -> p h d", h=heads))
                        act.wait_ge(summed.sem, summed.at(i, max(2 * j - 1 + side, 0)))
                        nc.scalar.activation(square[:, side, :, :], wbank[n % 2][:, :].rearrange("p (h d) -> p h d", h=heads), ACT.Square).then_inc(w_emptied.sem, w_emptied.one())
                        use[0] += 1
                    if j == 0:
                        act.wait_ge(tile_done.sem, tile_done.at(i, 0))
                    empty(lambda bank: nc.scalar.copy(vx[:, j, :, 0:hd], bank[:, :].rearrange("p (h d) -> p h d", h=heads)))
                else:
                    for dst in (qT, kT):
                        empty(lambda bank: nc.scalar.copy(dst[:, :, j * P:(j + 1) * P], bank[:, :].rearrange("p (b n) -> p b n", b=BLK)))
            act.wait_ge(m_copied.sem, m_copied.at(i, 0))
            empty(lambda bank: nc.scalar.copy(mrow[:, :], bank[0:heads, :]))
            for k in range(NT):
                for h in range(heads):
                    n = k * heads + h
                    lo, hi = queries_of(k)
                    if h == 0:
                        act.wait_ge(tile_done.sem, tile_done.at(i, max(k - 1, 0)))
                    act.wait_ge(scored_b.sem, scored_b.at(i, n + 1))
                    nc.scalar.activation(pT[:, k % 2, h, 0:hi - lo], sbank[n % 2][:, 0:hi - lo], ACT.Exp).then_inc(exped.sem, exped.one())
            for j in range(NT):
                empty(lambda bank: nc.scalar.copy(ctxT[:, :, j * P:(j + 1) * P], bank[:, :].rearrange("p (b n) -> p b n", b=BLK)))
            act.wait_ge(stored.sem, stored.at(i, 0))
            empty(lambda bank: nc.scalar.copy(stepo[:, :, :], bank[:, :].rearrange("p (j d) -> p j d", j=NT)))
            assert use[0] == W_USES

    @block.gpsimd
    def _(pool):
        pool.wait_ge(tables.sem, 3)
        with turns(pool, B) as i:
            if first:
                norm.on_gpsimd(nc, pool, c, i)
            for j in range(NT):
                pool.wait_ge(floored.sem, floored.at(i, j + 1))
                nc.gpsimd.tensor_tensor(inv[:, j % 2, :], inv[:, j % 2, :], c.minus_half16[:, :], ALU.pow).then_inc(inverted.sem, inverted.one())
                sin = sines[:, j, :, :].unsqueeze(2).to_broadcast([P, 2, heads, hd])
                nc.gpsimd.tensor_tensor(turned[:, j % 2, :, :, 0:hd // 2], raw[:, j % 2, :, :, hd // 2:hd], sin[:, :, :, 0:hd // 2], ALU.mult)
                nc.gpsimd.tensor_tensor(turned[:, j % 2, :, :, hd // 2:hd], raw[:, j % 2, :, :, 0:hd // 2], sin[:, :, :, hd // 2:hd], ALU.mult).then_inc(sines_done.sem, sines_done.one())

    @block.vector
    def _(dve):
        wait_weights(dve, c, w)
        nc.vector.memset(vx[:, :, :, hd:E], 1.0)
        nc.vector.memset(mT[:, :].bitcast(F32), 0.0)
        nc.vector.memset(inv[:, :, :], 1.0)
        nc.vector.memset(uT[H2:P, 0:1], 0.0).then_inc(tables.sem, tables.one())
        rows = lambda t: t.rearrange("p (j s d) -> p j s d", j=NT, s=2)
        gains = lambda t: t.rearrange("p (s d) -> p s d", s=2).unsqueeze(1).to_broadcast([P, NT, 2, hd])
        nc.vector.tensor_tensor(cosines[:, :, :, :], rows(w["cosines"]), gains(w["gains"]), ALU.mult).then_inc(tables.sem, tables.one())
        nc.vector.tensor_tensor(sines[:, :, :, :], rows(w["sines"]), gains(w["gains_turned"]), ALU.mult).then_inc(tables.sem, tables.one())
        dve.wait_ge(tables.sem, 3)
        with turns(dve, B) as i:
            def then(ins):
                ins.then_inc(step.sem, step.one())
                dve.wait_ge(step.sem, step.at(i, step.n))

            dve.wait_ge(stored.sem, stored.at(i, 0))
            if first:
                norm.on_vector(nc, dve, c, i, lambda j: tile_of(c.x, i, j), lambda j: src[:, j, :], step).then_inc(src_ready.sem, src_ready.one())
            else:
                nc.vector.tensor_copy(src[:, :, :], tiles_of(c.y, i)).then_inc(src_ready.sem, src_ready.one())
            at_use = 1
            seen = {}
            for what, j in order():
                seen[what, j] = at_use
                at_use += 3 if what == "qkv" else 2
            for j in range(NT):
                for side in range(2):
                    dve.wait_ge(w_emptied.sem, w_emptied.at(i, seen["qkv", j] + side + 1))
                    nc.vector.tensor_reduce(inv[:, j % 2, side * heads:(side + 1) * heads], square[:, side, :, :], AX.X, ALU.add).then_inc(summed.sem, summed.one())
                dve.wait_ge(summed.sem, summed.at(i, 2 * (j + 1)))
                nc.vector.tensor_scalar(inv[:, j % 2, :], inv[:, j % 2, :], 1e-24, None, ALU.max).then_inc(floored.sem, floored.one())
                dve.wait_ge(sines_done.sem, sines_done.at(i, j + 1))
                cos = cosines[:, j, :, :].unsqueeze(2).to_broadcast([P, 2, heads, hd])
                r = raw[:, j % 2, :, :, :]
                t = turned[:, j % 2, :, :, :]
                then(nc.vector.tensor_tensor(r, r, cos, ALU.mult))
                then(nc.vector.tensor_tensor(t, t, r, ALU.add))
                t = t.rearrange("p s h d -> p (s h) d")
                nc.vector.tensor_tensor(t, t, inv[:, j % 2, :].unsqueeze(2).to_broadcast([P, 2 * heads, hd]), ALU.mult).then_inc(rotated.sem, rotated.one())
            for n in range(units):
                q, h = n // heads, n % heads
                lo, hi = keys_of(q)
                dve.wait_ge(scored_a.sem, scored_a.at(i, n + 1))
                nc.vector.tensor_reduce(negmax[:, q, h:h + 1], sbank[n % 2][:, 0:hi - lo], AX.X, ALU.max, negate=True).then_inc(maxed.sem, maxed.one())
            dve.wait_ge(w_emptied.sem, w_emptied.at(i, at_use + 1))
            nc.vector.tensor_copy(mT[0:heads, :], mrow[:, :]).then_inc(m_copied.sem, m_copied.one())
            n = m_copied.n
            dve.wait_ge(m_copied.sem, m_copied.at(i, n))
            nc.vector.tensor_tensor(mT[32:32 + heads, :], mrow[:, :], mT[0:heads, :].bitcast(F32), ALU.subtract).then_inc(m_copied.sem, m_copied.one())
            for q in range(NT):
                dve.wait_ge(tile_done.sem, tile_done.at(i, q + 1))
                for b in range(2):
                    o = obank[q % 2][b][:, 0:4 * E].rearrange("p (h e) -> p h e", e=E)
                    ins = nc.vector.reciprocal(rden[:, q % 2, 4 * b:4 * b + 4], o[:, :, hd])
                then(ins)
                for b in range(2):
                    o = obank[q % 2][b][:, 0:4 * E].rearrange("p (h e) -> p h e", e=E)
                    dst = ctxt[:, q, b * 4 * hd:(b + 1) * 4 * hd].rearrange("p (h e) -> p h e", e=hd)
                    ins = nc.vector.tensor_tensor(dst, o[:, :, 0:hd], rden[:, q % 2, 4 * b:4 * b + 4].unsqueeze(2).to_broadcast([P, 4, hd]), ALU.mult)
                ins.then_inc(o_taken.sem, o_taken.one())
            dve.wait_ge(w_emptied.sem, w_emptied.at(i, W_USES))
            nc.vector.tensor_tensor(tiles_of(c.y, i), stepo[:, :, :], src[:, :, :], ALU.add).then_inc(stored.sem, stored.one())
            assert step.n == step.per, step.n
            turn_done(maxed, m_copied, o_taken, rotated, floored)
    ph.close()



def linear_attention_phase(nc, c, name, w):
    heads, hd = 16, 8
    F = D + heads
    W_USES = 4
    ph = Phase(nc, name)
    S = ph.flag
    src = ph.sb("src", [P, NT, D])
    uT, qT = ph.sb("uT", [P, T]), ph.sb("qT", [P, T])
    ktok = ph.sb("ktok", [P, NT, D])
    vtok = ph.sb("vtok", [P, NT, D + 1])
    kv = ph.sb("kv", [P, F])
    kv_sum = ph.sb("kv_sum", [P, 1])
    den = ph.sb("den", [P, NT, heads])
    acc, tmp = ph.sb("acc", [P, NT, D]), ph.sb("tmp", [P, NT, D])
    wbank = (c.bank[0], c.bank[1])
    kvbank, obank = c.bank[2], (c.bank[3], c.bank[4])
    src_ready = S("src_ready")
    w_filled, w_emptied = S("w_filled", W_USES), S("w_emptied", W_USES)
    kv_summed, kv_ready = S("kv_summed"), S("kv_ready", 2)
    context, o_taken = S("context"), S("o_taken")
    ready = S("ready", 0)
    step = S("dve_step", 9)
    norm = Norm(ph, 3)
    block = ph.block()

    @block.sync
    def _(sp):
        load_next(sp, c)

    @block.tensor
    def _(pe):
        wait_weights(pe, c, w)
        pe.wait_ge(ready.sem, 1)
        with turns(pe, B) as i:
            n = [0]

            def fill(emit):
                pe.wait_ge(w_emptied.sem, w_emptied.at(i, max(n[0] - 1, 0)))
                emit(wbank[n[0] % 2]).then_inc(w_filled.sem, w_filled.one())
                n[0] += 1

            def turn(bank):
                for j in range(NT):
                    ins = nc.tensor.transpose(bank[:, j * P:(j + 1) * P], src[:, j, :], c.ident[:, :])
                return ins

            def tokens(weights, b):
                def emit(bank):
                    for j in range(NT):
                        dst = bank[:, j * P:(j + 1) * P]
                        nc.tensor.matmul(dst, uT[:, j * P:(j + 1) * P], weights, start=True, stop=False)
                        ins = nc.tensor.matmul(dst, c.ones[0:1, :], b, start=False, stop=True)
                    return ins
                return emit

            pe.wait_ge(src_ready.sem, src_ready.at(i, 1))
            fill(turn)
            pe.wait_ge(w_emptied.sem, w_emptied.at(i, 1))
            fill(tokens(w["wk"], w["bk_b"]))
            fill(tokens(w["wv"], w["bv"]))
            fill(lambda bank: nc.tensor.matmul(bank[:, :], w["wq"], uT[:, :], start=True, stop=True))
            pe.wait_ge(w_emptied.sem, w_emptied.at(i, 3))
            pe.wait_ge(kv_ready.sem, kv_ready.at(i, 0))
            for j in range(NT):
                ins = nc.tensor.matmul(kvbank[:, 0:D + 1], ktok[:, j, :], vtok[:, j, :], start=j == 0, stop=j == NT - 1)
            ins.then_inc(kv_summed.sem, kv_summed.one())
            pe.wait_ge(kv_ready.sem, kv_ready.at(i, 2))
            pe.wait_ge(w_emptied.sem, w_emptied.at(i, 4))
            pe.wait_ge(o_taken.sem, o_taken.at(i, 0))
            for j in range(NT):
                ins = nc.tensor.matmul(obank[j // 2][:, j % 2 * F:(j % 2 + 1) * F], qT[:, j * P:(j + 1) * P], kv[:, :], start=True, stop=True)
            ins.then_inc(context.sem, context.one())

    @block.scalar
    def _(act):
        wait_weights(act, c, w)
        with turns(act, B) as i:
            n = [0]

            def empty(emit):
                act.wait_ge(w_filled.sem, w_filled.at(i, n[0] + 1))
                emit(wbank[n[0] % 2]).then_inc(w_emptied.sem, w_emptied.one())
                n[0] += 1
            empty(lambda bank: nc.scalar.copy(uT[:, :], bank[:, :]))
            empty(lambda bank: nc.scalar.activation(ktok[:, :, :], bank[:, :].rearrange("p (j d) -> p j d", j=NT), ACT.Relu))
            empty(lambda bank: nc.scalar.copy(vtok[:, :, 0:D], bank[:, :].rearrange("p (j d) -> p j d", j=NT)))
            empty(lambda bank: nc.scalar.activation(qT[:, :], bank[:, :], ACT.Relu, bias=w["bq"]))

    @block.gpsimd
    def _(pool):
        with turns(pool, B) as i:
            for _ in range(3):
                norm.on_gpsimd(nc, pool, c, i)

    @block.vector
    def _(dve):
        wait_weights(dve, c, w)
        nc.vector.memset(vtok[:, :, D:D + 1], 1.0).then_inc(ready.sem, ready.one())
        with turns(dve, B) as i:
            def then(ins):
                ins.then_inc(step.sem, step.one())
                dve.wait_ge(step.sem, step.at(i, step.n))

            dve.wait_ge(w_filled.sem, w_filled.at(i, 0))
            norm.on_vector(nc, dve, c, i, lambda j: tile_of(c.x, i, j), lambda j: src[:, j, :], step).then_inc(src_ready.sem, src_ready.one())
            dve.wait_ge(kv_summed.sem, kv_summed.at(i, 1))
            dve.wait_ge(context.sem, context.at(i, 0))
            nc.vector.tensor_tensor(kv[:, 0:D], kvbank[:, 0:D], w["same_head"], ALU.mult).then_inc(kv_ready.sem, kv_ready.one())
            then(nc.vector.tensor_copy(kv_sum[:, :], kvbank[:, D:D + 1]))
            nc.vector.tensor_scalar(kv[:, D:F], w["head_of"], kv_sum[:, 0:1], None, ALU.mult).then_inc(kv_ready.sem, kv_ready.one())
            dve.wait_ge(context.sem, context.at(i, 1))
            for b in range(2):
                o = obank[b][:, 0:2 * F].rearrange("p (j f) -> p j f", j=2)
                ins = nc.vector.tensor_scalar(den[:, 2 * b:2 * b + 2, :], o[:, :, D:F], 1e-6, None, ALU.max)
            then(ins)
            then(nc.vector.reciprocal(den[:, :, :], den[:, :, :]))
            for b in range(2):
                o = obank[b][:, 0:2 * F].rearrange("p (j f) -> p j f", j=2)[:, :, 0:D].rearrange("p j (h e) -> p j h e", h=heads)
                ins = nc.vector.tensor_tensor(acc[:, 2 * b:2 * b + 2, :].rearrange("p j (h e) -> p j h e", h=heads), o,
                                              den[:, 2 * b:2 * b + 2, :].unsqueeze(3).to_broadcast([P, 2, heads, hd]), ALU.mult)
            ins.then_inc(o_taken.sem, o_taken.one())
            dve.wait_ge(o_taken.sem, o_taken.at(i, 1))
            then(nc.vector.tensor_tensor(acc[:, :, :], acc[:, :, :], src[:, :, :], ALU.add))
            then(norm.on_vector(nc, dve, c, i, lambda j: acc[:, j, :], lambda j: tmp[:, j, :], step))
            then(nc.vector.tensor_tensor(tmp[:, :, :], tmp[:, :, :], wide(w["gamma"]), ALU.mult))
            then(nc.vector.tensor_tensor(acc[:, :, :], tmp[:, :, :], wide(w["beta"]), ALU.add))
            then(norm.on_vector(nc, dve, c, i, lambda j: acc[:, j, :], lambda j: tmp[:, j, :], step))
            then(nc.vector.tensor_tensor(tiles_of(c.x, i), tiles_of(c.x, i), tmp[:, :, :], ALU.add))
            assert step.n == step.per, step.n
    ph.close()


def reorder_phase(nc, c, name, by_position):
    ph = Phase(nc, name)
    written, read = ph.flag("written", 0), ph.flag("read", 0)
    block = ph.block()
    natural = c.scratch.rearrange("b (j p) d -> p (b j) d", p=P)

    @block.sync
    def _(sp):
        parts = [(c.x[:, k:k + 2 * NT, :], natural[:, k:k + 2 * NT, :]) for k in range(0, TILES, 2 * NT)]
        grouped = [(c.x[b::B, :, :], c.scratch[b].rearrange("(g t) d -> t g d", t=P // B)) for b in range(B)]
        first, then = (parts, grouped) if by_position else (grouped, parts)
        for tile, dram in first:
            sp.dma_start(dram, tile).then_inc(written.sem, 16)
        sp.wait_ge(written.sem, 16 * len(first))
        for tile, dram in then:
            sp.dma_start(tile, dram).then_inc(read.sem, 16)
        sp.wait_ge(read.sem, 16 * len(then))
    ph.close()



class Pack:

    def __init__(self):
        self.names, self.cols, self.host = {}, 0, []

    def add(self, name, n, lay):
        self.names[name] = (self.cols, n)
        self.cols += n
        self.host.append((n, lay))


def rows_to(a, n=P):
    a = np.asarray(a)
    if a.ndim == 1:
        a = a[None, :]
    out = np.zeros((n, a.shape[1]), a.dtype)
    out[:a.shape[0]] = a
    return out


def blocks(a):
    a = np.asarray(a)
    k = a.shape[0] // P
    return a.reshape(k, P, -1).transpose(1, 0, 2).reshape(P, -1)


def column(v):
    return np.asarray(v).reshape(-1, P).T


def stack_index(heads):
    hd = D // heads
    r = np.arange(NQ * D)
    return r // (NQ * hd) * hd + r % hd


def stack_masks(heads):
    part = np.arange(P) % (NQ * D // heads) // (D // heads)
    qlow, klow = part // 2, part % 2
    out = np.stack([1 - 2 * qlow, qlow, 1 - 2 * klow, klow], 1)
    return out.astype(np.float32)


def attention_pack(heads, scale, wq, wk, wv, bq=None, bk=None, bv=None):
    hd = D // heads
    pk = Pack()
    idx = stack_index(heads)
    pk.add("qk", 2 * NQ * P, lambda a: np.concatenate([wq(a)[:, idx], wk(a)[:, idx]], 1))
    pk.add("v", P, wv)
    pk.add("masks", 4, lambda a: stack_masks(heads))
    pk.add("maskq_scaled", 1, lambda a: stack_masks(heads)[:, 1:2] * np.float32(scale))
    if bq is not None:
        pk.add("bqk", 2 * NQ, lambda a: np.concatenate([column(bq(a)[idx]), column(bk(a)[idx])], 1))
        pk.add("bv", P, lambda a: rows_to(bv(a)))
    return pk


def views(pk, region, need):
    w = {n: region[:, o:o + m] for n, (o, m) in pk.names.items()}
    w["need"] = need
    for n in ("mod", "am", "bd"):
        if n in pk.names:
            w[n] = (lambda o, rows: lambda g: region[0:rows, o + g * P:o + (g + 1) * P])(pk.names[n][0], 16 if n == "am" else P)
    if "cons" in w:
        w["cons"] = w["cons"][0:16, :]
    if "qk" in w:
        o = pk.names["qk"][0]
        w["qk"] = lambda g: region[:, o + g * P:o + (g + 1) * P]
        m = pk.names["masks"][0]
        w["maskq"] = (region[:, m:m + 1], region[:, m + 1:m + 2])
        w["maskk"] = (region[:, m + 2:m + 3], region[:, m + 3:m + 4])
    for n in list(w):
        if n == "bv" or n.endswith("_b"):
            w[n] = w[n][0:1, :]
    return w


def wait_weights(eng, c, w):
    eng.wait_ge(c.loaded[w["need"]], 16)


CONSTS = Pack()
CONSTS.add("ident", P, lambda a: np.eye(P, dtype=np.float32))
CONSTS.add("later_keys", P, lambda a: np.triu(np.full((P, P), MASKED, np.float32), 1))
CONSTS.add("earlier_queries", P, lambda a: np.tril(np.full((P, P), MASKED, np.float32), -1))


def pick_rows():
    out = np.zeros((P, 16, P), np.float32)
    for h in range(16):
        out[h, h] = out[32 + h, h] = 1
    return out.reshape(P, -1)


CONSTS.add("other_groups", P, lambda a: np.where(np.arange(P)[:, None] // B == np.arange(P)[None, :] // B, 0, MASKED).astype(np.float32))
_q, _k = np.arange(P)[:, None], np.arange(P + 64)[None, :]
CONSTS.add("far_keys", P + 64, lambda a: np.where((_k >= _q) & (_k <= _q + 64), 0, MASKED).astype(np.float32))
CONSTS.add("far_queries", P + 64, lambda a: np.where((_k >= _q) & (_k <= _q + 64), 0, MASKED).astype(np.float32))
CONSTS.add("down8", 8, lambda a: np.tile(np.arange(8, 0, -1, dtype=np.float32), (P, 1)))
CONSTS.add("shift", 2 * P, lambda a: np.concatenate([np.eye(P, k=1, dtype=np.float32), np.eye(P, k=1 - P, dtype=np.float32)], 1))
CONSTS.add("pick", 16 * P, lambda a: pick_rows())


def setup_phase(nc, c, consts, x, pk0, w0):
    ph = Phase(nc, "setup")
    raw = ph.sb("raw", [P, CONSTS.cols])
    came, cast = ph.flag("came", 0), ph.flag("cast", 0)
    block = ph.block()

    def part(n):
        o, m = CONSTS.names[n]
        return raw[:, o:o + m]

    @block.sync
    def _(sp):
        sp.dma_start(raw[:, :], consts).then_inc(came.sem, 16)
        for b in range(0, TILES, NT * 2):
            sp.dma_start(c.x[:, b:b + NT * 2, :], x[:, b:b + NT * 2, :]).then_inc(came.sem, 16)
        load_weights(sp, c, pk0, w0)
        sp.wait_ge(came.sem, 80)

    @block.vector
    def _(dve):
        nc.vector.memset(c.ones[:, :], 1.0)
        nc.vector.memset(c.minus_half[:, :], -0.5)
        nc.vector.memset(c.eps[:, :], EPS)
        dve.wait_ge(came.sem, 80)
        nc.vector.tensor_copy(c.ident[:, :], part("ident"))
        nc.vector.tensor_copy(c.ident_bf[:, :], part("ident"))
        nc.vector.tensor_copy(c.later_keys[:, :], part("later_keys"))
        nc.vector.tensor_copy(c.earlier_queries[:, :], part("earlier_queries"))
        nc.vector.tensor_copy(c.other_groups[:, :], part("other_groups"))
        nc.vector.memset(c.minus_half16[:, :], -0.5)
        nc.vector.tensor_copy(c.far_keys[:, :], part("far_keys"))
        nc.vector.tensor_copy(c.far_queries[:, :], part("far_queries"))
        nc.vector.tensor_copy(c.down8[:, :], part("down8"))
        nc.vector.tensor_copy(c.shift[:, :, :], part("shift").rearrange("p (a n) -> p a n", a=2))
        nc.vector.tensor_copy(c.pick[:, :, :], part("pick").rearrange("p (h n) -> p h n", h=16)).then_inc(cast.sem, 1)
        dve.wait_ge(cast.sem, 1)
    ph.close()


def load_weights(sp, c, pk, src):
    n_load = c.region_turn
    n = n_load % 2
    c.region_turn += 1
    sp.dma_start(c.region[n][:, 0:pk.cols], src).then_inc(c.loaded[n_load], 16)


def load_next(sp, c):
    if c.next is not None:
        load_weights(sp, c, *c.next)


def store_phase(nc, c, out):
    ph = Phase(nc, "store")
    stored = ph.flag("stored", 0)
    block = ph.block()

    @block.sync
    def _(sp):
        for b in range(0, TILES, NT * 2):
            sp.dma_start(out[:, b:b + NT * 2, :], c.x[:, b:b + NT * 2, :]).then_inc(stored.sem, 16)
        sp.wait_ge(stored.sem, 64)
    ph.close()


def rotary_tables():
    hd, window = 64, 64
    half = np.arange(0, hd, 2, dtype=np.float32)
    t = np.arange(T, dtype=np.float32)
    freqs = t[:, None] * (np.float32(1) / np.float32(10000) ** (half / np.float32(hd)))[None]
    base = (half + np.float32(0.4 * hd)) / np.float32(1.4 * hd)
    power = (t - T // 2) / np.float32(window // 2)
    scale = base[None, :] ** power[:, None]
    out = []
    for f, sign in ((np.cos(freqs), 1.0), (np.sin(freqs), -1.0)):
        q = np.concatenate([sign * f * scale, f * scale], 1) * 8.0
        k = np.concatenate([sign * f / scale, f / scale], 1)
        tab = np.stack([q, k], 1).astype(np.float32)
        out.append(tab.reshape(NT, P, 2, hd).transpose(1, 0, 2, 3).reshape(P, -1))
    return out


def phase_list():
    T_ = lambda n: (lambda a: np.asarray(a[n]).T)
    V_ = lambda n: (lambda a: np.asarray(a[n]))
    out = []
    f32 = lambda v: float(np.float32(v))
    W4 = lambda k: (lambda a: np.asarray(a["L0_attn_W_qkvf"])[k * D:(k + 1) * D].T)

    def conv_blocks(a):
        conv = np.asarray(a["L0_attn_W_conv"])
        o = np.zeros((16, 8, 4, 16, 8), np.float32)
        for h in range(16):
            o[h, :, :, h, :] = conv.transpose(0, 2, 1)
        return o.reshape(D, 4 * D)
    sc0 = f32(8 ** -0.5)
    pk = attention_pack(16, sc0, W4(0), W4(1), W4(2))
    pk.add("q", P, W4(0))
    pk.add("wf", P, lambda a: np.asarray(a["L0_attn_W_qkvf"])[3 * D:])
    pk.add("wkT", P, W4(1))
    pk.add("wvT", P, W4(2))
    pk.add("bd", 4 * P, conv_blocks)
    pk.add("gain", 1, lambda a: column(a["L0_attn_ln1_g"]))
    pk.add("shift", 1, lambda a: column(a["L0_attn_ln1_b"]))
    pk.add("proj", P, T_("L0_attn_W_proj"))
    out.append(("L0a", pk, lambda nc, c, w: attention_phase(nc, c, "l0a", w, 16, sc0, causal=True, affine=True, future=True, out_steps=("proj",), finish="y")))
    pk = Pack()
    pk.add("ff1", 4 * P, V_("L0_attn_W_ff1"))
    pk.add("ff2", 4 * P, lambda a: blocks(a["L0_attn_W_ff2"]))
    pk.add("gain", 1, lambda a: column(a["L0_attn_ln2_g"]))
    pk.add("shift", 1, lambda a: column(a["L0_attn_ln2_b"]))

    def l0g(nc, c, w):
        blk = lambda t, k: t[:, k * P:(k + 1) * P]
        L = [Layer(1, 4, lambda k, m: blk(w["ff1"], m), ACT.Gelu)]
        mlp_phase(nc, c, "l0g", w, lambda e: L, lambda e: (4, lambda k: blk(w["ff2"], k)), source="y", affine=True, add_y=True)
    out.append(("L0g", pk, l0g))
    for d in range(2):
        G = lambda n, d=d: (lambda a: np.asarray(a["L0_ffn_" + n])[d])
        pk = Pack()
        pk.add("qkv", 1536, G("wqkv"))
        pk.add("wo", 4 * P, (lambda g: lambda a: blocks(g(a)))(G("wo")))
        pk.add("cosines", 4 * P, lambda a: rotary_tables()[0])
        pk.add("sines", 4 * P, lambda a: rotary_tables()[1])
        pk.add("gains", P, (lambda d: lambda a: np.broadcast_to(np.concatenate([a["L0_ffn_q_scale"][d], a["L0_ffn_k_scale"][d]]), (P, P)))(d))
        pk.add("gains_turned", P, (lambda d: lambda a: np.broadcast_to(np.concatenate([np.roll(a["L0_ffn_q_scale"][d], 32), np.roll(a["L0_ffn_k_scale"][d], 32)]), (P, P)))(d))
        out.append((f"L0w{d}", pk, (lambda d: lambda nc, c, w: local_attention_phase(nc, c, f"l0w{d}", w, first=d == 0))(d)))
        pk = Pack()
        HID, HB = 341, 3

        def padded(v, n=HB * P):
            return np.concatenate([v, np.zeros(v.shape[:-1] + (n - v.shape[-1],), v.dtype)], -1)
        pk.add("wa", HB * P, (lambda g: lambda a: padded(g(a)[:, :HID]))(G("w1")))
        pk.add("wg", HB * P, (lambda g: lambda a: padded(g(a)[:, HID:]))(G("w1")))
        pk.add("ba", HB, (lambda g: lambda a: column(padded(g(a)[:HID])))(G("b1")))
        pk.add("bg", HB, (lambda g: lambda a: column(padded(g(a)[HID:])))(G("b1")))
        pk.add("w2", HB * P, (lambda g: lambda a: blocks(padded(g(a).T).T))(G("w2")))
        pk.add("final_b", P, (lambda g: lambda a: rows_to(g(a)))(G("b2")))
        pk.add("gain", 1, (lambda g: lambda a: column(g(a)))(G("ln_g")))
        pk.add("shift", 1, (lambda g: lambda a: column(g(a)))(G("ln_b")))

        def l0h(nc, c, w, d=d):
            blk = lambda t, k: t[:, k * P:(k + 1) * P]
            L = [Layer(1, 3, lambda k, m: blk(w["wg"], m), ACT.Gelu, bias=lambda m: w["bg"][:, m:m + 1],
                       V=lambda k, m: blk(w["wa"], m), v_op=ALU.add, v_arg=lambda m: w["ba"][:, m:m + 1])]
            mlp_phase(nc, c, f"l0h{d}", w, lambda e: L, lambda e: (3, lambda k: blk(w["w2"], k)), source="y", affine=True,
                      shifted=True, add_y=True, finish="residual_norm" if d else "y")
        out.append((f"L0h{d}", pk, l0h))
    fl = lambda n: (lambda a: np.asarray(a[n]).reshape(D, D).T)
    fb = lambda n: (lambda a: np.asarray(a[n]).reshape(D))
    sc = float(np.float32(1 / np.sqrt(8.0)))
    pk = attention_pack(16, sc, fl("L1_attn_Wq"), fl("L1_attn_Wk"), fl("L1_attn_Wv"), fb("L1_attn_bq"), fb("L1_attn_bk"), fb("L1_attn_bv"))
    out.append(("L1a", pk, lambda nc, c, w: attention_phase(nc, c, "l1a", w, 16, sc, causal=True, bias=True)))
    pk = Pack()
    for n in ("w1", "w2"):
        pk.add(n, 4 * P, T_(f"L1_ffn_{n}_w"))
        pk.add(n + "s", 4, (lambda n: lambda a: column(a[f"L1_ffn_{n}_s"]))(n))
    for n in ("h1", "h2"):
        pk.add(n, 16 * P, (lambda n: lambda a: blocks(np.asarray(a[f"L1_ffn_{n}_w"]).T))(n))
        pk.add(n + "s", 4, (lambda n: lambda a: column(a[f"L1_ffn_{n}_s"]))(n))
    pk.add("w3", 4 * P, lambda a: blocks(np.asarray(a["L1_ffn_w3_w"]).T))
    pk.add("out_scale", P, lambda a: np.broadcast_to(np.asarray(a["L1_ffn_w3_s"]), (P, P)))

    def l1f(nc, c, w):
        m1 = lambda t: (lambda k, m: t[:, (k * 4 + m) * P:(k * 4 + m + 1) * P])
        s1 = lambda t: (lambda m: t[:, m:m + 1])
        L = [Layer(1, 4, m1(w["w1"]), ACT.Silu, scale=s1(w["w1s"]), V=m1(w["w2"]), v_arg=s1(w["w2s"])),
             Layer(4, 4, m1(w["h1"]), ACT.Gelu, scale=s1(w["h1s"])),
             Layer(4, 4, m1(w["h2"]), ACT.Gelu, scale=s1(w["h2s"]))]
        mlp_phase(nc, c, "l1f", w, lambda e: L, lambda e: (4, lambda k: w["w3"][:, k * P:(k + 1) * P]), out_scale=True)
    out.append(("L1f", pk, l1f))
    h16 = stack_index(16) // 8
    col = lambda n, k: (lambda a: np.asarray(a[n])[:, k * D:(k + 1) * D])
    row = lambda n, k: (lambda a: np.asarray(a[n])[k * D:(k + 1) * D])
    pk = attention_pack(16, sc, V_("L2_attn_Wq"), V_("L2_attn_Wk"), V_("L2_attn_Wv"), V_("L2_attn_bq"), V_("L2_attn_bk"), V_("L2_attn_bv"))
    pk.add("mod", 4 * P, lambda a: np.asarray(a["L2_attn_cg_W"])[:, h16])
    pk.add("am", 4 * P, lambda a: rows_to(np.asarray(a["L2_attn_am_W"])[:, h16]))
    pk.add("cons", 1, lambda a: rows_to(np.asarray(a["L2_attn_cons_vec"])[:, None]))
    pk.add("cg_am_bias", 8, lambda a: np.concatenate([column(np.asarray(a["L2_attn_cg_b"])[h16]), column(np.asarray(a["L2_attn_am_b"])[h16])], 1))
    out.append(("L2m", pk, lambda nc, c, w: attention_phase(nc, c, "l2m", w, 16, sc, bias=True, modulated=True, finish="context")))
    s32 = f32(1 / np.sqrt(32.0))
    pk = attention_pack(4, s32, col("L2_attn_ca_Win", 0), col("L2_attn_ca_Win", 1), col("L2_attn_ca_Win", 2), row("L2_attn_ca_bin", 0), row("L2_attn_ca_bin", 1), row("L2_attn_ca_bin", 2))
    pk.add("causal_out", P, V_("L2_attn_ca_Wout"))
    pk.add("causal_out_b", P, lambda a: rows_to(a["L2_attn_ca_bout"]))
    out.append(("L2c", pk, lambda nc, c, w: attention_phase(nc, c, "l2c", w | {"mix": (1.0 - 0.7, 0.7)}, 4, s32, bias=True, out_steps=("causal_out",), finish="y")))
    meta = (0.9 - 0.8) / 0.2 * 0.3
    pk = attention_pack(4, s32, col("L2_attn_mc_Win", 0), col("L2_attn_mc_Win", 1), col("L2_attn_mc_Win", 2), row("L2_attn_mc_bin", 0), row("L2_attn_mc_bin", 1), row("L2_attn_mc_bin", 2))
    pk.add("meta_out", P, V_("L2_attn_mc_Wout"))
    pk.add("meta_out_b", P, lambda a: rows_to(a["L2_attn_mc_bout"]))
    pk.add("out", P, V_("L2_attn_Wo"))
    pk.add("out_b", P, lambda a: rows_to(a["L2_attn_bo"]))
    out.append(("L2t", pk, lambda nc, c, w: attention_phase(nc, c, "l2t", w | {"mix": (1.0 - meta, meta)}, 4, s32, bias=True, source="given", out_steps=("meta_out", "out"))))
    pk = Pack()
    out.append(("R1", None, lambda nc, c, w: reorder_phase(nc, c, "to_positions", True)))
    wq = lambda k: (lambda a: np.asarray(a["L2_ffn_Wqkv"])[k * D:(k + 1) * D].T)
    bq = lambda k: (lambda a: np.asarray(a["L2_ffn_bqkv"])[k * D:(k + 1) * D])
    pk = attention_pack(4, s32, wq(0), wq(1), wq(2), bq(0), bq(1), bq(2))
    pk.add("mixed", P, T_("L2_ffn_Wo"))
    pk.add("mixed_b", P, lambda a: rows_to(a["L2_ffn_bo"]))
    bcast = lambda n: (lambda a: np.broadcast_to(np.asarray(a[n]), (P, P)))
    pk.add("g1", P, bcast("L2_ffn_g1"))
    pk.add("be1", P, bcast("L2_ffn_be1"))
    out.append(("L2p", pk, lambda nc, c, w: attention_phase(nc, c, "l2p", w, 4, s32, bias=True, grouped=True, out_steps=("mixed",), finish="y")))
    pk = Pack()
    pk.add("W1", 32 * P, lambda a: np.asarray(a["L2_ffn_W1"]).transpose(1, 0, 2).reshape(P, -1))
    pk.add("W2", 32 * P, lambda a: np.asarray(a["L2_ffn_W2"]).reshape(32, P, D).transpose(1, 0, 2).reshape(P, -1))
    pk.add("b1", 32, lambda a: np.asarray(a["L2_ffn_b1"]).reshape(32, P).T)
    pk.add("gate", 8, T_("L2_ffn_Wg"))
    pk.add("expert_bias", P, lambda a: rows_to(a["L2_ffn_b2"]))
    pk.add("g2", P, bcast("L2_ffn_g2"))
    pk.add("be2", P, bcast("L2_ffn_be2"))

    def l2e(nc, c, w):
        w = w | {"expert_bias": w["expert_bias"][0:8, :]}
        blk = lambda t, k: t[:, k * P:(k + 1) * P]
        L = lambda e: [Layer(1, 4, lambda k, m: blk(w["W1"], 4 * e + m), ACT.Relu, bias=lambda m: w["b1"][:, 4 * e + m:4 * e + m + 1])]
        mlp_phase(nc, c, "l2e", w, L, lambda e: (4, lambda k: blk(w["W2"], 4 * e + k)), experts=8, source="y", gate="top1", tail_gain=True)
    out.append(("L2e", pk, l2e))
    out.append(("R2", None, lambda nc, c, w: reorder_phase(nc, c, "to_batches", False)))
    pk = Pack()
    pk.add("wq", P, T_("L3_attn_Wq"))
    pk.add("wk", P, T_("L3_attn_Wk"))
    pk.add("wv", P, T_("L3_attn_Wv"))
    pk.add("bq", 1, lambda a: column(a["L3_attn_bq"]))
    pk.add("bk_b", P, lambda a: rows_to(a["L3_attn_bk"]))
    pk.add("bv", P, lambda a: rows_to(a["L3_attn_bv"]))
    pk.add("gamma", P, bcast("L3_attn_gamma"))
    pk.add("beta", P, bcast("L3_attn_beta"))
    pk.add("same_head", P, lambda a: np.kron(np.eye(16), np.ones((8, 8))).astype(np.float32))
    pk.add("head_of", 16, lambda a: np.kron(np.eye(16), np.ones((8, 1))).astype(np.float32))
    out.append(("L3a", pk, lambda nc, c, w: linear_attention_phase(nc, c, "l3a", w)))
    pk = Pack()
    pk.add("Wg", P // 16, V_("L3_ffn_Wg"))
    for n in ("W11", "W12"):
        pk.add(n, 16 * P, (lambda n: lambda a: np.asarray(a[f"L3_ffn_{n}"]).transpose(1, 0, 2).reshape(P, -1))(n))
    pk.add("W2", 16 * P, lambda a: np.asarray(a["L3_ffn_W2"]).reshape(16, P, D).transpose(1, 0, 2).reshape(P, -1))

    def l3e(nc, c, w):
        w = w | {"gate": w["Wg"]}
        blk = lambda t, k: t[:, k * P:(k + 1) * P]
        L = lambda e: [Layer(1, 2, lambda k, m: blk(w["W11"], 2 * e + m), ACT.Silu, V=lambda k, m: blk(w["W12"], 2 * e + m))]
        mlp_phase(nc, c, "l3e", w, L, lambda e: (2, lambda k: blk(w["W2"], 2 * e + k)), experts=8, gate="top2")
    out.append(("L3e", pk, l3e))
    return out


def program(nc, consts, x, packs, out, phases):
    c = Chip()
    with ExitStack() as ctx:
        sb = lambda n, s, d=F32: ctx.enter_context(nc.sbuf_tensor(n, s, d))
        c.x = sb("x", [P, TILES, D])
        c.y = sb("y", [P, TILES, D])
        c.ctx = sb("ctx", [P, TILES, D])
        c.ident = sb("ident", [P, P])
        c.ident_bf = sb("ident_bf", [P, P], BF16)
        c.later_keys = sb("later_keys", [P, P], BF16)
        c.earlier_queries = sb("earlier_queries", [P, P], BF16)
        c.other_groups = sb("other_groups", [P, P], BF16)
        c.far_keys = sb("far_keys", [P, P + 64], BF16)
        c.far_queries = sb("far_queries", [P, P + 64], BF16)
        c.minus_half16 = sb("minus_half16", [P, 16])
        c.down8 = sb("down8", [P, 8])
        c.shift = sb("shift", [P, 2, P])
        c.pick = sb("pick", [P, 16, P], F32R)
        c.ones = sb("ones", [1, P])
        c.minus_half = sb("minus_half", [P, NT])
        c.eps = sb("eps", [P, NT])
        c.bank = [ctx.enter_context(nc.psum_tensor(f"bank{k}", [P, 512], F32)) for k in range(8)]
        c.scratch = nc.dram_tensor("scratch", (B, T, D), F32, kind="Internal").ap()
        loads = [(pk, packs[name]) for name, pk, _ in phases if pk is not None]
        cols = [max([pk.cols for pk, _ in loads[k::2]] + [1]) for k in range(2)]
        tiles = lambda a: a.rearrange("b (j p) d -> p (b j) d", p=P)
        c.loaded = [ctx.enter_context(nc.semaphore(f"weights_loaded{k}")) for k in range(len(loads))]
        c.region_turn = 0
        with nc.sbuf_tensor("weights0", [P, cols[0]], F32) as r0, nc.sbuf_tensor("weights1", [P, cols[1]], F32) as r1:
            c.region = [r0, r1]
            setup_phase(nc, c, consts, tiles(x), *loads[0])
            n = 0
            for name, pk, build in phases:
                if pk is None:
                    build(nc, c, None)
                    continue
                c.next = loads[n + 1] if n + 1 < len(loads) else None
                build(nc, c, views(pk, c.region[n % 2], n))
                n += 1
        store_phase(nc, c, tiles(out))


def lay_out(pk, inputs):
    cols = []
    for n, lay in pk.host:
        a = np.asarray(lay(inputs))
        assert a.shape == (P, n), (a.shape, n)
        cols.append(a)
    return np.ascontiguousarray(np.concatenate(cols, 1))


def kernel(**inputs):
    from concourse import bacc
    from concourse.bass_utils import run_bass_kernel_spmd

    nc = bacc.Bacc("TRN2", target_bir_lowering=False, num_devices=1)
    nc.disable_value_cache = True
    phases = phase_list()
    arrays = {"x_in": np.ascontiguousarray(inputs["L0_attn_x"]), "consts": lay_out(CONSTS, inputs)}
    for name, pk, _ in phases:
        if pk is not None:
            arrays[f"w_{name}"] = lay_out(pk, inputs)
    aps = {n: nc.dram_tensor(n, a.shape, F32, kind="ExternalInput").ap() for n, a in arrays.items()}
    out = nc.dram_tensor("x_out", (B, T, D), F32, kind="ExternalOutput").ap()
    program(nc, aps["consts"], aps["x_in"], {p[0]: aps[f"w_{p[0]}"] for p in phases if p[1] is not None}, out, phases)
    return run_bass_kernel_spmd(nc, [arrays], core_ids=[0]).results[0]["x_out"]
```

```python
from contextlib import ExitStack, contextmanager

import numpy as np

import concourse.bass as bass
from concourse import mybir

F32 = mybir.dt.float32
F32R = mybir.dt.float32r
BF16 = mybir.dt.bfloat16
ALU = mybir.AluOpType
ACT = mybir.ActivationFunctionType
AX = mybir.AxisListType

P = 128
B, T, D = 8, 512, 128
NT = T // P
TILES = B * NT
EPS = 1e-5
MASKED = -1e30
H2 = D // 2
NQ = 4


class Signal:

    def __init__(self, sem, per, before=None):
        self.sem, self.per, self.n, self.before = sem, per, 0, before

    def at(self, turn, n=0):
        if self.before is None:
            return turn.times(self.per) + (n + 1)
        return turn.times(self.per) + (self.before + n + 1) if not turn.ahead else n + 1

    def one(self):
        self.n += 1
        return 1

    def turn_done(self):
        assert self.n == self.per, (self.sem, self.n, self.per)

    def ahead_done(self):
        assert self.before in (None, self.n), (self.sem, self.n, self.before)
        self.n = 0


class Turn:

    def __init__(self, eng, i):
        self.eng, self.i, self.products = eng, i, {1: i}

    def times(self, per):
        if per not in self.products:
            self.products[per] = self.eng.snap(self.i * per)
        return self.products[per]

    def tiles(self, t):
        return t[:, bass.ds(self.times(NT), NT), :]

    def tile(self, t, j):
        return t[:, bass.ds(self.times(NT) + j, 1), :]

    ahead = False

    def next_tiles(self, t):
        return t[:, bass.ds(self.times(NT) + NT, NT), :]

    def next_tile(self, t, j):
        return t[:, bass.ds(self.times(NT) + NT + j, 1), :]


class Ahead:
    ahead = True

    def times(self, per):
        return -per

    def next_tiles(self, t):
        return t[:, 0:NT, :]

    def next_tile(self, t, j):
        return t[:, j:j + 1, :]


@contextmanager
def turns(eng, n):
    with eng.Fori(0, n) as i:
        yield Turn(eng, i)


class Phase:

    def __init__(self, nc, name):
        self.nc, self.name, self.made, self.signals, self.ctx = nc, name, [], [], ExitStack()

    def flag(self, what, per=1, before=None):
        sem = self.nc.alloc_semaphore(f"{self.name}_{what}")
        self.made.append(sem)
        self.signals.append(Signal(sem, per, before))
        return self.signals[-1]

    def sb(self, what, shape, dt=F32):
        return self.ctx.enter_context(self.nc.sbuf_tensor(f"{self.name}_{what}", shape, dt))

    def block(self):
        for s in self.signals:
            if s.per:
                self.nc.sync.sem_inc(s.sem, 1)
        self.nc.all_engine_barrier()
        return self.ctx.enter_context(self.nc.Block())

    def close(self):
        self.ctx.close()
        self.nc.clear_and_free_semaphores(self.made)
        self.nc.all_engine_barrier()


class Chip:
    pass


def tiles_of(t, i):
    return i.tiles(t)


def tile_of(t, i, j):
    return i.tile(t, j)



class Norm:
    def __init__(self, ph, per, before=None):
        self.variance, self.eps_added, self.rstd_ready = (ph.flag(s, per, before) for s in ("variance", "eps_added", "rstd_ready"))
        self.bn = ph.sb("bn", [P, NT, 6])
        self.mv = ph.sb("mv", [P, NT, 2])
        self.veps = ph.sb("veps", [P, NT])
        self.rstd = ph.sb("rstd", [P, NT])

    def on_gpsimd(self, nc, pool, c, i):
        pool.wait_ge(self.variance.sem, self.variance.at(i, self.rstd_ready.n + 1))
        nc.gpsimd.tensor_tensor(self.veps[:, :], self.mv[:, :, 1], c.eps[:, :], ALU.add).then_inc(self.eps_added.sem, self.eps_added.one())
        n = self.eps_added.n
        pool.wait_ge(self.eps_added.sem, self.eps_added.at(i, n))
        nc.gpsimd.tensor_tensor(self.rstd[:, :], self.veps[:, :], c.minus_half[:, :], ALU.pow).then_inc(self.rstd_ready.sem, self.rstd_ready.one())

    def on_vector(self, nc, dve, c, i, src, dst, step):
        self.statistics(nc, dve, src)
        return self.scaled(nc, dve, i, src, dst)

    def statistics(self, nc, dve, src):
        for j in range(NT):
            ins = nc.vector.bn_stats(self.bn[:, j, :], src(j))
        dve.drain()
        for j in range(NT):
            ins = nc.vector.bn_aggr(self.mv[:, j, :], self.bn[:, j, :])
        ins.then_inc(self.variance.sem, self.variance.one())

    def scaled(self, nc, dve, i, src, dst):
        n = self.variance.n
        dve.wait_ge(self.rstd_ready.sem, self.rstd_ready.at(i, n))
        for j in range(NT):
            ins = nc.vector.tensor_scalar(dst(j), src(j), self.mv[:, j, 0:1], self.rstd[:, j:j + 1], ALU.subtract, ALU.mult)
        return ins


def wide(row):
    return row.unsqueeze(1).to_broadcast([P, NT, row.shape[-1]])


def turn_done(*signals):
    for s in signals:
        s.turn_done()



def attention_phase(nc, c, name, w, heads, scale, causal=False, bias=False, source=None, affine=False, grouped=False,
                    future=False, modulated=False, out_steps=(), finish="residual_norm"):
    ph = Phase(nc, name)
    hd = D // heads
    rows = NQ * hd
    in_group = P // rows
    G = heads // in_group
    E = hd + 1
    half = heads // 2
    R = half * E
    units = heads * NT
    MG = 4
    mg = heads // MG
    norms_ahead = {None: 1, "given": 0}[source] + affine
    norms = norms_ahead + (finish == "residual_norm") + ("mixed" in out_steps)

    places = {}

    def place(step, k, *what):
        places.setdefault((step, k), []).extend(what)

    for g in range(1, MG):
        place(g * mg - 1, 0, f"max{g}")
    uT_at = (1, 0) if mg > 1 else (0, 2)
    place(*uT_at, "uT")
    if modulated:
        place(2, 0, *(f"mod{g}" for g in range(G)))
    stack_at = [in_group * (g + 1) - (in_group > 1) for g in range(G)]
    for g in range(G):
        place(stack_at[g], 0, f"q{g}")
        place(stack_at[g], 2 if stack_at[g] < heads else 0, f"k{g}")
    place(half, 3, "sums0")
    if future:
        place(13, 0, "fq", "fk0", "fv0")
        place(14, 0, "fk1", "fv1")
        place(14, 2, "fk2", "fv2")
        place(15, 2, "fk3", "fv3")
    place(heads, 0, "v", "sums1", "max_next")
    for s in range(len(out_steps)):
        place(heads, 0, f"turned{s}", f"projected{s}")
    W_TURN = [what for at in sorted(places) for what in places[at]]
    W_AHEAD = ["uT"] + [f"mod{g}" for g in range(G)] * modulated + [f"{a}{g}" for g in range(G) for a in "qk"] + ["v"]
    W_AHEAD += (["fq"] + [f"f{a}{f}" for f in range(4) for a in "kv"]) * future + ["max_next"]

    def w_n(i, what):
        return (W_AHEAD if i.ahead else W_TURN).index(what) + 1

    src = ph.sb("src", [P, NT, D])
    uT = ph.sb("uT", [P, T])
    high = ph.sb("high", [P, 2, T], F32R)
    lowpart = ph.sb("lowpart", [P, 2, T])
    qs = ph.sb("qs", [P, G, T], F32R)
    ks = ph.sb("ks", [P, G, T], F32R)
    vx = ph.sb("vx", [P, NT, heads, R + E])
    vx_flat = vx[:, :, :, :].rearrange("p j h m -> p j (h m)")
    sums = ph.sb("sums", [R, 2, T])
    sums_tok = ph.sb("sums_tok", [P, 2, NT, half, E])
    negmax = ph.sb("negmax", [P, NT, heads])
    mrow = ph.sb("mrow", [mg, T])
    mT = ph.sb("mT", [48, 2, T], F32R)
    pT = ph.sb("pT", [P, 2, NT, T])
    rden = ph.sb("rden", [P, 2, NT, half])
    ctxt = ph.sb("ctx", [P, NT, D])
    tmp = ph.sb("tmp", [P, NT, D])
    stepT = uT
    stepo = ph.sb("stepo", [P, NT, D]) if out_steps else None
    if modulated:
        modT = ph.sb("modT", [P, G, T])
        mod_bias = ph.sb("mod_bias", [P, G])
        scaled = lowpart[:, 0, :]
    sb_scaled = ph.sb("biases", [P, 4 * G]) if bias else None
    if future:
        qtok = stepo
        kf = c.ctx[:, 0:4 * NT, :].rearrange("p (f j) d -> p f j d", f=4)
        vf = c.ctx[:, 4 * NT:8 * NT, :].rearrange("p (f j) d -> p f j d", f=4)
        afT = kf[:, 0, :, :]
        wkf, wvf = (ph.sb(n, [P, 4, P]) for n in ("wkf", "wvf"))
        fut = ph.sb("fut", [P, 4, NT, heads])
        futmax = ph.sb("futmax", [P, NT, heads])
        pf = ph.sb("pf", [P, 4, NT, heads])
        futden = ph.sb("futden", [P, NT, heads])

    w0, w1 = c.bank[0], c.bank[1]
    wbank = (w0, w1)
    abank = (c.bank[2], c.bank[3])
    bbank = (c.bank[4], c.bank[5])
    obank = (c.bank[6], c.bank[7])

    def S(what, per=1, before=None):
        return ph.flag(what, per, before)
    prepared, mod_added = S("prepared", 0), S("mod_added", 0)
    src_ready = S("src_ready")
    w_filled, w_emptied = S("w_filled", len(W_TURN), len(W_AHEAD)), S("w_emptied", len(W_TURN), len(W_AHEAD))
    parts_ready, stacked = S("parts_ready", G), S("stacked", 2 * G)
    scored_a, maxed = S("scored_a", units), S("maxed", units)
    m_copied = S("m_copied", 2 * MG)
    m_final = S("m_final", MG)
    scored_b, exped = S("scored_b", units), S("exped", units)
    head_done = S("head_done", heads)
    sums_copied = S("sums_copied", 2)
    ctx_ready = S("ctx_ready")
    step_taken = S("step_taken", max(len(out_steps), 1))
    mod_scaled = S("mod_scaled", G)
    norm = Norm(ph, max(norms, 1), norms_ahead)
    then_ahead = affine + 8 * future
    step = S("dve_step", affine + 14 * future + sum({"causal_out": 1, "meta_out": 1, "mixed": 3}.get(s, 0) for s in out_steps)
             + (finish == "residual_norm") * (1 + (not out_steps)) + (finish == "context") + 1 - future, then_ahead)
    fut_asked, fut_exped, fut_used = S("fut_asked"), S("fut_exped"), S("fut_used")

    def keys_of(q):
        return (q * P if grouped else 0), ((q + 1) * P if causal or grouped else T)

    def queries_of(k):
        return (k * P if causal or grouped else 0), ((k + 1) * P if grouped else T)

    masked = causal or grouped
    mask_a, mask_b = (c.other_groups, c.other_groups) if grouped else (c.later_keys, c.earlier_queries)
    block = ph.block()

    @block.sync
    def _(sp):
        load_next(sp, c)

    @block.tensor
    def _(pe):
        wait_weights(pe, c, w)
        if future:
            for f in range(4):
                ins = nc.tensor.matmul(w0[:, f * P:(f + 1) * P], w["bd"](f), w["wf"], start=True, stop=True)
            ins.then_inc(prepared.sem, prepared.one())
            pe.wait_ge(prepared.sem, 2)
            for which, bank in (("wkT", w1), ("wvT", w0)):
                for f in range(4):
                    ins = nc.tensor.matmul(bank[:, f * P:(f + 1) * P], afT[:, f, :], w[which], start=True, stop=True)
            ins.then_inc(prepared.sem, prepared.one())
            pe.wait_ge(prepared.sem, 5)
        if modulated:
            for g in range(G):
                ins = nc.tensor.matmul(w0[:, g:g + 1], w["am"](g), w["cons"], start=True, stop=True)
            ins.then_inc(prepared.sem, prepared.one())

        def fill(i, what, emit):
            n = w_filled.n
            assert w_n(i, what) == n + 1, what
            if n > 0 or not i.ahead:
                pe.wait_ge(w_emptied.sem, w_emptied.at(i, n - 1))
            bank = wbank[(n + (0 if i.ahead else len(W_AHEAD))) % 2]
            emit(bank).then_inc(w_filled.sem, w_filled.one())

        def turn(s):
            def emit(bank):
                for j in range(NT):
                    ins = nc.tensor.transpose(bank[:, j * P:(j + 1) * P], s[:, j, :], c.ident[:, :])
                return ins
            return emit

        def tokens(sT, weights, b=None):
            def emit(bank):
                for j in range(NT):
                    ins = nc.tensor.matmul(bank[:, j * P:(j + 1) * P], sT[:, j * P:(j + 1) * P], weights, start=True, stop=b is None)
                    if b is not None:
                        ins = nc.tensor.matmul(bank[:, j * P:(j + 1) * P], c.ones[0:1, :], b, start=False, stop=True)
                return ins
            return emit

        def features(weights):
            return lambda bank: nc.tensor.matmul(bank[:, :], weights, uT[:, :], start=True, stop=True)

        def prepare(i, what):
            kind, g = what[0], int(what[-1]) if what[-1].isdigit() else 0
            if what == "uT":
                pe.wait_ge(src_ready.sem, src_ready.at(i, 2))
                fill(i, what, turn(src))
                return
            pe.wait_ge(w_emptied.sem, w_emptied.at(i, w_n(i, "uT")))
            if kind == "m":
                fill(i, what, features(w["mod"](g)))
            elif kind in "qk":
                fill(i, what, features(w["qk"](g if kind == "q" else G + g)))
            elif what == "v":
                fill(i, what, tokens(uT, w["v"], w.get("bv")))
            elif what == "fq":
                fill(i, what, tokens(uT, w["q"]))
            else:
                fill(i, what, tokens(uT, (wkf if what[1] == "k" else wvf)[:, g, :]))

        def score_a(i, h, q):
            n = h * NT + q
            h, own = h % heads, 2 * G * (h // heads)
            g, at = h // in_group, (h % in_group) * rows
            if q == 0:
                pe.wait_ge(stacked.sem, stacked.at(i, own + 2 * (g + 1)))
            if not (i.ahead and n < units + 2):
                pe.wait_ge(maxed.sem, maxed.at(i, n - 1))
            lo, hi = keys_of(q)
            bank = abank[n % 2]
            ins = nc.tensor.matmul(bank[:, lo:hi], qs[at:at + rows, g, q * P:(q + 1) * P], ks[at:at + rows, g, lo:hi], start=True, stop=not masked)
            if masked:
                ins = nc.tensor.matmul(bank[:, q * P:hi], c.ident_bf[:, :], mask_a[:, :], start=False, stop=True)
            ins.then_inc(scored_a.sem, scored_a.one())

        def maxima(i, group, what):
            if future:
                pe.wait_ge(m_final.sem, m_final.at(i, group + 1))
            else:
                pe.wait_ge(maxed.sem, maxed.at(i, (group + 1) * mg * NT))

            def emit(bank):
                for q in range(NT):
                    first = group % MG * mg
                    ins = nc.tensor.transpose(bank[0:mg, q * P:(q + 1) * P], negmax[:, q, first:first + mg], c.ident[:, :])
                return ins
            fill(i, what, emit)

        def score_b(i, h, k):
            g, at = h // in_group, (h % in_group) * rows
            n = h * NT + k
            if k == 0 and h % mg == 0:
                pe.wait_ge(m_copied.sem, m_copied.at(i, 2 * (h // mg + 1)))
            pe.wait_ge(exped.sem, exped.at(i, max(n - 1, 0)))
            lo, hi = queries_of(k)
            bank = bbank[n % 2]
            nc.tensor.matmul(bank[:, lo:hi], ks[at:at + rows, g, k * P:(k + 1) * P], qs[at:at + rows, g, lo:hi], start=True, stop=False)
            ins = nc.tensor.matmul(bank[:, lo:hi], c.pick[0:48, h % mg, :], mT[:, h // mg % 2, lo:hi], start=False, stop=not masked)
            if masked:
                ins = nc.tensor.matmul(bank[:, lo:lo + P], c.ident_bf[:, :], mask_b[:, :], start=False, stop=True)
            ins.then_inc(scored_b.sem, scored_b.one())

        def value(i, h, k):
            if h == 0 and k == 0:
                pe.wait_ge(w_emptied.sem, w_emptied.at(i, 0))
                pe.wait_ge(sums_copied.sem, sums_copied.at(i, 0))
            pe.wait_ge(exped.sem, exped.at(i, NT * h + k + 1))
            side, b = h // half, h % half
            col = side * half * (R + E) + b * R
            lo, hi = queries_of(k)
            ins = nc.tensor.matmul(obank[side][0:R, lo:hi], vx_flat[:, k, col:col + R], pT[:, h % 2, k, lo:hi],
                                   start=b == 0 and k == 0, stop=b == half - 1 and k == NT - 1, skip_group_check=True)
            if k == NT - 1:
                ins.then_inc(head_done.sem, head_done.one())

        def turn_sums(side):
            def emit(bank):
                for q in range(NT):
                    ins = nc.tensor.transpose(bank[:, q * R:(q + 1) * R], sums[:, side, q * P:(q + 1) * P], c.ident[0:R, 0:R])
                return ins
            return emit

        def at_place(i, h, k):
            for what in places.get((h, k), []):
                if what[0:3] == "max":
                    group = MG if what == "max_next" else int(what[-1])
                    maxima(i, group, what)
                elif what[0:4] == "sums":
                    side = int(what[-1])
                    pe.wait_ge(sums_copied.sem, sums_copied.at(i, side + 1))
                    fill(i, what, turn_sums(side))
                elif what[0:6] == "turned":
                    s = int(what[-1])
                    if s > 0:
                        pe.wait_ge(step_taken.sem, step_taken.at(i, s))
                    else:
                        pe.wait_ge(ctx_ready.sem, ctx_ready.at(i, 1))
                    fill(i, what, turn(ctxt))
                elif what[0:9] == "projected":
                    s = int(what[-1])
                    pe.wait_ge(w_emptied.sem, w_emptied.at(i, w_n(i, f"turned{s}")))
                    fill(i, what, tokens(stepT, w[out_steps[s]], w.get(out_steps[s] + "_b")))
                else:
                    prepare(i, what)

        ahead = Ahead()
        for what in W_AHEAD[:-1]:
            prepare(ahead, what)
        for h in range(heads, heads + mg + 1):
            for q in range(NT):
                score_a(ahead, h, q)
        maxima(ahead, MG, "max_next")
        for signal in (w_filled, scored_a):
            signal.ahead_done()
        with turns(pe, B) as i:
            for h in range(-1, heads):
                for k in range(NT):
                    at_place(i, h, k)
                    if h >= 0:
                        score_a(i, h + 1 + mg, k)
                        value(i, h, k)
                    if h + 1 < heads:
                        score_b(i, h + 1, k)
            at_place(i, heads, 0)
            turn_done(w_filled, scored_a, scored_b, head_done)

    @block.scalar
    def _(act):
        if future:
            act.wait_ge(prepared.sem, 1)
            nc.scalar.copy(afT[:, :, :], w0[:, :].rearrange("p (f n) -> p f n", f=4)).then_inc(prepared.sem, prepared.one())
            act.wait_ge(prepared.sem, 3)
            nc.scalar.copy(wkf[:, :, :], w1[:, :].rearrange("p (f n) -> p f n", f=4)).then_inc(prepared.sem, prepared.one())
            nc.scalar.copy(wvf[:, :, :], w0[:, :].rearrange("p (f n) -> p f n", f=4)).then_inc(prepared.sem, prepared.one())
        if bias or affine:
            wait_weights(act, c, w)
        if bias:
            act.wait_ge(prepared.sem, 2 if modulated else 1)

        def empty(i, what, *emits):
            n = w_emptied.n
            assert w_n(i, what) == n + 1, what
            act.wait_ge(w_filled.sem, w_filled.at(i, n + 1))
            bank = wbank[(n + (0 if i.ahead else len(W_AHEAD))) % 2]
            for emit in emits:
                ins = emit(bank)
            ins.then_inc(w_emptied.sem, w_emptied.one())

        def tokens_to(dst):
            return lambda bank: nc.scalar.copy(dst, bank[:, :].rearrange("p (j d) -> p j d", j=NT))

        def prepare(i, what):
            kind, g = what[0], int(what[-1]) if what[-1].isdigit() else 0
            if what == "uT":
                if affine:
                    empty(i, what, lambda bank: nc.scalar.activation(uT[:, :], bank[:, :], ACT.Identity, bias=w["shift"], scale=w["gain"]))
                else:
                    empty(i, what, lambda bank: nc.scalar.copy(uT[:, :], bank[:, :]))
            elif kind == "m":
                if not i.ahead:
                    act.wait_ge(mod_scaled.sem, mod_scaled.at(i, G))
                empty(i, what, lambda bank: nc.scalar.activation(modT[:, g, :], bank[:, :], ACT.Sigmoid, bias=mod_bias[:, g:g + 1]))
            elif kind in "qk":
                m = 2 * g + (kind == "k")
                if m >= 2 or not i.ahead:
                    act.wait_ge(stacked.sem, stacked.at(i, 2 * G + m - 1))
                part, isc = (0, scale) if kind == "q" else (1, 1.0)
                low_scale = w["maskq_scaled"] if kind == "q" else w["maskk"][1]
                at = part * G + g
                if modulated and kind == "q":
                    empty(i, what, lambda bank: nc.scalar.activation(scaled, bank[:, :], ACT.Identity, bias=sb_scaled[:, g:g + 1], scale=isc))
                    return
                empty(i, what,
                      lambda bank: nc.scalar.activation(high[:, part, :], bank[:, :], ACT.Identity, bias=sb_scaled[:, at:at + 1] if bias else 0.0, scale=isc),
                      lambda bank: nc.scalar.activation(lowpart[:, part, :], bank[:, :], ACT.Identity, bias=sb_scaled[:, 2 * G + at:2 * G + at + 1] if bias else 0.0, scale=low_scale))
            elif what == "v":
                if not i.ahead:
                    act.wait_ge(head_done.sem, head_done.at(i, heads))
                empty(i, what, lambda bank: nc.scalar.copy(vx[:, :, :, 0:hd], bank[:, :].rearrange("p (j h e) -> p j h e", j=NT, h=heads)))
            elif what == "fq":
                act.wait_ge(fut_used.sem, fut_used.at(i, 1))
                empty(i, what, tokens_to(qtok[:, :, :]))
            else:
                if i.ahead:
                    act.wait_ge(prepared.sem, 5)
                empty(i, what, tokens_to((kf if what[1] == "k" else vf)[:, g, :, :]))

        def modulated_parts(i, g):
            act.wait_ge(mod_scaled.sem, mod_scaled.at(i, G + g + 1))
            nc.scalar.copy(high[:, 0, :], scaled)
            nc.scalar.mul(lowpart[:, 0, :], scaled, w["maskq"][1]).then_inc(parts_ready.sem, parts_ready.one())

        def rows_of_maxima(i, group, what):
            if not i.ahead:
                act.wait_ge(m_copied.sem, m_copied.at(i, 2 * group))
            empty(i, what, lambda bank: nc.scalar.copy(mrow[:, :], bank[0:mg, :]))

        def at_place(i, h, k):
            for what in places.get((h, k), []):
                if what[0:3] == "max":
                    rows_of_maxima(i, MG if what == "max_next" else int(what[-1]), what)
                    if future and what == f"max{MG - 1}":
                        act.wait_ge(fut_asked.sem, fut_asked.at(i, 1))
                        nc.scalar.activation(pf[:, :, :, :], fut[:, :, :, :], ACT.Exp).then_inc(fut_exped.sem, fut_exped.one())
                elif what[0:4] == "sums":
                    side = int(what[-1])
                    empty(i, what, lambda bank: nc.scalar.copy(sums_tok[:, side, :, :, :], bank[:, 0:NT * R].rearrange("p (j b e) -> p j b e", j=NT, e=E)))
                elif what[0:6] == "turned":
                    empty(i, what, lambda bank: nc.scalar.copy(stepT[:, :], bank[:, :]))
                elif what[0:9] == "projected":
                    act.wait_ge(step_taken.sem, step_taken.at(i, int(what[-1])))
                    empty(i, what, tokens_to(stepo[:, :, :]))
                else:
                    prepare(i, what)

        def copy_sums(i, side):
            act.wait_ge(head_done.sem, head_done.at(i, (side + 1) * half))
            nc.scalar.copy(sums[:, side, :], obank[side][0:R, :]).then_inc(sums_copied.sem, sums_copied.one())

        ahead = Ahead()
        for what in W_AHEAD[:-1]:
            prepare(ahead, what)
            if modulated and what[0] == "q":
                modulated_parts(ahead, int(what[-1]))
        rows_of_maxima(ahead, MG, "max_next")
        w_emptied.ahead_done()
        parts_ready.ahead_done()
        with turns(act, B) as i:
            for h in range(-1, heads):
                if 0 <= h + 1 < heads:
                    act.wait_ge(head_done.sem, head_done.at(i, max(h, 0)))
                for k in range(NT):
                    at_place(i, h, k)
                    if h + 1 < heads:
                        lo, hi = queries_of(k)
                        n = (h + 1) * NT + k
                        act.wait_ge(scored_b.sem, scored_b.at(i, n + 1))
                        nc.scalar.activation(pT[:, (h + 1) % 2, k, lo:hi], bbank[n % 2][:, lo:hi], ACT.Exp).then_inc(exped.sem, exped.one())
                    if modulated and h in stack_at and k == 1:
                        modulated_parts(i, stack_at.index(h))
                    if h == half and k == 1:
                        copy_sums(i, 0)
            copy_sums(i, 1)
            at_place(i, heads, 0)
            turn_done(w_emptied, exped, sums_copied)

    @block.gpsimd
    def _(pool):
        for _ in range(norms_ahead):
            norm.on_gpsimd(nc, pool, c, Ahead())
        for signal in (norm.eps_added, norm.rstd_ready):
            signal.ahead_done()
        with turns(pool, B) as i:
            for _ in range(norms):
                norm.on_gpsimd(nc, pool, c, i)

    @block.vector
    def _(dve):
        wait_weights(dve, c, w)
        nc.vector.memset(vx[:, :, :, :], 0.0)
        dve.drain()
        nc.vector.memset(vx[:, :, :, hd:E], 1.0)
        nc.vector.memset(mT[:, :, :].bitcast(F32), 0.0)
        if bias:
            nc.vector.tensor_scalar(sb_scaled[:, 0:G], w["bqk"][:, 0:G], scale, None, ALU.mult)
            nc.vector.tensor_copy(sb_scaled[:, G:2 * G], w["bqk"][:, G:2 * G])
            nc.vector.tensor_scalar(sb_scaled[:, 2 * G:3 * G], w["bqk"][:, 0:G], w["maskq"][1], scale, ALU.mult, ALU.mult)
            ins = nc.vector.tensor_scalar(sb_scaled[:, 3 * G:4 * G], w["bqk"][:, G:2 * G], w["maskk"][1], None, ALU.mult)
            if modulated:
                dve.wait_ge(prepared.sem, 1)
                nc.vector.tensor_tensor(mod_bias[:, :], w0[:, 0:G], w["cg_am_bias"][:, 0:G], ALU.add).then_inc(mod_added.sem, mod_added.one())
                dve.wait_ge(mod_added.sem, 1)
                ins = nc.vector.tensor_tensor(mod_bias[:, :], mod_bias[:, :], w["cg_am_bias"][:, G:2 * G], ALU.add)
            ins.then_inc(prepared.sem, prepared.one())

        def then_in(i):
            def then(ins):
                ins.then_inc(step.sem, step.one())
                dve.wait_ge(step.sem, step.at(i, step.n))
            return then

        def next_statistics(i):
            if source is None:
                norm.statistics(nc, dve, lambda j: i.next_tile(c.x, j))

        def next_source(i):
            dve.wait_ge(w_filled.sem, w_filled.at(i, 0) if not i.ahead else 1)
            if source is None:
                if affine:
                    then_in(i)(norm.scaled(nc, dve, i, lambda j: i.next_tile(c.x, j), lambda j: i.next_tile(c.y, j)))
                    ins = norm.on_vector(nc, dve, c, i, lambda j: i.next_tile(c.y, j), lambda j: src[:, j, :], step)
                else:
                    ins = norm.scaled(nc, dve, i, lambda j: i.next_tile(c.x, j), lambda j: src[:, j, :])
            else:
                ins = nc.vector.tensor_copy(src[:, :, :], i.next_tiles(c.ctx))
            ins.then_inc(src_ready.sem, src_ready.one())
            if "mixed" in out_steps:
                dve.wait_ge(src_ready.sem, src_ready.at(i, 2))
                nc.vector.tensor_copy(i.next_tiles(c.y), src[:, :, :])

        def modulate(i, g):
            dve.wait_ge(w_emptied.sem, w_emptied.at(i, w_n(i, f"q{g}")))
            nc.vector.tensor_tensor(scaled, scaled, modT[:, g, :], ALU.mult).then_inc(mod_scaled.sem, mod_scaled.one())

        def stack(i, g, kind):
            if modulated and kind == "q":
                dve.wait_ge(parts_ready.sem, parts_ready.at(i, G + g + 1))
            else:
                dve.wait_ge(w_emptied.sem, w_emptied.at(i, w_n(i, f"{kind}{g}")))
            if not i.ahead:
                dve.wait_ge(scored_b.sem, scored_b.at(i, in_group * (g + 1) * NT))
            part, m, dst = (0, w["maskq"], qs[:, g, :]) if kind == "q" else (1, w["maskk"], ks[:, g, :])
            nc.vector.scalar_tensor_tensor(out=dst, in0=high[:, part, :].bitcast(F32), scalar=m[0], in1=lowpart[:, part, :], op0=ALU.mult, op1=ALU.add).then_inc(stacked.sem, stacked.one())

        def future_scores(i, f):
            then = then_in(i)
            dve.wait_ge(w_emptied.sem, w_emptied.at(i, w_n(i, f"fk{f}")))
            then(nc.vector.tensor_tensor(kf[:, f, :, :], kf[:, f, :, :], qtok[:, :, :], ALU.mult))
            then(nc.vector.tensor_reduce(fut[:, f, :, :], kf[:, f, :, :].rearrange("p j (h e) -> p j h e", h=heads), AX.X, ALU.add))
            if f == 3:
                nc.vector.tensor_reduce(futmax[:, :, :], fut[:, :, :, :].rearrange("p f j h -> p j h f"), AX.X, ALU.max, negate=True)
                dve.drain()

        def reduce_a(i, h, q):
            n = h * NT + q
            group = h // mg
            if q == 0 and h % mg == 0 and not i.ahead:
                dve.wait_ge(w_filled.sem, w_filled.at(i, w_n(i, f"max{group - MG}") if group > MG else 0))
            dve.wait_ge(scored_a.sem, scored_a.at(i, n + 1))
            nc.vector.tensor_reduce(negmax[:, q, h % heads:h % heads + 1], abank[n % 2][:, keys_of(q)[0]:keys_of(q)[1]], AX.X, ALU.max, negate=True).then_inc(maxed.sem, maxed.one())

        def maxima(i, group, what):
            of_group = slice(group % MG * mg, (group % MG + 1) * mg)
            if future:
                dve.wait_ge(maxed.sem, maxed.at(i, (group + 1) * mg * NT))
                nc.vector.tensor_tensor(negmax[:, :, of_group], negmax[:, :, of_group], futmax[:, :, of_group], ALU.min).then_inc(m_final.sem, m_final.one())
                if group == MG - 1:
                    dve.wait_ge(m_final.sem, m_final.at(i, MG))
                    nc.vector.tensor_tensor(fut[:, :, :, :], fut[:, :, :, :], negmax[:, :, :].unsqueeze(1).to_broadcast([P, 4, NT, heads]), ALU.add).then_inc(fut_asked.sem, fut_asked.one())
            dve.wait_ge(w_emptied.sem, w_emptied.at(i, w_n(i, what)))
            if not i.ahead:
                dve.wait_ge(scored_b.sem, scored_b.at(i, (group - 1) * mg * NT))
            part = mT[:, group % 2, :]
            nc.vector.tensor_copy(part[0:mg, :], mrow[:, :]).then_inc(m_copied.sem, m_copied.one())
            dve.wait_ge(m_copied.sem, m_copied.at(i, 2 * group + 1))
            nc.vector.tensor_tensor(part[32:32 + mg, :], mrow[:, :], part[0:mg, :].bitcast(F32), ALU.subtract).then_inc(m_copied.sem, m_copied.one())

        def future_values(i, then):
            dve.wait_ge(fut_exped.sem, fut_exped.at(i, 1))
            for f in range(4):
                ins = nc.vector.tensor_tensor(vf[:, f, :, :].rearrange("p j (h e) -> p (j h) e", h=heads), vf[:, f, :, :].rearrange("p j (h e) -> p (j h) e", h=heads),
                                              pf[:, f, :, :].rearrange("p j h -> p (j h)").unsqueeze(2).to_broadcast([P, NT * heads, hd]), ALU.mult)
            nc.vector.tensor_reduce(futden[:, :, :], pf[:, :, :, :].rearrange("p f j h -> p j h f"), AX.X, ALU.add)
            then(ins)
            then(nc.vector.tensor_tensor(vf[:, 0:2, :, :], vf[:, 0:2, :, :], vf[:, 2:4, :, :], ALU.add))
            nc.vector.tensor_tensor(tmp[:, :, :], vf[:, 0, :, :], vf[:, 1, :, :], ALU.add).then_inc(fut_used.sem, fut_used.one())
            dve.wait_ge(fut_used.sem, fut_used.at(i, 1))

        ahead = Ahead()
        next_statistics(ahead)
        next_source(ahead)
        for g in range(G):
            if modulated:
                modulate(ahead, g)
            stack(ahead, g, "q")
            stack(ahead, g, "k")
        if future:
            for f in range(4):
                future_scores(ahead, f)
        for h in range(heads, heads + mg + 1):
            for q in range(NT):
                reduce_a(ahead, h, q)
        maxima(ahead, MG, "max_next")
        for signal in (step, norm.variance, stacked, maxed, m_copied, m_final, src_ready, mod_scaled):
            signal.ahead_done()
        with turns(dve, B) as i:
            then = then_in(i)
            for h in range(-1, heads):
                if h == -1:
                    next_statistics(i)
                if h == 0:
                    next_source(i)
                if 0 < h + 1 < heads and (h + 1) % mg == 0:
                    maxima(i, (h + 1) // mg, f"max{(h + 1) // mg}")
                if future and h == 12:
                    future_values(i, then)
                for k in range(NT):
                    if h in stack_at:
                        g = stack_at.index(h)
                        if modulated and k == 1:
                            modulate(i, g)
                        if k == 2 + modulated:
                            stack(i, g, "q")
                    if h - 1 in stack_at and k == (mg > 1):
                        stack(i, stack_at.index(h - 1), "k")
                    if future and (h, k) in ((14, 0), (15, 0), (15, 2)):
                        future_scores(i, ((14, 0), (15, 0), (15, 2)).index((h, k)))
                    if h >= 0:
                        reduce_a(i, h + 1 + mg, k)
            stack(i, stack_at.index(heads - 1), "k")
            if heads in stack_at:
                stack(i, G - 1, "q")
                stack(i, G - 1, "k")
            if future:
                future_scores(i, 3)
            maxima(i, MG, "max_next")
            dve.wait_ge(w_emptied.sem, w_emptied.at(i, w_n(i, "sums1")))
            if future:
                then(nc.vector.tensor_tensor(rden[:, :, :, :], sums_tok[:, :, :, :, hd], futden[:, :, :].rearrange("p j (s b) -> p s j b", s=2), ALU.add))
                then(nc.vector.reciprocal(rden[:, :, :, :], rden[:, :, :, :]))
            else:
                then(nc.vector.reciprocal(rden[:, :, :, :], sums_tok[:, :, :, :, hd]))
            for side in range(2):
                den = rden[:, side, :, :].unsqueeze(3).to_broadcast([P, NT, half, hd])
                part = slice(side * half * hd, (side + 1) * half * hd)
                dst = ctxt[:, :, part].rearrange("p j (b e) -> p j b e", b=half)
                if future:
                    more = tmp[:, :, part].rearrange("p j (b e) -> p j b e", b=half)
                    then(nc.vector.tensor_tensor(more, more, sums_tok[:, side, :, :, 0:hd], ALU.add))
                    ins = nc.vector.tensor_tensor(dst, more, den, ALU.mult)
                else:
                    ins = nc.vector.tensor_tensor(dst, sums_tok[:, side, :, :, 0:hd], den, ALU.mult)
            ins.then_inc(ctx_ready.sem, ctx_ready.one())
            dve.wait_ge(ctx_ready.sem, ctx_ready.at(i, 1))
            result = ctxt
            for s in range(len(out_steps)):
                kind = out_steps[s]
                dve.wait_ge(w_emptied.sem, w_emptied.at(i, w_n(i, f"projected{s}")))
                if kind == "mixed":
                    nc.vector.tensor_tensor(tmp[:, :, :], stepo[:, :, :], tiles_of(c.y, i), ALU.add).then_inc(step_taken.sem, step_taken.one())
                    dve.wait_ge(step_taken.sem, step_taken.at(i, s + 1))
                    then(norm.on_vector(nc, dve, c, i, lambda j: tmp[:, j, :], lambda j: ctxt[:, j, :], step))
                    then(nc.vector.tensor_tensor(ctxt[:, :, :], ctxt[:, :, :], wide(w["g1"]), ALU.mult))
                    then(nc.vector.tensor_tensor(tiles_of(c.y, i), ctxt[:, :, :], wide(w["be1"]), ALU.add))
                elif kind == "proj":
                    nc.vector.tensor_tensor(tiles_of(c.y, i), stepo[:, :, :], tiles_of(c.y, i), ALU.add).then_inc(step_taken.sem, step_taken.one())
                elif kind == "causal_out":
                    then(nc.vector.tensor_scalar(stepo[:, :, :], stepo[:, :, :], w["mix"][1], None, ALU.mult))
                    nc.vector.scalar_tensor_tensor(out=tiles_of(c.ctx, i), in0=tiles_of(c.ctx, i), scalar=w["mix"][0], in1=stepo[:, :, :], op0=ALU.mult, op1=ALU.add).then_inc(step_taken.sem, step_taken.one())
                elif kind == "meta_out":
                    then(nc.vector.tensor_scalar(stepo[:, :, :], stepo[:, :, :], w["mix"][1], None, ALU.mult))
                    nc.vector.scalar_tensor_tensor(out=ctxt[:, :, :], in0=tiles_of(c.ctx, i), scalar=w["mix"][0], in1=stepo[:, :, :], op0=ALU.mult, op1=ALU.add).then_inc(step_taken.sem, step_taken.one())
                else:
                    result = stepo
            if finish == "residual_norm":
                then(norm.on_vector(nc, dve, c, i, lambda j: result[:, j, :], lambda j: tmp[:, j, :], step))
                ins = nc.vector.tensor_tensor(tiles_of(c.x, i), tiles_of(c.x, i), tmp[:, :, :], ALU.add)
                if result is stepo:
                    ins.then_inc(step_taken.sem, step_taken.one())
                    dve.wait_ge(step_taken.sem, step_taken.at(i, len(out_steps)))
                else:
                    then(ins)
            elif finish == "context":
                then(nc.vector.tensor_copy(tiles_of(c.ctx, i), ctxt[:, :, :]))
            turn_done(step, norm.variance, stacked, maxed, m_copied, ctx_ready)
    ph.close()



class Layer:

    def __init__(self, kb, mb, W, func, scale=None, bias=None, V=None, v_op=None, v_arg=None):
        self.kb, self.mb, self.W, self.func, self.scale, self.bias = kb, mb, W, func, scale, bias
        self.V, self.v_op, self.v_arg = V, v_op, v_arg


def mlp_phase(nc, c, name, w, layers, final, experts=1, source="x", affine=False, shifted=False, gate=None,
              out_scale=False, add_y=False, tail_gain=False, finish="residual_norm"):
    ph = Phase(nc, name)
    S = ph.flag
    L = layers(0)
    gated = any(l.V is not None for l in L)
    moe = experts > 1
    top1 = gate == "top1"
    NA = 1 + experts * sum(l.mb for l in L) + top1
    NB = shifted + moe + experts * (1 + sum(l.mb for l in L if l.V is not None)) + top1
    widest = max(l.mb for l in L)
    norms_ahead = int(source == "x" or affine or shifted)
    norms = norms_ahead + (finish == "residual_norm") + tail_gain
    src = ph.sb("src", [P, NT, D])
    uT = ph.sb("uT", [P, T])
    hidden = [ph.sb(f"hidden{k}", [P, widest, T]) for k in range(2)]
    gates = ph.sb("gates", [P, 2, T]) if gated else None
    acc = ph.sb("acc", [P, NT, D])
    tmp = ph.sb("tmp", [P, NT, D])
    if moe:
        logit = ph.sb("logit", [P, NT, 8])
        chosen = ph.sb("chosen", [P, NT, 8])
        second = ph.sb("second", [P, NT, 8])
        small = ph.sb("small", [P, 4, NT])
        chosenT = ph.sb("chosenT", [8, T])
    ring_a, ring_b = c.bank[0:4], c.bank[4:8]
    a_filled, a_emptied, b_filled, b_emptied = S("a_filled", NA, 1), S("a_emptied", NA, 1), S("b_filled", NB, shifted + moe), S("b_emptied", NB, shifted + moe)
    src_ready, expected, exped = S("src_ready"), S("exp_asked"), S("gate_exped")
    chosen_ready = S("chosen_ready")
    steps = {"residual_norm": 2}.get(finish, 0) + 3 * tail_gain + {None: 0, "top1": 4, "top2": 18}[gate]
    step = S("dve_step", steps, {None: 0, "top1": 4, "top2": 18}[gate])
    norm = Norm(ph, max(norms, 1), norms_ahead)
    block = ph.block()

    @block.sync
    def _(sp):
        load_next(sp, c)

    def order():
        out = []
        for e in range(experts):
            out.append(("up", e))
            if e == 0 and top1:
                out.append(("chosen", 0))
            if e > 0:
                out.append(("down", e - 1))
        return out + [("down", experts - 1)]

    @block.tensor
    def _(pe):
        wait_weights(pe, c, w)

        def fill(i, ring, n, filled, emptied, emit):
            if n[0] > 3 or not i.ahead:
                pe.wait_ge(emptied.sem, emptied.at(i, max(n[0] - 3, 0)))
            emit(ring[n[0] % 4]).then_inc(filled.sem, filled.one())
            n[0] += 1

        def next_shifted(i, nb):
            def emit(bank):
                for j in range(NT):
                    dst = bank[:, j * H2:(j + 1) * H2]
                    ins = nc.tensor.matmul(dst, c.shift[:, 0, :], i.next_tile(c.y, j)[:, :, H2:D], start=True, stop=j == 0)
                    if j > 0:
                        ins = nc.tensor.matmul(dst, c.shift[:, 1, :], i.next_tile(c.y, j - 1)[:, :, H2:D], start=False, stop=True)
                return ins
            fill(i, ring_b, nb, b_filled, b_emptied, emit)

        def next_turned(i, na):
            pe.wait_ge(src_ready.sem, src_ready.at(i, 2))

            def turn(bank):
                for j in range(NT):
                    ins = nc.tensor.transpose(bank[:, j * P:(j + 1) * P], src[:, j, :], c.ident[:, :])
                return ins
            fill(i, ring_a, na, a_filled, a_emptied, turn)

        def next_logits(i, na, nb):
            pe.wait_ge(a_emptied.sem, a_emptied.at(i, na[0]))

            def emit(bank):
                for j in range(NT):
                    ins = nc.tensor.matmul(bank[:, j * 8:(j + 1) * 8], uT[:, j * P:(j + 1) * P], w["gate"], start=True, stop=True)
                return ins
            fill(i, ring_b, nb, b_filled, b_emptied, emit)

        ahead, na, nb = Ahead(), [0], [0]
        if shifted:
            next_shifted(ahead, nb)
        next_turned(ahead, na)
        if moe:
            next_logits(ahead, na, nb)
        a_filled.ahead_done()
        b_filled.ahead_done()
        with turns(pe, B) as i:
            na, nb = [0], [0]
            fill_a = lambda emit: fill(i, ring_a, na, a_filled, a_emptied, emit)
            fill_b = lambda emit: fill(i, ring_b, nb, b_filled, b_emptied, emit)
            if shifted:
                next_shifted(i, nb)
            pe.wait_ge(a_emptied.sem, a_emptied.at(i, 0))
            ready = {}

            def product(bank, W, m, kb, src_of):
                for k in range(kb):
                    ins = nc.tensor.matmul(bank[:, :], W(k, m), src_of(k), start=k == 0, stop=k == kb - 1)
                return ins

            for what, e in order():
                if what == "up":
                    src_of = lambda k: uT[:, :]
                    for l, layer in enumerate(layers(e)):
                        for m in range(layer.mb):
                            fill_a(lambda bank: product(bank, layer.W, m, layer.kb, src_of))
                            if layer.V is not None:
                                fill_b(lambda bank: product(bank, layer.V, m, layer.kb, src_of))
                        buf = hidden[(e + l) % 2]
                        ready[e] = (b_emptied, nb[0]) if layer.V is not None else (a_emptied, na[0])
                        src_of = (lambda b: lambda k: b[:, k, :])(buf)
                        if l + 1 < len(layers(e)):
                            pe.wait_ge(ready[e][0].sem, ready[e][0].at(i, ready[e][1]))
                elif what == "chosen":
                    pe.wait_ge(chosen_ready.sem, chosen_ready.at(i, 1))

                    def turn_chosen(bank):
                        for j in range(NT):
                            ins = nc.tensor.transpose(bank[0:8, j * P:(j + 1) * P], chosen[:, j, :], c.ident[:, :])
                        return ins
                    fill_a(turn_chosen)
                    pe.wait_ge(a_emptied.sem, a_emptied.at(i, na[0]))

                    def chosen_bias(bank):
                        for j in range(NT):
                            ins = nc.tensor.matmul(bank[:, j * P:(j + 1) * P], chosenT[:, j * P:(j + 1) * P], w["expert_bias"], start=True, stop=True)
                        return ins
                    fill_b(chosen_bias)
                else:
                    if e == experts - 1:
                        next_turned(i, na)
                    pe.wait_ge(ready[e][0].sem, ready[e][0].at(i, ready[e][1]))
                    kb, W = final(e)
                    buf = hidden[(e + len(L) - 1) % 2]

                    def down(bank):
                        for j in range(NT):
                            for k in range(kb):
                                ins = nc.tensor.matmul(bank[:, j * P:(j + 1) * P], buf[:, k, j * P:(j + 1) * P], W(k), start=k == 0, stop=k == kb - 1 and "final_b" not in w)
                            if "final_b" in w:
                                ins = nc.tensor.matmul(bank[:, j * P:(j + 1) * P], c.ones[0:1, :], w["final_b"], start=False, stop=True)
                        return ins
                    fill_b(down)
            if moe:
                next_logits(i, na, nb)
            turn_done(a_filled, b_filled)

    @block.scalar
    def _(act):
        wait_weights(act, c, w)

        def empty(i, na, emit):
            act.wait_ge(a_filled.sem, a_filled.at(i, na[0] + 1))
            emit(ring_a[na[0] % 4]).then_inc(a_emptied.sem, a_emptied.one())
            na[0] += 1

        def next_turned(i, na):
            if affine:
                empty(i, na, lambda bank: nc.scalar.activation(uT[:, :], bank[:, :], ACT.Identity, bias=w["shift"], scale=w["gain"]))
            else:
                empty(i, na, lambda bank: nc.scalar.copy(uT[:, :], bank[:, :]))

        def next_gate(i):
            if gate == "top2":
                act.wait_ge(expected.sem, expected.at(i, 2))
                nc.scalar.activation(logit[:, :, :], logit[:, :, :], ACT.Exp).then_inc(exped.sem, exped.one())

        next_turned(Ahead(), [0])
        next_gate(Ahead())
        a_emptied.ahead_done()
        with turns(act, B) as i:
            na, nb = [0], [int(shifted)]
            for what, e in order():
                if what == "up":
                    for l, layer in enumerate(layers(e)):
                        for m in range(layer.mb):
                            if layer.V is not None:
                                k = nb[0]
                                act.wait_ge(b_emptied.sem, b_emptied.at(i, max(k - 1, 0)))
                                dst = gates[:, nb[0] % 2, :]
                                nb[0] += 1
                            else:
                                dst = hidden[(e + l) % 2][:, m, :]
                            kw = {}
                            if layer.scale is not None:
                                kw["scale"] = layer.scale(m)
                            if layer.bias is not None:
                                kw["bias"] = layer.bias(m)
                            empty(i, na, lambda bank: nc.scalar.activation(dst, bank[:, :], layer.func, **kw))
                elif what == "chosen":
                    empty(i, na, lambda bank: nc.scalar.copy(chosenT[:, :], bank[0:8, :]))
                    nb[0] += 1
                else:
                    if e == experts - 1:
                        next_turned(i, na)
                    nb[0] += 1
            next_gate(i)
            turn_done(a_emptied)

    @block.gpsimd
    def _(pool):
        for _ in range(norms_ahead):
            norm.on_gpsimd(nc, pool, c, Ahead())
        for signal in (norm.eps_added, norm.rstd_ready):
            signal.ahead_done()
        with turns(pool, B) as i:
            for _ in range(norms):
                norm.on_gpsimd(nc, pool, c, i)

    @block.vector
    def _(dve):
        wait_weights(dve, c, w)
        whole = c.x if source == "x" else c.y

        def then_in(i):
            def then(ins):
                ins.then_inc(step.sem, step.one())
                dve.wait_ge(step.sem, step.at(i, step.n))
            return then

        def empty_b(i, nb, emit):
            dve.wait_ge(b_filled.sem, b_filled.at(i, nb[0] + 1))
            emit(ring_b[nb[0] % 4]).then_inc(b_emptied.sem, b_emptied.one())
            nb[0] += 1
            return nb[0]

        def next_begun(i, nb):
            if shifted:
                if not i.ahead:
                    dve.wait_ge(a_filled.sem, a_filled.at(i, 0))

                def take_shifted(bank):
                    nc.vector.tensor_copy(src[:, :, 0:H2], i.next_tiles(c.y)[:, :, 0:H2])
                    return nc.vector.tensor_copy(src[:, :, H2:D], bank[:, 0:NT * H2].rearrange("p (j d) -> p j d", j=NT))
                n = empty_b(i, nb, take_shifted)
                dve.wait_ge(b_emptied.sem, b_emptied.at(i, n))
                norm.statistics(nc, dve, lambda j: src[:, j, :])
            elif source == "x" or affine:
                norm.statistics(nc, dve, lambda j: i.next_tile(whole, j))

        def next_scaled(i):
            if not i.ahead:
                dve.wait_ge(a_filled.sem, a_filled.at(i, 0))
            if shifted:
                ins = norm.scaled(nc, dve, i, lambda j: src[:, j, :], lambda j: src[:, j, :])
            elif source == "x" or affine:
                ins = norm.scaled(nc, dve, i, lambda j: i.next_tile(whole, j), lambda j: src[:, j, :])
            else:
                ins = nc.vector.tensor_copy(src[:, :, :], i.next_tiles(whole))
            ins.then_inc(src_ready.sem, src_ready.one())

        def next_gate(i, nb):
            then = then_in(i)
            bc = lambda a: a.unsqueeze(2).to_broadcast([P, NT, 8])
            down8 = c.down8[:, :].unsqueeze(1).to_broadcast([P, NT, 8])
            n = empty_b(i, nb, lambda bank: nc.vector.tensor_copy(logit[:, :, :], bank[:, 0:8 * NT].rearrange("p (j e) -> p j e", e=8)))
            dve.wait_ge(b_emptied.sem, b_emptied.at(i, n))

            def first_of(values, largest, dst):
                then(nc.vector.tensor_tensor(dst, values, bc(largest), ALU.is_ge))
                then(nc.vector.tensor_tensor(dst, dst, down8, ALU.mult))
                then(nc.vector.tensor_reduce(small[:, 3, :], dst, AX.X, ALU.max))
                return nc.vector.tensor_tensor(dst, dst, bc(small[:, 3, :]), ALU.is_equal)

            then(nc.vector.tensor_reduce(small[:, 0, :], logit[:, :, :], AX.X, ALU.max))
            if gate == "top1":
                first_of(logit[:, :, :], small[:, 0, :], chosen[:, :, :]).then_inc(chosen_ready.sem, chosen_ready.one())
                dve.wait_ge(chosen_ready.sem, chosen_ready.at(i, 2))
                return
            nc.vector.tensor_tensor(logit[:, :, :], logit[:, :, :], bc(small[:, 0, :]), ALU.subtract).then_inc(expected.sem, expected.one())
            dve.wait_ge(exped.sem, exped.at(i, 2))
            then(nc.vector.tensor_reduce(small[:, 0, :], logit[:, :, :], AX.X, ALU.add))
            then(nc.vector.reciprocal(small[:, 0, :], small[:, 0, :]))
            then(nc.vector.tensor_tensor(logit[:, :, :], logit[:, :, :], bc(small[:, 0, :]), ALU.mult))
            then(nc.vector.tensor_reduce(small[:, 0, :], logit[:, :, :], AX.X, ALU.max))
            then(first_of(logit[:, :, :], small[:, 0, :], chosen[:, :, :]))
            then(nc.vector.scalar_tensor_tensor(out=second[:, :, :], in0=chosen[:, :, :], scalar=-2.0, in1=logit[:, :, :], op0=ALU.mult, op1=ALU.add))
            then(nc.vector.tensor_reduce(small[:, 1, :], second[:, :, :], AX.X, ALU.max))
            nc.vector.tensor_tensor(small[:, 2, :], small[:, 0, :], small[:, 1, :], ALU.add)
            then(first_of(second[:, :, :], small[:, 1, :], second[:, :, :]))
            nc.vector.tensor_tensor(chosen[:, :, :], chosen[:, :, :], second[:, :, :], ALU.add)
            then(nc.vector.tensor_scalar(small[:, 2, :], small[:, 2, :], 1e-8, None, ALU.add))
            nc.vector.tensor_tensor(chosen[:, :, :], chosen[:, :, :], logit[:, :, :], ALU.mult)
            then(nc.vector.reciprocal(small[:, 2, :], small[:, 2, :]))
            then(nc.vector.tensor_tensor(chosen[:, :, :], chosen[:, :, :], bc(small[:, 2, :]), ALU.mult))

        ahead, nb = Ahead(), [0]
        next_begun(ahead, nb)
        next_scaled(ahead)
        if moe:
            next_gate(ahead, nb)
        for signal in (step, b_emptied, norm.variance, src_ready, chosen_ready):
            signal.ahead_done()
        with turns(dve, B) as i:
            na, nb = [0], [0]
            then = then_in(i)
            emptyb = lambda emit: empty_b(i, nb, emit)
            if not moe:
                next_begun(i, nb)
            for what, e in order():
                if moe and (what, e) == ("up", experts - 2):
                    next_begun(i, nb)
                if (what, e) == ("down", max(experts - 2, 0)):
                    next_scaled(i)
                if what == "up":
                    for l, layer in enumerate(layers(e)):
                        for m in range(layer.mb):
                            na[0] += 1
                            if layer.V is not None:
                                dve.wait_ge(a_emptied.sem, a_emptied.at(i, na[0]))
                                g = gates[:, nb[0] % 2, :]
                                arg = layer.v_arg(m) if layer.v_arg is not None else 1.0
                                emptyb(lambda bank: nc.vector.scalar_tensor_tensor(out=hidden[(e + l) % 2][:, m, :], in0=bank[:, :], scalar=arg, in1=g, op0=layer.v_op or ALU.mult, op1=ALU.mult))
                elif what == "chosen":
                    na[0] += 1
                    n = emptyb(lambda bank: nc.vector.tensor_tensor(acc[:, :, :], bank[:, :].rearrange("p (j d) -> p j d", j=NT), src[:, :, :], ALU.add))
                    dve.wait_ge(b_emptied.sem, b_emptied.at(i, n))
                elif moe:
                    def add(bank):
                        for j in range(NT):
                            part = bank[:, j * P:(j + 1) * P]
                            if e == 0 and not top1:
                                ins = nc.vector.tensor_scalar(acc[:, j, :], part, chosen[:, j, e:e + 1], None, ALU.mult)
                            else:
                                ins = nc.vector.scalar_tensor_tensor(out=acc[:, j, :], in0=part, scalar=chosen[:, j, e:e + 1], in1=acc[:, j, :], op0=ALU.mult, op1=ALU.add)
                        return ins
                    n = emptyb(add)
                    dve.wait_ge(b_emptied.sem, b_emptied.at(i, n))
                else:
                    def take(bank):
                        part = bank[:, :].rearrange("p (j d) -> p j d", j=NT)
                        if out_scale:
                            return nc.vector.tensor_tensor(acc[:, :, :], part, wide(w["out_scale"]), ALU.mult)
                        dst = tiles_of(c.y, i) if finish == "y" else acc[:, :, :]
                        return nc.vector.tensor_tensor(dst, part, tiles_of(c.y, i), ALU.add)
                    n = emptyb(take)
                    dve.wait_ge(b_emptied.sem, b_emptied.at(i, n))
            if moe:
                next_gate(i, nb)
            if tail_gain:
                then(norm.on_vector(nc, dve, c, i, lambda j: acc[:, j, :], lambda j: tmp[:, j, :], step))
                then(nc.vector.tensor_tensor(tmp[:, :, :], tmp[:, :, :], wide(w["g2"]), ALU.mult))
                then(nc.vector.tensor_tensor(acc[:, :, :], tmp[:, :, :], wide(w["be2"]), ALU.add))
            if finish == "residual_norm":
                then(norm.on_vector(nc, dve, c, i, lambda j: acc[:, j, :], lambda j: tmp[:, j, :], step))
                then(nc.vector.tensor_tensor(tiles_of(c.x, i), tiles_of(c.x, i), tmp[:, :, :], ALU.add))
            turn_done(b_emptied, step)
    ph.close()



def local_attention_phase(nc, c, name, w, first):
    heads, hd = 8, 64
    E = hd + 1
    inner = heads * hd
    BLK = inner // P
    SPAN = P + hd
    units = NT * heads
    ph = Phase(nc, name)
    S = ph.flag
    W_USES = 1 + 3 * NT + 2 * NT + 1 + NT + 1
    src = ph.sb("src", [P, NT, D])
    uT = ph.sb("uT", [P, T])
    raw = ph.sb("raw", [P, 2, 2, heads, hd])
    square = ph.sb("square", [P, 2, heads, hd])
    turned = ph.sb("turned", [P, 2, 2, heads, hd])
    inv = ph.sb("inv", [P, 2, 2 * heads])
    cosines = ph.sb("cosines", [P, NT, 2, hd])
    sines = ph.sb("sines", [P, NT, 2, hd])
    qT = ph.sb("qT", [P, BLK, T])
    kT = ph.sb("kT", [P, BLK, T])
    vx = ph.sb("vx", [P, NT, heads, E])
    negmax = ph.sb("negmax", [P, NT, heads])
    mrow = ph.sb("mrow", [heads, T])
    mT = ph.sb("mT", [P, T], F32R)
    pT = ph.sb("pT", [P, 2, heads, SPAN])
    rden = ph.sb("rden", [P, 2, heads])
    stepo = ph.sb("stepo", [P, NT, D])
    ctxt = c.ctx[:, 0:NT * BLK, :].rearrange("p (j b) d -> p j (b d)", j=NT)
    ctxT = c.ctx[:, NT * BLK:2 * NT * BLK, :].rearrange("p (b j) d -> p b (j d)", b=BLK)

    wbank = (c.bank[0], c.bank[1])
    sbank = (c.bank[2], c.bank[3])
    obank = ((c.bank[4], c.bank[5]), (c.bank[6], c.bank[7]))
    tables = S("tables", 0)
    src_ready = S("src_ready")
    w_filled, w_emptied = S("w_filled", W_USES), S("w_emptied", W_USES)
    squared, summed, inverted = S("squared", 2 * NT), S("summed", 2 * NT), S("inverted", 2 * NT)
    floored = S("floored", NT)
    sines_done, rotated = S("sines_done", NT), S("rotated", NT)
    scored_a, maxed = S("scored_a", units), S("maxed", units)
    m_copied = S("m_copied", 2)
    scored_b, exped = S("scored_b", units), S("exped", units)
    tile_done, o_taken = S("tile_done", NT), S("o_taken", NT)
    step = S("dve_step", 3 * NT)
    stored = S("stored")
    norm = Norm(ph, 1)
    block = ph.block()

    def keys_of(q):
        return max(q * P - hd, 0), (q + 1) * P

    def queries_of(k):
        return k * P, min(k * P + SPAN, T)

    def order():
        out = [("qkv", 0)]
        for j in range(1, NT):
            out += [("qkv", j), ("turn", j - 1)]
        return out + [("turn", NT - 1)]

    @block.sync
    def _(sp):
        load_next(sp, c)

    @block.tensor
    def _(pe):
        wait_weights(pe, c, w)
        with turns(pe, B) as i:
            use = [0]

            def fill(emit):
                n = use[0]
                pe.wait_ge(w_emptied.sem, w_emptied.at(i, max(n - 1, 0)))
                emit(wbank[n % 2]).then_inc(w_filled.sem, w_filled.one())
                use[0] += 1

            def turn(tiles, width=P):
                def emit(bank):
                    for k, t in enumerate(tiles):
                        ins = nc.tensor.transpose(bank[0:width, k * P:(k + 1) * P], t, c.ident[:, :])
                    return ins
                return emit

            pe.wait_ge(src_ready.sem, src_ready.at(i, 1))
            fill(turn([src[:, j, :] for j in range(NT)]))
            pe.wait_ge(w_emptied.sem, w_emptied.at(i, 1))
            for what, j in order():
                if what == "qkv":
                    for part in range(3):
                        fill(lambda bank: nc.tensor.matmul(bank[:, :], uT[:, j * P:(j + 1) * P], w["qkv"][:, part * inner:(part + 1) * inner], start=True, stop=True))
                else:
                    pe.wait_ge(rotated.sem, rotated.at(i, j + 1))
                    for side in range(2):
                        flat = turned[:, j % 2, side, :, :].rearrange("p h d -> p (h d)")
                        fill(turn([flat[:, b * P:(b + 1) * P] for b in range(BLK)]))
            pe.wait_ge(w_emptied.sem, w_emptied.at(i, use[0]))
            pe.wait_ge(exped.sem, exped.at(i, 0))
            for q in range(NT):
                lo, hi = keys_of(q)
                for h in range(heads):
                    n, at = q * heads + h, h % 2 * hd
                    pe.wait_ge(maxed.sem, maxed.at(i, max(n - 1, 0)))
                    bank = sbank[n % 2]
                    nc.tensor.matmul(bank[:, 0:hi - lo], qT[at:at + hd, h // 2, q * P:(q + 1) * P], kT[at:at + hd, h // 2, lo:hi], start=True, stop=False)
                    nc.tensor.matmul(bank[:, 0:hi - lo], c.ident_bf[:, :], c.far_keys[:, SPAN - (hi - lo):SPAN], start=False, stop=True).then_inc(scored_a.sem, scored_a.one())
            pe.wait_ge(maxed.sem, maxed.at(i, units))
            fill(turn([negmax[:, q, :] for q in range(NT)], heads))
            pe.wait_ge(m_copied.sem, m_copied.at(i, 2))

            def scores_b(k, h):
                n, at = k * heads + h, h % 2 * hd
                lo, hi = queries_of(k)
                pe.wait_ge(exped.sem, exped.at(i, max(n - 1, 0)))
                bank = sbank[n % 2]
                nc.tensor.matmul(bank[:, 0:hi - lo], kT[at:at + hd, h // 2, k * P:(k + 1) * P], qT[at:at + hd, h // 2, lo:hi], start=True, stop=False)
                nc.tensor.matmul(bank[:, 0:hi - lo], c.pick[:, h, :], mT[:, lo:hi], start=False, stop=False)
                nc.tensor.matmul(bank[:, 0:hi - lo], c.ident_bf[:, :], c.far_queries[:, 0:hi - lo], start=False, stop=True).then_inc(scored_b.sem, scored_b.one())

            def values(q, h):
                pe.wait_ge(exped.sem, exped.at(i, q * heads + h + 1))
                if h == 0:
                    pe.wait_ge(o_taken.sem, o_taken.at(i, max(q - 1, 0)))
                dst = obank[q % 2][h // 4][:, h % 4 * E:(h % 4 + 1) * E]
                ins = nc.tensor.matmul(dst, pT[:, q % 2, h, 0:P], vx[:, q, h, :], start=True, stop=True)
                if q > 0:
                    ins = nc.tensor.matmul(dst[0:hd, :], pT[:, (q - 1) % 2, h, P:SPAN], vx[:, q - 1, h, :], start=False, stop=True, skip_group_check=True)
                if h == heads - 1:
                    ins.then_inc(tile_done.sem, tile_done.one())

            for k in range(NT):
                for h in range(heads):
                    scores_b(k, h)
                    if h >= 2:
                        values(k, h - 2)
                values(k, heads - 2)
                values(k, heads - 1)
            for j in range(NT):
                pe.wait_ge(o_taken.sem, o_taken.at(i, j + 1))
                fill(turn([ctxt[:, j, b * P:(b + 1) * P] for b in range(BLK)]))
            pe.wait_ge(w_emptied.sem, w_emptied.at(i, use[0]))

            def out(bank):
                for j in range(NT):
                    for b in range(BLK):
                        ins = nc.tensor.matmul(bank[:, j * P:(j + 1) * P], ctxT[:, b, j * P:(j + 1) * P], w["wo"][:, b * P:(b + 1) * P], start=b == 0, stop=b == BLK - 1)
                return ins
            fill(out)
            assert use[0] == W_USES
            turn_done(w_filled, scored_a, scored_b, tile_done)

    @block.scalar
    def _(act):
        with turns(act, B) as i:
            use = [0]

            def empty(emit):
                n = use[0]
                act.wait_ge(w_filled.sem, w_filled.at(i, n + 1))
                emit(wbank[n % 2]).then_inc(w_emptied.sem, w_emptied.one())
                use[0] += 1

            def take_shifted(bank):
                nc.scalar.copy(uT[0:H2, :], bank[0:H2, :])
                return nc.scalar.copy(uT[H2:P, 1:T], bank[H2:P, 0:T - 1])
            if True:
                act.wait_ge(tables.sem, 3)
            empty(take_shifted)
            for what, j in order():
                if what == "qkv":
                    for side in range(2):
                        n = use[0]
                        if side == 0:
                            act.wait_ge(rotated.sem, rotated.at(i, max(j - 1, 0)))
                        act.wait_ge(w_filled.sem, w_filled.at(i, n + 1))
                        nc.scalar.copy(raw[:, j % 2, side, :, :], wbank[n % 2][:, :].rearrange("p (h d) -> p h d", h=heads))
                        act.wait_ge(summed.sem, summed.at(i, max(2 * j - 1 + side, 0)))
                        nc.scalar.activation(square[:, side, :, :], wbank[n % 2][:, :].rearrange("p (h d) -> p h d", h=heads), ACT.Square).then_inc(w_emptied.sem, w_emptied.one())
                        use[0] += 1
                    if j == 0:
                        act.wait_ge(tile_done.sem, tile_done.at(i, 0))
                    empty(lambda bank: nc.scalar.copy(vx[:, j, :, 0:hd], bank[:, :].rearrange("p (h d) -> p h d", h=heads)))
                else:
                    for dst in (qT, kT):
                        empty(lambda bank: nc.scalar.copy(dst[:, :, j * P:(j + 1) * P], bank[:, :].rearrange("p (b n) -> p b n", b=BLK)))
            act.wait_ge(m_copied.sem, m_copied.at(i, 0))
            empty(lambda bank: nc.scalar.copy(mrow[:, :], bank[0:heads, :]))
            for k in range(NT):
                for h in range(heads):
                    n = k * heads + h
                    lo, hi = queries_of(k)
                    if h == 0:
                        act.wait_ge(tile_done.sem, tile_done.at(i, max(k - 1, 0)))
                    act.wait_ge(scored_b.sem, scored_b.at(i, n + 1))
                    nc.scalar.activation(pT[:, k % 2, h, 0:hi - lo], sbank[n % 2][:, 0:hi - lo], ACT.Exp).then_inc(exped.sem, exped.one())
            for j in range(NT):
                empty(lambda bank: nc.scalar.copy(ctxT[:, :, j * P:(j + 1) * P], bank[:, :].rearrange("p (b n) -> p b n", b=BLK)))
            act.wait_ge(stored.sem, stored.at(i, 0))
            empty(lambda bank: nc.scalar.copy(stepo[:, :, :], bank[:, :].rearrange("p (j d) -> p j d", j=NT)))
            assert use[0] == W_USES

    @block.gpsimd
    def _(pool):
        pool.wait_ge(tables.sem, 3)
        with turns(pool, B) as i:
            if first:
                norm.on_gpsimd(nc, pool, c, i)
            for j in range(NT):
                pool.wait_ge(floored.sem, floored.at(i, j + 1))
                nc.gpsimd.tensor_tensor(inv[:, j % 2, :], inv[:, j % 2, :], c.minus_half16[:, :], ALU.pow).then_inc(inverted.sem, inverted.one())
                sin = sines[:, j, :, :].unsqueeze(2).to_broadcast([P, 2, heads, hd])
                nc.gpsimd.tensor_tensor(turned[:, j % 2, :, :, 0:hd // 2], raw[:, j % 2, :, :, hd // 2:hd], sin[:, :, :, 0:hd // 2], ALU.mult)
                nc.gpsimd.tensor_tensor(turned[:, j % 2, :, :, hd // 2:hd], raw[:, j % 2, :, :, 0:hd // 2], sin[:, :, :, hd // 2:hd], ALU.mult).then_inc(sines_done.sem, sines_done.one())

    @block.vector
    def _(dve):
        wait_weights(dve, c, w)
        nc.vector.memset(vx[:, :, :, hd:E], 1.0)
        nc.vector.memset(mT[:, :].bitcast(F32), 0.0)
        nc.vector.memset(inv[:, :, :], 1.0)
        nc.vector.memset(uT[H2:P, 0:1], 0.0).then_inc(tables.sem, tables.one())
        rows = lambda t: t.rearrange("p (j s d) -> p j s d", j=NT, s=2)
        gains = lambda t: t.rearrange("p (s d) -> p s d", s=2).unsqueeze(1).to_broadcast([P, NT, 2, hd])
        nc.vector.tensor_tensor(cosines[:, :, :, :], rows(w["cosines"]), gains(w["gains"]), ALU.mult).then_inc(tables.sem, tables.one())
        nc.vector.tensor_tensor(sines[:, :, :, :], rows(w["sines"]), gains(w["gains_turned"]), ALU.mult).then_inc(tables.sem, tables.one())
        dve.wait_ge(tables.sem, 3)
        with turns(dve, B) as i:
            def then(ins):
                ins.then_inc(step.sem, step.one())
                dve.wait_ge(step.sem, step.at(i, step.n))

            dve.wait_ge(stored.sem, stored.at(i, 0))
            if first:
                norm.on_vector(nc, dve, c, i, lambda j: tile_of(c.x, i, j), lambda j: src[:, j, :], step).then_inc(src_ready.sem, src_ready.one())
            else:
                nc.vector.tensor_copy(src[:, :, :], tiles_of(c.y, i)).then_inc(src_ready.sem, src_ready.one())
            at_use = 1
            seen = {}
            for what, j in order():
                seen[what, j] = at_use
                at_use += 3 if what == "qkv" else 2
            for j in range(NT):
                for side in range(2):
                    dve.wait_ge(w_emptied.sem, w_emptied.at(i, seen["qkv", j] + side + 1))
                    nc.vector.tensor_reduce(inv[:, j % 2, side * heads:(side + 1) * heads], square[:, side, :, :], AX.X, ALU.add).then_inc(summed.sem, summed.one())
                dve.wait_ge(summed.sem, summed.at(i, 2 * (j + 1)))
                nc.vector.tensor_scalar(inv[:, j % 2, :], inv[:, j % 2, :], 1e-24, None, ALU.max).then_inc(floored.sem, floored.one())
                dve.wait_ge(sines_done.sem, sines_done.at(i, j + 1))
                cos = cosines[:, j, :, :].unsqueeze(2).to_broadcast([P, 2, heads, hd])
                r = raw[:, j % 2, :, :, :]
                t = turned[:, j % 2, :, :, :]
                then(nc.vector.tensor_tensor(r, r, cos, ALU.mult))
                then(nc.vector.tensor_tensor(t, t, r, ALU.add))
                t = t.rearrange("p s h d -> p (s h) d")
                nc.vector.tensor_tensor(t, t, inv[:, j % 2, :].unsqueeze(2).to_broadcast([P, 2 * heads, hd]), ALU.mult).then_inc(rotated.sem, rotated.one())
            for n in range(units):
                q, h = n // heads, n % heads
                lo, hi = keys_of(q)
                dve.wait_ge(scored_a.sem, scored_a.at(i, n + 1))
                nc.vector.tensor_reduce(negmax[:, q, h:h + 1], sbank[n % 2][:, 0:hi - lo], AX.X, ALU.max, negate=True).then_inc(maxed.sem, maxed.one())
            dve.wait_ge(w_emptied.sem, w_emptied.at(i, at_use + 1))
            nc.vector.tensor_copy(mT[0:heads, :], mrow[:, :]).then_inc(m_copied.sem, m_copied.one())
            n = m_copied.n
            dve.wait_ge(m_copied.sem, m_copied.at(i, n))
            nc.vector.tensor_tensor(mT[32:32 + heads, :], mrow[:, :], mT[0:heads, :].bitcast(F32), ALU.subtract).then_inc(m_copied.sem, m_copied.one())
            for q in range(NT):
                dve.wait_ge(tile_done.sem, tile_done.at(i, q + 1))
                for b in range(2):
                    o = obank[q % 2][b][:, 0:4 * E].rearrange("p (h e) -> p h e", e=E)
                    ins = nc.vector.reciprocal(rden[:, q % 2, 4 * b:4 * b + 4], o[:, :, hd])
                then(ins)
                for b in range(2):
                    o = obank[q % 2][b][:, 0:4 * E].rearrange("p (h e) -> p h e", e=E)
                    dst = ctxt[:, q, b * 4 * hd:(b + 1) * 4 * hd].rearrange("p (h e) -> p h e", e=hd)
                    ins = nc.vector.tensor_tensor(dst, o[:, :, 0:hd], rden[:, q % 2, 4 * b:4 * b + 4].unsqueeze(2).to_broadcast([P, 4, hd]), ALU.mult)
                ins.then_inc(o_taken.sem, o_taken.one())
            dve.wait_ge(w_emptied.sem, w_emptied.at(i, W_USES))
            nc.vector.tensor_tensor(tiles_of(c.y, i), stepo[:, :, :], src[:, :, :], ALU.add).then_inc(stored.sem, stored.one())
            assert step.n == step.per, step.n
            turn_done(maxed, m_copied, o_taken, rotated, floored)
    ph.close()



def linear_attention_phase(nc, c, name, w):
    heads, hd = 16, 8
    F = D + heads
    W_USES = 4
    ph = Phase(nc, name)
    S = ph.flag
    src = ph.sb("src", [P, NT, D])
    uT, qT = ph.sb("uT", [P, T]), ph.sb("qT", [P, T])
    ktok = ph.sb("ktok", [P, NT, D])
    vtok = ph.sb("vtok", [P, NT, D + 1])
    kv = ph.sb("kv", [P, F])
    kv_sum = ph.sb("kv_sum", [P, 1])
    den = ph.sb("den", [P, NT, heads])
    acc, tmp = ph.sb("acc", [P, NT, D]), ph.sb("tmp", [P, NT, D])
    wbank = (c.bank[0], c.bank[1])
    kvbank, obank = c.bank[2], (c.bank[3], c.bank[4])
    src_ready = S("src_ready")
    w_filled, w_emptied = S("w_filled", W_USES), S("w_emptied", W_USES)
    kv_summed, kv_ready = S("kv_summed"), S("kv_ready", 2)
    context, o_taken = S("context"), S("o_taken")
    ready = S("ready", 0)
    step = S("dve_step", 9)
    norm = Norm(ph, 3)
    block = ph.block()

    @block.sync
    def _(sp):
        load_next(sp, c)

    @block.tensor
    def _(pe):
        wait_weights(pe, c, w)
        pe.wait_ge(ready.sem, 1)
        with turns(pe, B) as i:
            n = [0]

            def fill(emit):
                pe.wait_ge(w_emptied.sem, w_emptied.at(i, max(n[0] - 1, 0)))
                emit(wbank[n[0] % 2]).then_inc(w_filled.sem, w_filled.one())
                n[0] += 1

            def turn(bank):
                for j in range(NT):
                    ins = nc.tensor.transpose(bank[:, j * P:(j + 1) * P], src[:, j, :], c.ident[:, :])
                return ins

            def tokens(weights, b):
                def emit(bank):
                    for j in range(NT):
                        dst = bank[:, j * P:(j + 1) * P]
                        nc.tensor.matmul(dst, uT[:, j * P:(j + 1) * P], weights, start=True, stop=False)
                        ins = nc.tensor.matmul(dst, c.ones[0:1, :], b, start=False, stop=True)
                    return ins
                return emit

            pe.wait_ge(src_ready.sem, src_ready.at(i, 1))
            fill(turn)
            pe.wait_ge(w_emptied.sem, w_emptied.at(i, 1))
            fill(tokens(w["wk"], w["bk_b"]))
            fill(tokens(w["wv"], w["bv"]))
            fill(lambda bank: nc.tensor.matmul(bank[:, :], w["wq"], uT[:, :], start=True, stop=True))
            pe.wait_ge(w_emptied.sem, w_emptied.at(i, 3))
            pe.wait_ge(kv_ready.sem, kv_ready.at(i, 0))
            for j in range(NT):
                ins = nc.tensor.matmul(kvbank[:, 0:D + 1], ktok[:, j, :], vtok[:, j, :], start=j == 0, stop=j == NT - 1)
            ins.then_inc(kv_summed.sem, kv_summed.one())
            pe.wait_ge(kv_ready.sem, kv_ready.at(i, 2))
            pe.wait_ge(w_emptied.sem, w_emptied.at(i, 4))
            pe.wait_ge(o_taken.sem, o_taken.at(i, 0))
            for j in range(NT):
                ins = nc.tensor.matmul(obank[j // 2][:, j % 2 * F:(j % 2 + 1) * F], qT[:, j * P:(j + 1) * P], kv[:, :], start=True, stop=True)
            ins.then_inc(context.sem, context.one())

    @block.scalar
    def _(act):
        wait_weights(act, c, w)
        with turns(act, B) as i:
            n = [0]

            def empty(emit):
                act.wait_ge(w_filled.sem, w_filled.at(i, n[0] + 1))
                emit(wbank[n[0] % 2]).then_inc(w_emptied.sem, w_emptied.one())
                n[0] += 1
            empty(lambda bank: nc.scalar.copy(uT[:, :], bank[:, :]))
            empty(lambda bank: nc.scalar.activation(ktok[:, :, :], bank[:, :].rearrange("p (j d) -> p j d", j=NT), ACT.Relu))
            empty(lambda bank: nc.scalar.copy(vtok[:, :, 0:D], bank[:, :].rearrange("p (j d) -> p j d", j=NT)))
            empty(lambda bank: nc.scalar.activation(qT[:, :], bank[:, :], ACT.Relu, bias=w["bq"]))

    @block.gpsimd
    def _(pool):
        with turns(pool, B) as i:
            for _ in range(3):
                norm.on_gpsimd(nc, pool, c, i)

    @block.vector
    def _(dve):
        wait_weights(dve, c, w)
        nc.vector.memset(vtok[:, :, D:D + 1], 1.0).then_inc(ready.sem, ready.one())
        with turns(dve, B) as i:
            def then(ins):
                ins.then_inc(step.sem, step.one())
                dve.wait_ge(step.sem, step.at(i, step.n))

            dve.wait_ge(w_filled.sem, w_filled.at(i, 0))
            norm.on_vector(nc, dve, c, i, lambda j: tile_of(c.x, i, j), lambda j: src[:, j, :], step).then_inc(src_ready.sem, src_ready.one())
            dve.wait_ge(kv_summed.sem, kv_summed.at(i, 1))
            dve.wait_ge(context.sem, context.at(i, 0))
            nc.vector.tensor_tensor(kv[:, 0:D], kvbank[:, 0:D], w["same_head"], ALU.mult).then_inc(kv_ready.sem, kv_ready.one())
            then(nc.vector.tensor_copy(kv_sum[:, :], kvbank[:, D:D + 1]))
            nc.vector.tensor_scalar(kv[:, D:F], w["head_of"], kv_sum[:, 0:1], None, ALU.mult).then_inc(kv_ready.sem, kv_ready.one())
            dve.wait_ge(context.sem, context.at(i, 1))
            for b in range(2):
                o = obank[b][:, 0:2 * F].rearrange("p (j f) -> p j f", j=2)
                ins = nc.vector.tensor_scalar(den[:, 2 * b:2 * b + 2, :], o[:, :, D:F], 1e-6, None, ALU.max)
            then(ins)
            then(nc.vector.reciprocal(den[:, :, :], den[:, :, :]))
            for b in range(2):
                o = obank[b][:, 0:2 * F].rearrange("p (j f) -> p j f", j=2)[:, :, 0:D].rearrange("p j (h e) -> p j h e", h=heads)
                ins = nc.vector.tensor_tensor(acc[:, 2 * b:2 * b + 2, :].rearrange("p j (h e) -> p j h e", h=heads), o,
                                              den[:, 2 * b:2 * b + 2, :].unsqueeze(3).to_broadcast([P, 2, heads, hd]), ALU.mult)
            ins.then_inc(o_taken.sem, o_taken.one())
            dve.wait_ge(o_taken.sem, o_taken.at(i, 1))
            then(nc.vector.tensor_tensor(acc[:, :, :], acc[:, :, :], src[:, :, :], ALU.add))
            then(norm.on_vector(nc, dve, c, i, lambda j: acc[:, j, :], lambda j: tmp[:, j, :], step))
            then(nc.vector.tensor_tensor(tmp[:, :, :], tmp[:, :, :], wide(w["gamma"]), ALU.mult))
            then(nc.vector.tensor_tensor(acc[:, :, :], tmp[:, :, :], wide(w["beta"]), ALU.add))
            then(norm.on_vector(nc, dve, c, i, lambda j: acc[:, j, :], lambda j: tmp[:, j, :], step))
            then(nc.vector.tensor_tensor(tiles_of(c.x, i), tiles_of(c.x, i), tmp[:, :, :], ALU.add))
            assert step.n == step.per, step.n
    ph.close()


def reorder_phase(nc, c, name, by_position):
    ph = Phase(nc, name)
    written, read = ph.flag("written", 0), ph.flag("read", 0)
    block = ph.block()
    natural = c.scratch.rearrange("b (j p) d -> p (b j) d", p=P)

    @block.sync
    def _(sp):
        parts = [(c.x[:, k:k + 2 * NT, :], natural[:, k:k + 2 * NT, :]) for k in range(0, TILES, 2 * NT)]
        grouped = [(c.x[b::B, 0:TILES, :], c.scratch[b].rearrange("(g t) d -> t g d", t=P // B)) for b in range(B)]
        first, then = (parts, grouped) if by_position else (grouped, parts)
        for tile, dram in first:
            sp.dma_start(dram, tile).then_inc(written.sem, 16)
        sp.wait_ge(written.sem, 16 * len(first))
        for tile, dram in then:
            sp.dma_start(tile, dram).then_inc(read.sem, 16)
        sp.wait_ge(read.sem, 16 * len(then))
    ph.close()



class Pack:

    def __init__(self):
        self.names, self.cols, self.host = {}, 0, []

    def add(self, name, n, lay):
        self.names[name] = (self.cols, n)
        self.cols += n
        self.host.append((n, lay))


def rows_to(a, n=P):
    a = np.asarray(a)
    if a.ndim == 1:
        a = a[None, :]
    out = np.zeros((n, a.shape[1]), a.dtype)
    out[:a.shape[0]] = a
    return out


def blocks(a):
    a = np.asarray(a)
    k = a.shape[0] // P
    return a.reshape(k, P, -1).transpose(1, 0, 2).reshape(P, -1)


def column(v):
    return np.asarray(v).reshape(-1, P).T


def stack_index(heads):
    hd = D // heads
    r = np.arange(NQ * D)
    return r // (NQ * hd) * hd + r % hd


def stack_masks(heads):
    part = np.arange(P) % (NQ * D // heads) // (D // heads)
    qlow, klow = part // 2, part % 2
    out = np.stack([1 - 2 * qlow, qlow, 1 - 2 * klow, klow], 1)
    return out.astype(np.float32)


def attention_pack(heads, scale, wq, wk, wv, bq=None, bk=None, bv=None):
    hd = D // heads
    pk = Pack()
    idx = stack_index(heads)
    pk.add("qk", 2 * NQ * P, lambda a: np.concatenate([wq(a)[:, idx], wk(a)[:, idx]], 1))
    pk.add("v", P, wv)
    pk.add("masks", 4, lambda a: stack_masks(heads))
    pk.add("maskq_scaled", 1, lambda a: stack_masks(heads)[:, 1:2] * np.float32(scale))
    if bq is not None:
        pk.add("bqk", 2 * NQ, lambda a: np.concatenate([column(bq(a)[idx]), column(bk(a)[idx])], 1))
        pk.add("bv", P, lambda a: rows_to(bv(a)))
    return pk


def views(pk, region, need):
    w = {n: region[:, o:o + m] for n, (o, m) in pk.names.items()}
    w["need"] = need
    for n in ("mod", "am", "bd"):
        if n in pk.names:
            w[n] = (lambda o, rows: lambda g: region[0:rows, o + g * P:o + (g + 1) * P])(pk.names[n][0], 16 if n == "am" else P)
    if "cons" in w:
        w["cons"] = w["cons"][0:16, :]
    if "qk" in w:
        o = pk.names["qk"][0]
        w["qk"] = lambda g: region[:, o + g * P:o + (g + 1) * P]
        m = pk.names["masks"][0]
        w["maskq"] = (region[:, m:m + 1], region[:, m + 1:m + 2])
        w["maskk"] = (region[:, m + 2:m + 3], region[:, m + 3:m + 4])
    for n in list(w):
        if n == "bv" or n.endswith("_b"):
            w[n] = w[n][0:1, :]
    return w


def wait_weights(eng, c, w):
    eng.wait_ge(c.loaded[w["need"]], 16)


CONSTS = Pack()
CONSTS.add("ident", P, lambda a: np.eye(P, dtype=np.float32))
CONSTS.add("later_keys", P, lambda a: np.triu(np.full((P, P), MASKED, np.float32), 1))
CONSTS.add("earlier_queries", P, lambda a: np.tril(np.full((P, P), MASKED, np.float32), -1))


def pick_rows():
    out = np.zeros((P, 8, P), np.float32)
    for h in range(8):
        out[h, h] = out[32 + h, h] = 1
    return out.reshape(P, -1)


CONSTS.add("other_groups", P, lambda a: np.where(np.arange(P)[:, None] // B == np.arange(P)[None, :] // B, 0, MASKED).astype(np.float32))
_q, _k = np.arange(P)[:, None], np.arange(P + 64)[None, :]
CONSTS.add("far_keys", P + 64, lambda a: np.where((_k >= _q) & (_k <= _q + 64), 0, MASKED).astype(np.float32))
CONSTS.add("far_queries", P + 64, lambda a: np.where((_k >= _q) & (_k <= _q + 64), 0, MASKED).astype(np.float32))
CONSTS.add("down8", 8, lambda a: np.tile(np.arange(8, 0, -1, dtype=np.float32), (P, 1)))
CONSTS.add("shift", 2 * P, lambda a: np.concatenate([np.eye(P, k=1, dtype=np.float32), np.eye(P, k=1 - P, dtype=np.float32)], 1))
CONSTS.add("pick", 8 * P, lambda a: pick_rows())


def setup_phase(nc, c, consts, x, pk0, w0):
    ph = Phase(nc, "setup")
    raw = ph.sb("raw", [P, CONSTS.cols])
    came, cast = ph.flag("came", 0), ph.flag("cast", 0)
    block = ph.block()

    def part(n):
        o, m = CONSTS.names[n]
        return raw[:, o:o + m]

    @block.sync
    def _(sp):
        sp.dma_start(raw[:, :], consts).then_inc(came.sem, 16)
        for b in range(0, TILES, NT * 2):
            sp.dma_start(c.x[:, b:b + NT * 2, :], x[:, b:b + NT * 2, :]).then_inc(came.sem, 16)
        load_weights(sp, c, pk0, w0)
        sp.wait_ge(came.sem, 80)

    @block.vector
    def _(dve):
        nc.vector.memset(c.ones[:, :], 1.0)
        nc.vector.memset(c.x[:, TILES:, :], 0.0)
        nc.vector.memset(c.ctx[:, TILES:, :], 0.0)
        nc.vector.memset(c.y[:, TILES:, :], 0.0)
        nc.vector.memset(c.minus_half[:, :], -0.5)
        nc.vector.memset(c.eps[:, :], EPS)
        dve.wait_ge(came.sem, 80)
        nc.vector.tensor_copy(c.ident[:, :], part("ident"))
        nc.vector.tensor_copy(c.ident_bf[:, :], part("ident"))
        nc.vector.tensor_copy(c.later_keys[:, :], part("later_keys"))
        nc.vector.tensor_copy(c.earlier_queries[:, :], part("earlier_queries"))
        nc.vector.tensor_copy(c.other_groups[:, :], part("other_groups"))
        nc.vector.memset(c.minus_half16[:, :], -0.5)
        nc.vector.tensor_copy(c.far_keys[:, :], part("far_keys"))
        nc.vector.tensor_copy(c.far_queries[:, :], part("far_queries"))
        nc.vector.tensor_copy(c.down8[:, :], part("down8"))
        nc.vector.tensor_copy(c.shift[:, :, :], part("shift").rearrange("p (a n) -> p a n", a=2))
        nc.vector.tensor_copy(c.pick[:, :, :], part("pick").rearrange("p (h n) -> p h n", h=8)).then_inc(cast.sem, 1)
        dve.wait_ge(cast.sem, 1)
    ph.close()


def load_weights(sp, c, pk, src):
    n_load = c.region_turn
    n = n_load % 2
    c.region_turn += 1
    sp.dma_start(c.region[n][:, 0:pk.cols], src).then_inc(c.loaded[n_load], 16)


def load_next(sp, c):
    if c.next is not None:
        load_weights(sp, c, *c.next)


def store_phase(nc, c, out):
    ph = Phase(nc, "store")
    stored = ph.flag("stored", 0)
    block = ph.block()

    @block.sync
    def _(sp):
        for b in range(0, TILES, NT * 2):
            sp.dma_start(out[:, b:b + NT * 2, :], c.x[:, b:b + NT * 2, :]).then_inc(stored.sem, 16)
        sp.wait_ge(stored.sem, 64)
    ph.close()


def rotary_tables():
    hd, window = 64, 64
    half = np.arange(0, hd, 2, dtype=np.float32)
    t = np.arange(T, dtype=np.float32)
    freqs = t[:, None] * (np.float32(1) / np.float32(10000) ** (half / np.float32(hd)))[None]
    base = (half + np.float32(0.4 * hd)) / np.float32(1.4 * hd)
    power = (t - T // 2) / np.float32(window // 2)
    scale = base[None, :] ** power[:, None]
    out = []
    for f, sign in ((np.cos(freqs), 1.0), (np.sin(freqs), -1.0)):
        q = np.concatenate([sign * f * scale, f * scale], 1) * 8.0
        k = np.concatenate([sign * f / scale, f / scale], 1)
        tab = np.stack([q, k], 1).astype(np.float32)
        out.append(tab.reshape(NT, P, 2, hd).transpose(1, 0, 2, 3).reshape(P, -1))
    return out


def phase_list():
    T_ = lambda n: (lambda a: np.asarray(a[n]).T)
    V_ = lambda n: (lambda a: np.asarray(a[n]))
    out = []
    f32 = lambda v: float(np.float32(v))
    W4 = lambda k: (lambda a: np.asarray(a["L0_attn_W_qkvf"])[k * D:(k + 1) * D].T)

    def conv_blocks(a):
        conv = np.asarray(a["L0_attn_W_conv"])
        o = np.zeros((16, 8, 4, 16, 8), np.float32)
        for h in range(16):
            o[h, :, :, h, :] = conv.transpose(0, 2, 1)
        return o.reshape(D, 4 * D)
    sc0 = f32(8 ** -0.5)
    pk = attention_pack(16, sc0, W4(0), W4(1), W4(2))
    pk.add("q", P, W4(0))
    pk.add("wf", P, lambda a: np.asarray(a["L0_attn_W_qkvf"])[3 * D:])
    pk.add("wkT", P, W4(1))
    pk.add("wvT", P, W4(2))
    pk.add("bd", 4 * P, conv_blocks)
    pk.add("gain", 1, lambda a: column(a["L0_attn_ln1_g"]))
    pk.add("shift", 1, lambda a: column(a["L0_attn_ln1_b"]))
    pk.add("proj", P, T_("L0_attn_W_proj"))
    out.append(("L0a", pk, lambda nc, c, w: attention_phase(nc, c, "l0a", w, 16, sc0, causal=True, affine=True, future=True, out_steps=("proj",), finish="y")))
    pk = Pack()
    pk.add("ff1", 4 * P, V_("L0_attn_W_ff1"))
    pk.add("ff2", 4 * P, lambda a: blocks(a["L0_attn_W_ff2"]))
    pk.add("gain", 1, lambda a: column(a["L0_attn_ln2_g"]))
    pk.add("shift", 1, lambda a: column(a["L0_attn_ln2_b"]))

    def l0g(nc, c, w):
        blk = lambda t, k: t[:, k * P:(k + 1) * P]
        L = [Layer(1, 4, lambda k, m: blk(w["ff1"], m), ACT.Gelu)]
        mlp_phase(nc, c, "l0g", w, lambda e: L, lambda e: (4, lambda k: blk(w["ff2"], k)), source="y", affine=True, add_y=True)
    out.append(("L0g", pk, l0g))
    for d in range(2):
        G = lambda n, d=d: (lambda a: np.asarray(a["L0_ffn_" + n])[d])
        pk = Pack()
        pk.add("qkv", 1536, G("wqkv"))
        pk.add("wo", 4 * P, (lambda g: lambda a: blocks(g(a)))(G("wo")))
        pk.add("cosines", 4 * P, lambda a: rotary_tables()[0])
        pk.add("sines", 4 * P, lambda a: rotary_tables()[1])
        pk.add("gains", P, (lambda d: lambda a: np.broadcast_to(np.concatenate([a["L0_ffn_q_scale"][d], a["L0_ffn_k_scale"][d]]), (P, P)))(d))
        pk.add("gains_turned", P, (lambda d: lambda a: np.broadcast_to(np.concatenate([np.roll(a["L0_ffn_q_scale"][d], 32), np.roll(a["L0_ffn_k_scale"][d], 32)]), (P, P)))(d))
        out.append((f"L0w{d}", pk, (lambda d: lambda nc, c, w: local_attention_phase(nc, c, f"l0w{d}", w, first=d == 0))(d)))
        pk = Pack()
        HID, HB = 341, 3

        def padded(v, n=HB * P):
            return np.concatenate([v, np.zeros(v.shape[:-1] + (n - v.shape[-1],), v.dtype)], -1)
        pk.add("wa", HB * P, (lambda g: lambda a: padded(g(a)[:, :HID]))(G("w1")))
        pk.add("wg", HB * P, (lambda g: lambda a: padded(g(a)[:, HID:]))(G("w1")))
        pk.add("ba", HB, (lambda g: lambda a: column(padded(g(a)[:HID])))(G("b1")))
        pk.add("bg", HB, (lambda g: lambda a: column(padded(g(a)[HID:])))(G("b1")))
        pk.add("w2", HB * P, (lambda g: lambda a: blocks(padded(g(a).T).T))(G("w2")))
        pk.add("final_b", P, (lambda g: lambda a: rows_to(g(a)))(G("b2")))
        pk.add("gain", 1, (lambda g: lambda a: column(g(a)))(G("ln_g")))
        pk.add("shift", 1, (lambda g: lambda a: column(g(a)))(G("ln_b")))

        def l0h(nc, c, w, d=d):
            blk = lambda t, k: t[:, k * P:(k + 1) * P]
            L = [Layer(1, 3, lambda k, m: blk(w["wg"], m), ACT.Gelu, bias=lambda m: w["bg"][:, m:m + 1],
                       V=lambda k, m: blk(w["wa"], m), v_op=ALU.add, v_arg=lambda m: w["ba"][:, m:m + 1])]
            mlp_phase(nc, c, f"l0h{d}", w, lambda e: L, lambda e: (3, lambda k: blk(w["w2"], k)), source="y", affine=True,
                      shifted=True, add_y=True, finish="residual_norm" if d else "y")
        out.append((f"L0h{d}", pk, l0h))
    fl = lambda n: (lambda a: np.asarray(a[n]).reshape(D, D).T)
    fb = lambda n: (lambda a: np.asarray(a[n]).reshape(D))
    sc = float(np.float32(1 / np.sqrt(8.0)))
    pk = attention_pack(16, sc, fl("L1_attn_Wq"), fl("L1_attn_Wk"), fl("L1_attn_Wv"), fb("L1_attn_bq"), fb("L1_attn_bk"), fb("L1_attn_bv"))
    out.append(("L1a", pk, lambda nc, c, w: attention_phase(nc, c, "l1a", w, 16, sc, causal=True, bias=True)))
    pk = Pack()
    for n in ("w1", "w2"):
        pk.add(n, 4 * P, T_(f"L1_ffn_{n}_w"))
        pk.add(n + "s", 4, (lambda n: lambda a: column(a[f"L1_ffn_{n}_s"]))(n))
    for n in ("h1", "h2"):
        pk.add(n, 16 * P, (lambda n: lambda a: blocks(np.asarray(a[f"L1_ffn_{n}_w"]).T))(n))
        pk.add(n + "s", 4, (lambda n: lambda a: column(a[f"L1_ffn_{n}_s"]))(n))
    pk.add("w3", 4 * P, lambda a: blocks(np.asarray(a["L1_ffn_w3_w"]).T))
    pk.add("out_scale", P, lambda a: np.broadcast_to(np.asarray(a["L1_ffn_w3_s"]), (P, P)))

    def l1f(nc, c, w):
        m1 = lambda t: (lambda k, m: t[:, (k * 4 + m) * P:(k * 4 + m + 1) * P])
        s1 = lambda t: (lambda m: t[:, m:m + 1])
        L = [Layer(1, 4, m1(w["w1"]), ACT.Silu, scale=s1(w["w1s"]), V=m1(w["w2"]), v_arg=s1(w["w2s"])),
             Layer(4, 4, m1(w["h1"]), ACT.Gelu, scale=s1(w["h1s"])),
             Layer(4, 4, m1(w["h2"]), ACT.Gelu, scale=s1(w["h2s"]))]
        mlp_phase(nc, c, "l1f", w, lambda e: L, lambda e: (4, lambda k: w["w3"][:, k * P:(k + 1) * P]), out_scale=True)
    out.append(("L1f", pk, l1f))
    h16 = stack_index(16) // 8
    col = lambda n, k: (lambda a: np.asarray(a[n])[:, k * D:(k + 1) * D])
    row = lambda n, k: (lambda a: np.asarray(a[n])[k * D:(k + 1) * D])
    pk = attention_pack(16, sc, V_("L2_attn_Wq"), V_("L2_attn_Wk"), V_("L2_attn_Wv"), V_("L2_attn_bq"), V_("L2_attn_bk"), V_("L2_attn_bv"))
    pk.add("mod", 4 * P, lambda a: np.asarray(a["L2_attn_cg_W"])[:, h16])
    pk.add("am", 4 * P, lambda a: rows_to(np.asarray(a["L2_attn_am_W"])[:, h16]))
    pk.add("cons", 1, lambda a: rows_to(np.asarray(a["L2_attn_cons_vec"])[:, None]))
    pk.add("cg_am_bias", 8, lambda a: np.concatenate([column(np.asarray(a["L2_attn_cg_b"])[h16]), column(np.asarray(a["L2_attn_am_b"])[h16])], 1))
    out.append(("L2m", pk, lambda nc, c, w: attention_phase(nc, c, "l2m", w, 16, sc, bias=True, modulated=True, finish="context")))
    s32 = f32(1 / np.sqrt(32.0))
    pk = attention_pack(4, s32, col("L2_attn_ca_Win", 0), col("L2_attn_ca_Win", 1), col("L2_attn_ca_Win", 2), row("L2_attn_ca_bin", 0), row("L2_attn_ca_bin", 1), row("L2_attn_ca_bin", 2))
    pk.add("causal_out", P, V_("L2_attn_ca_Wout"))
    pk.add("causal_out_b", P, lambda a: rows_to(a["L2_attn_ca_bout"]))
    out.append(("L2c", pk, lambda nc, c, w: attention_phase(nc, c, "l2c", w | {"mix": (1.0 - 0.7, 0.7)}, 4, s32, bias=True, out_steps=("causal_out",), finish="y")))
    meta = (0.9 - 0.8) / 0.2 * 0.3
    pk = attention_pack(4, s32, col("L2_attn_mc_Win", 0), col("L2_attn_mc_Win", 1), col("L2_attn_mc_Win", 2), row("L2_attn_mc_bin", 0), row("L2_attn_mc_bin", 1), row("L2_attn_mc_bin", 2))
    pk.add("meta_out", P, V_("L2_attn_mc_Wout"))
    pk.add("meta_out_b", P, lambda a: rows_to(a["L2_attn_mc_bout"]))
    pk.add("out", P, V_("L2_attn_Wo"))
    pk.add("out_b", P, lambda a: rows_to(a["L2_attn_bo"]))
    out.append(("L2t", pk, lambda nc, c, w: attention_phase(nc, c, "l2t", w | {"mix": (1.0 - meta, meta)}, 4, s32, bias=True, source="given", out_steps=("meta_out", "out"))))
    pk = Pack()
    out.append(("R1", None, lambda nc, c, w: reorder_phase(nc, c, "to_positions", True)))
    wq = lambda k: (lambda a: np.asarray(a["L2_ffn_Wqkv"])[k * D:(k + 1) * D].T)
    bq = lambda k: (lambda a: np.asarray(a["L2_ffn_bqkv"])[k * D:(k + 1) * D])
    pk = attention_pack(4, s32, wq(0), wq(1), wq(2), bq(0), bq(1), bq(2))
    pk.add("mixed", P, T_("L2_ffn_Wo"))
    pk.add("mixed_b", P, lambda a: rows_to(a["L2_ffn_bo"]))
    bcast = lambda n: (lambda a: np.broadcast_to(np.asarray(a[n]), (P, P)))
    pk.add("g1", P, bcast("L2_ffn_g1"))
    pk.add("be1", P, bcast("L2_ffn_be1"))
    out.append(("L2p", pk, lambda nc, c, w: attention_phase(nc, c, "l2p", w, 4, s32, bias=True, grouped=True, out_steps=("mixed",), finish="y")))
    pk = Pack()
    pk.add("W1", 32 * P, lambda a: np.asarray(a["L2_ffn_W1"]).transpose(1, 0, 2).reshape(P, -1))
    pk.add("W2", 32 * P, lambda a: np.asarray(a["L2_ffn_W2"]).reshape(32, P, D).transpose(1, 0, 2).reshape(P, -1))
    pk.add("b1", 32, lambda a: np.asarray(a["L2_ffn_b1"]).reshape(32, P).T)
    pk.add("gate", 8, T_("L2_ffn_Wg"))
    pk.add("expert_bias", P, lambda a: rows_to(a["L2_ffn_b2"]))
    pk.add("g2", P, bcast("L2_ffn_g2"))
    pk.add("be2", P, bcast("L2_ffn_be2"))

    def l2e(nc, c, w):
        w = w | {"expert_bias": w["expert_bias"][0:8, :]}
        blk = lambda t, k: t[:, k * P:(k + 1) * P]
        L = lambda e: [Layer(1, 4, lambda k, m: blk(w["W1"], 4 * e + m), ACT.Relu, bias=lambda m: w["b1"][:, 4 * e + m:4 * e + m + 1])]
        mlp_phase(nc, c, "l2e", w, L, lambda e: (4, lambda k: blk(w["W2"], 4 * e + k)), experts=8, source="y", gate="top1", tail_gain=True)
    out.append(("L2e", pk, l2e))
    out.append(("R2", None, lambda nc, c, w: reorder_phase(nc, c, "to_batches", False)))
    pk = Pack()
    pk.add("wq", P, T_("L3_attn_Wq"))
    pk.add("wk", P, T_("L3_attn_Wk"))
    pk.add("wv", P, T_("L3_attn_Wv"))
    pk.add("bq", 1, lambda a: column(a["L3_attn_bq"]))
    pk.add("bk_b", P, lambda a: rows_to(a["L3_attn_bk"]))
    pk.add("bv", P, lambda a: rows_to(a["L3_attn_bv"]))
    pk.add("gamma", P, bcast("L3_attn_gamma"))
    pk.add("beta", P, bcast("L3_attn_beta"))
    pk.add("same_head", P, lambda a: np.kron(np.eye(16), np.ones((8, 8))).astype(np.float32))
    pk.add("head_of", 16, lambda a: np.kron(np.eye(16), np.ones((8, 1))).astype(np.float32))
    out.append(("L3a", pk, lambda nc, c, w: linear_attention_phase(nc, c, "l3a", w)))
    pk = Pack()
    pk.add("Wg", P // 16, V_("L3_ffn_Wg"))
    for n in ("W11", "W12"):
        pk.add(n, 16 * P, (lambda n: lambda a: np.asarray(a[f"L3_ffn_{n}"]).transpose(1, 0, 2).reshape(P, -1))(n))
    pk.add("W2", 16 * P, lambda a: np.asarray(a["L3_ffn_W2"]).reshape(16, P, D).transpose(1, 0, 2).reshape(P, -1))

    def l3e(nc, c, w):
        w = w | {"gate": w["Wg"]}
        blk = lambda t, k: t[:, k * P:(k + 1) * P]
        L = lambda e: [Layer(1, 2, lambda k, m: blk(w["W11"], 2 * e + m), ACT.Silu, V=lambda k, m: blk(w["W12"], 2 * e + m))]
        mlp_phase(nc, c, "l3e", w, L, lambda e: (2, lambda k: blk(w["W2"], 2 * e + k)), experts=8, gate="top2")
    out.append(("L3e", pk, l3e))
    return out


def program(nc, consts, x, packs, out, phases):
    c = Chip()
    with ExitStack() as ctx:
        sb = lambda n, s, d=F32: ctx.enter_context(nc.sbuf_tensor(n, s, d))
        c.x = sb("x", [P, TILES + NT, D])
        c.y = sb("y", [P, TILES + NT, D])
        c.ctx = sb("ctx", [P, TILES + NT, D])
        c.ident = sb("ident", [P, P])
        c.ident_bf = sb("ident_bf", [P, P], BF16)
        c.later_keys = sb("later_keys", [P, P], BF16)
        c.earlier_queries = sb("earlier_queries", [P, P], BF16)
        c.other_groups = sb("other_groups", [P, P], BF16)
        c.far_keys = sb("far_keys", [P, P + 64], BF16)
        c.far_queries = sb("far_queries", [P, P + 64], BF16)
        c.minus_half16 = sb("minus_half16", [P, 16])
        c.down8 = sb("down8", [P, 8])
        c.shift = sb("shift", [P, 2, P])
        c.pick = sb("pick", [P, 8, P], F32R)
        c.ones = sb("ones", [1, P])
        c.minus_half = sb("minus_half", [P, NT])
        c.eps = sb("eps", [P, NT])
        c.bank = [ctx.enter_context(nc.psum_tensor(f"bank{k}", [P, 512], F32)) for k in range(8)]
        c.scratch = nc.dram_tensor("scratch", (B, T, D), F32, kind="Internal").ap()
        loads = [(pk, packs[name]) for name, pk, _ in phases if pk is not None]
        cols = [max([pk.cols for pk, _ in loads[k::2]] + [1]) for k in range(2)]
        tiles = lambda a: a.rearrange("b (j p) d -> p (b j) d", p=P)
        c.loaded = [ctx.enter_context(nc.semaphore(f"weights_loaded{k}")) for k in range(len(loads))]
        c.region_turn = 0
        with nc.sbuf_tensor("weights0", [P, cols[0]], F32) as r0, nc.sbuf_tensor("weights1", [P, cols[1]], F32) as r1:
            c.region = [r0, r1]
            setup_phase(nc, c, consts, tiles(x), *loads[0])
            n = 0
            for name, pk, build in phases:
                if pk is None:
                    build(nc, c, None)
                    continue
                c.next = loads[n + 1] if n + 1 < len(loads) else None
                build(nc, c, views(pk, c.region[n % 2], n))
                n += 1
        store_phase(nc, c, tiles(out))


def lay_out(pk, inputs):
    cols = []
    for n, lay in pk.host:
        a = np.asarray(lay(inputs))
        assert a.shape == (P, n), (a.shape, n)
        cols.append(a)
    return np.ascontiguousarray(np.concatenate(cols, 1))


def kernel(**inputs):
    from concourse import bacc
    from concourse.bass_utils import run_bass_kernel_spmd

    nc = bacc.Bacc("TRN2", target_bir_lowering=False, num_devices=1)
    nc.disable_value_cache = True
    phases = phase_list()
    arrays = {"x_in": np.ascontiguousarray(inputs["L0_attn_x"]), "consts": lay_out(CONSTS, inputs)}
    for name, pk, _ in phases:
        if pk is not None:
            arrays[f"w_{name}"] = lay_out(pk, inputs)
    aps = {n: nc.dram_tensor(n, a.shape, F32, kind="ExternalInput").ap() for n, a in arrays.items()}
    out = nc.dram_tensor("x_out", (B, T, D), F32, kind="ExternalOutput").ap()
    program(nc, aps["consts"], aps["x_in"], {p[0]: aps[f"w_{p[0]}"] for p in phases if p[1] is not None}, out, phases)
    return run_bass_kernel_spmd(nc, [arrays], core_ids=[0]).results[0]["x_out"]
```

```python
from contextlib import ExitStack, contextmanager

import numpy as np

import concourse.bass as bass
from concourse import mybir

F32 = mybir.dt.float32
F32R = mybir.dt.float32r
BF16 = mybir.dt.bfloat16
ALU = mybir.AluOpType
ACT = mybir.ActivationFunctionType
AX = mybir.AxisListType

P = 128
B, T, D = 8, 512, 128
NT = T // P
TILES = B * NT
EPS = 1e-5
MASKED = -1e30
H2 = D // 2
NQ = 4


class Signal:

    def __init__(self, sem, per, before=None):
        self.sem, self.per, self.n, self.before = sem, per, 0, before

    def at(self, turn, n=0):
        if self.before is None:
            return turn.times(self.per) + (n + 1)
        return turn.times(self.per) + (self.before + n + 1) if not turn.ahead else n + 1

    def one(self):
        self.n += 1
        return 1

    def turn_done(self):
        assert self.n == self.per, (self.sem, self.n, self.per)

    def ahead_done(self):
        assert self.before in (None, self.n), (self.sem, self.n, self.before)
        self.n = 0


class Turn:

    def __init__(self, eng, i):
        self.eng, self.i, self.products = eng, i, {1: i}

    def times(self, per):
        if per not in self.products:
            self.products[per] = self.eng.snap(self.i * per)
        return self.products[per]

    def tiles(self, t):
        return t[:, bass.ds(self.times(NT), NT), :]

    def tile(self, t, j):
        return t[:, bass.ds(self.times(NT) + j, 1), :]

    ahead = False

    def next_tiles(self, t):
        return t[:, bass.ds(self.times(NT) + NT, NT), :]

    def next_tile(self, t, j):
        return t[:, bass.ds(self.times(NT) + NT + j, 1), :]


class Ahead:
    ahead = True

    def times(self, per):
        return -per

    def next_tiles(self, t):
        return t[:, 0:NT, :]

    def next_tile(self, t, j):
        return t[:, j:j + 1, :]


@contextmanager
def turns(eng, n):
    with eng.Fori(0, n) as i:
        yield Turn(eng, i)


class Phase:

    def __init__(self, nc, name):
        self.nc, self.name, self.made, self.signals, self.ctx = nc, name, [], [], ExitStack()

    def flag(self, what, per=1, before=None):
        sem = self.nc.alloc_semaphore(f"{self.name}_{what}")
        self.made.append(sem)
        self.signals.append(Signal(sem, per, before))
        return self.signals[-1]

    def sb(self, what, shape, dt=F32):
        return self.ctx.enter_context(self.nc.sbuf_tensor(f"{self.name}_{what}", shape, dt))

    def block(self):
        for s in self.signals:
            if s.per:
                self.nc.sync.sem_inc(s.sem, 1)
        self.nc.all_engine_barrier()
        return self.ctx.enter_context(self.nc.Block())

    def close(self):
        self.ctx.close()
        self.nc.clear_and_free_semaphores(self.made)
        self.nc.all_engine_barrier()


class Chip:
    pass


def tiles_of(t, i):
    return i.tiles(t)


def tile_of(t, i, j):
    return i.tile(t, j)



class Norm:
    def __init__(self, ph, per, before=None):
        self.variance, self.eps_added, self.rstd_ready = (ph.flag(s, per, before) for s in ("variance", "eps_added", "rstd_ready"))
        self.bn = ph.sb("bn", [P, NT, 6])
        self.mv = ph.sb("mv", [P, NT, 2])
        self.veps = ph.sb("veps", [P, NT])
        self.rstd = ph.sb("rstd", [P, NT])

    def on_gpsimd(self, nc, pool, c, i):
        pool.wait_ge(self.variance.sem, self.variance.at(i, self.rstd_ready.n + 1))
        nc.gpsimd.tensor_tensor(self.veps[:, :], self.mv[:, :, 1], c.eps[:, :], ALU.add).then_inc(self.eps_added.sem, self.eps_added.one())
        n = self.eps_added.n
        pool.wait_ge(self.eps_added.sem, self.eps_added.at(i, n))
        nc.gpsimd.tensor_tensor(self.rstd[:, :], self.veps[:, :], c.minus_half[:, :], ALU.pow).then_inc(self.rstd_ready.sem, self.rstd_ready.one())

    def on_vector(self, nc, dve, i, src, dst):
        self.statistics(nc, dve, src)
        return self.scaled(nc, dve, i, src, dst)

    def statistics(self, nc, dve, src):
        for j in range(NT):
            ins = nc.vector.bn_stats(self.bn[:, j, :], src(j))
        dve.drain()
        for j in range(NT):
            ins = nc.vector.bn_aggr(self.mv[:, j, :], self.bn[:, j, :])
        ins.then_inc(self.variance.sem, self.variance.one())

    def scaled(self, nc, dve, i, src, dst):
        n = self.variance.n
        dve.wait_ge(self.rstd_ready.sem, self.rstd_ready.at(i, n))
        for j in range(NT):
            ins = nc.vector.tensor_scalar(dst(j), src(j), self.mv[:, j, 0:1], self.rstd[:, j:j + 1], ALU.subtract, ALU.mult)
        return ins


def wide(row):
    return row.unsqueeze(1).to_broadcast([P, NT, row.shape[-1]])


def turn_done(*signals):
    for s in signals:
        s.turn_done()



def attention_phase(nc, c, name, w, heads, scale, causal=False, bias=False, source=None, affine=False, grouped=False,
                    future=False, modulated=False, out_steps=(), finish="residual_norm"):
    ph = Phase(nc, name)
    hd = D // heads
    rows = NQ * hd
    in_group = P // rows
    G = heads // in_group
    E = hd + 1
    half = heads // 2
    R = half * E
    units = heads * NT
    MG = 4
    mg = heads // MG
    norms_ahead = {None: 1, "given": 0}[source] + affine
    norms = norms_ahead + (finish == "residual_norm") + ("mixed" in out_steps)

    places = {}

    def place(step, k, *what):
        places.setdefault((step, k), []).extend(what)

    for g in range(1, MG):
        place(g * mg - 1, 0, f"max{g}")
    late = mg > 1 and not (affine or modulated)
    next_at = ((1, 0), (1, 2)) if late else ((-1, 0), (0, 0))
    uT_at = (2, 0) if late else (1, 0) if mg > 1 else (0, 2)
    place(*uT_at, "uT")
    if modulated:
        place(2, 0, *(f"mod{g}" for g in range(G)))
    stack_at = [in_group * (g + 1) - (in_group > 1) for g in range(G - 1)]
    for g in range(G - 1):
        place(stack_at[g], 0, f"q{g}")
        place(stack_at[g], 2, f"k{g}")
    place(half, 3, "sums0")
    if future:
        place(13, 0, "fq", "fk0", "fv0")
        place(14, 0, "fk1", "fv1")
        place(14, 2, "fk2", "fv2")
        place(15, 2, "fk3", "fv3")
    place(heads, 0, "v", "sums1", "max_next", f"q{G - 1}", f"k{G - 1}")
    for s in range(len(out_steps)):
        place(heads, 0, f"turned{s}", f"projected{s}")
    W_TURN = [what for at in sorted(places) for what in places[at]]
    W_AHEAD = ["uT"] + [f"mod{g}" for g in range(G)] * modulated + [f"{a}{g}" for g in range(G) for a in "qk"] + ["v"]
    W_AHEAD += (["fq"] + [f"f{a}{f}" for f in range(4) for a in "kv"]) * future + ["max_next"]

    def w_n(i, what):
        return (W_AHEAD if i.ahead else W_TURN).index(what) + 1

    def units_a(h, k):
        if mg == 1 or h > 2:
            return [(h + 1 + mg, k)] if h >= 0 else []
        return {1: [(mg + 1, k)], 2: [(mg + 2 + k // 2, 2 * k % NT), (mg + 2 + k // 2, 2 * k % NT + 1)]}.get(h, [])

    src = ph.sb("src", [P, NT, D])
    uT = ph.sb("uT", [P, T])
    high = ph.sb("high", [P, 2, T], F32R)
    lowpart = ph.sb("lowpart", [P, 2, T])
    qs = ph.sb("qs", [P, G, T], F32R)
    ks = ph.sb("ks", [P, G, T], F32R)
    vx = ph.sb("vx", [P, NT, heads, R + E])
    vx_flat = vx[:, :, :, :].rearrange("p j h m -> p j (h m)")
    sums = ph.sb("sums", [R, 2, T])
    sums_tok = ph.sb("sums_tok", [P, 2, NT, half, E])
    negmax = ph.sb("negmax", [P, NT, heads])
    mrow = ph.sb("mrow", [mg, T])
    mT = ph.sb("mT", [48, 2, T], F32R)
    pT = ph.sb("pT", [P, 2, NT, T])
    rden = ph.sb("rden", [P, 2, NT, half])
    ctxt = ph.sb("ctx", [P, NT, D])
    tmp = ph.sb("tmp", [P, NT, D])
    stepT = uT
    stepo = ph.sb("stepo", [P, NT, D]) if out_steps else None
    if modulated:
        modT = ph.sb("modT", [P, G, T])
        mod_bias = ph.sb("mod_bias", [P, G])
        scaled = lowpart[:, 0, :]
    biases = ph.sb("biases", [P, 4 * G]) if bias else None
    if future:
        qtok = stepo
        kf = c.ctx[:, 0:4 * NT, :].rearrange("p (f j) d -> p f j d", f=4)
        vf = c.ctx[:, 4 * NT:8 * NT, :].rearrange("p (f j) d -> p f j d", f=4)
        afT = kf[:, 0, :, :]
        wkf, wvf = (ph.sb(n, [P, 4, P]) for n in ("wkf", "wvf"))
        fut = ph.sb("fut", [P, 4, NT, heads])
        futmax = ph.sb("futmax", [P, NT, heads])
        pf = ph.sb("pf", [P, 4, NT, heads])
        futden = ph.sb("futden", [P, NT, heads])

    w0, w1 = c.bank[0], c.bank[1]
    wbank = (w0, w1)
    abank = (c.bank[2], c.bank[3])
    bbank = (c.bank[4], c.bank[5])
    obank = (c.bank[6], c.bank[7])

    S = ph.flag
    prepared, mod_added = S("prepared", 0), S("mod_added", 0)
    src_ready = S("src_ready")
    w_filled, w_emptied = S("w_filled", len(W_TURN), len(W_AHEAD)), S("w_emptied", len(W_TURN), len(W_AHEAD))
    parts_ready, stacked = S("parts_ready", G), S("stacked", 2 * G)
    scored_a, maxed = S("scored_a", units), S("maxed", units)
    m_copied = S("m_copied", 2 * MG)
    m_final = S("m_final", MG)
    scored_b, exped = S("scored_b", units), S("exped", units)
    head_done = S("head_done", heads)
    sums_copied = S("sums_copied", 2)
    ctx_ready = S("ctx_ready")
    step_taken = S("step_taken", max(len(out_steps), 1))
    mod_scaled = S("mod_scaled", G)
    norm = Norm(ph, max(norms, 1), norms_ahead)
    then_ahead = affine + 8 * future
    step = S("dve_step", affine + 14 * future + sum({"causal_out": 1, "meta_out": 1, "mixed": 3}.get(s, 0) for s in out_steps)
             + (finish == "residual_norm") * (1 + (not out_steps)) + (finish == "context") + 1 - future, then_ahead)
    fut_asked, fut_exped, fut_used = S("fut_asked"), S("fut_exped"), S("fut_used")

    def keys_of(q):
        return (q * P if grouped else 0), ((q + 1) * P if causal or grouped else T)

    def queries_of(k):
        return (k * P if causal or grouped else 0), ((k + 1) * P if grouped else T)

    masked = causal or grouped
    mask_a, mask_b = (c.other_groups, c.other_groups) if grouped else (c.later_keys, c.earlier_queries)
    block = ph.block()

    @block.sync
    def _(sp):
        load_next(sp, c)

    @block.tensor
    def _(pe):
        wait_weights(pe, c, w)
        if future:
            for f in range(4):
                ins = nc.tensor.matmul(w0[:, f * P:(f + 1) * P], w["bd"](f), w["wf"], start=True, stop=True)
            ins.then_inc(prepared.sem, prepared.one())
            pe.wait_ge(prepared.sem, 2)
            for which, bank in (("wkT", w1), ("wvT", w0)):
                for f in range(4):
                    ins = nc.tensor.matmul(bank[:, f * P:(f + 1) * P], afT[:, f, :], w[which], start=True, stop=True)
            ins.then_inc(prepared.sem, prepared.one())
            pe.wait_ge(prepared.sem, 5)
        if modulated:
            for g in range(G):
                ins = nc.tensor.matmul(w0[:, g:g + 1], w["am"](g), w["cons"], start=True, stop=True)
            ins.then_inc(prepared.sem, prepared.one())

        def fill(i, what, emit):
            n = w_filled.n
            assert w_n(i, what) == n + 1, what
            if n > 0 or not i.ahead:
                pe.wait_ge(w_emptied.sem, w_emptied.at(i, n - 1))
            bank = wbank[(n + (0 if i.ahead else len(W_AHEAD))) % 2]
            emit(bank).then_inc(w_filled.sem, w_filled.one())

        def turn(s):
            def emit(bank):
                for j in range(NT):
                    ins = nc.tensor.transpose(bank[:, j * P:(j + 1) * P], s[:, j, :], c.ident[:, :])
                return ins
            return emit

        def tokens(sT, weights, b=None):
            def emit(bank):
                for j in range(NT):
                    ins = nc.tensor.matmul(bank[:, j * P:(j + 1) * P], sT[:, j * P:(j + 1) * P], weights, start=True, stop=b is None)
                    if b is not None:
                        ins = nc.tensor.matmul(bank[:, j * P:(j + 1) * P], c.ones[0:1, :], b, start=False, stop=True)
                return ins
            return emit

        def features(weights):
            return lambda bank: nc.tensor.matmul(bank[:, :], weights, uT[:, :], start=True, stop=True)

        def prepare(i, what):
            kind, g = what[0], int(what[-1]) if what[-1].isdigit() else 0
            if what == "uT":
                pe.wait_ge(src_ready.sem, src_ready.at(i, 2))
                fill(i, what, turn(src))
                return
            pe.wait_ge(w_emptied.sem, w_emptied.at(i, w_n(i, "uT")))
            if kind == "m":
                fill(i, what, features(w["mod"](g)))
            elif kind in "qk":
                fill(i, what, features(w["qk"](g if kind == "q" else G + g)))
            elif what == "v":
                fill(i, what, tokens(uT, w["v"], w.get("bv")))
            elif what == "fq":
                fill(i, what, tokens(uT, w["q"]))
            else:
                fill(i, what, tokens(uT, (wkf if what[1] == "k" else wvf)[:, g, :]))

        def score_a(i, h, q):
            n = h * NT + q
            h, own = h % heads, 2 * G * (h // heads)
            g, at = h // in_group, (h % in_group) * rows
            if q == 0:
                pe.wait_ge(stacked.sem, stacked.at(i, own + 2 * (g + 1)))
            if not (i.ahead and n < units + 2):
                pe.wait_ge(maxed.sem, maxed.at(i, n - 1))
            lo, hi = keys_of(q)
            bank = abank[n % 2]
            ins = nc.tensor.matmul(bank[:, lo:hi], qs[at:at + rows, g, q * P:(q + 1) * P], ks[at:at + rows, g, lo:hi], start=True, stop=not masked)
            if masked:
                ins = nc.tensor.matmul(bank[:, q * P:hi], c.ident_bf[:, :], mask_a[:, :], start=False, stop=True)
            ins.then_inc(scored_a.sem, scored_a.one())

        def maxima(i, group, what):
            if future:
                pe.wait_ge(m_final.sem, m_final.at(i, group + 1))
            else:
                pe.wait_ge(maxed.sem, maxed.at(i, (group + 1) * mg * NT))

            def emit(bank):
                for q in range(NT):
                    first = group % MG * mg
                    ins = nc.tensor.transpose(bank[0:mg, q * P:(q + 1) * P], negmax[:, q, first:first + mg], c.ident[:, :])
                return ins
            fill(i, what, emit)

        def score_b(i, h, k):
            g, at = h // in_group, (h % in_group) * rows
            n = h * NT + k
            if k == 0 and h % mg == 0:
                pe.wait_ge(m_copied.sem, m_copied.at(i, 2 * (h // mg + 1)))
            pe.wait_ge(exped.sem, exped.at(i, max(n - 1, 0)))
            lo, hi = queries_of(k)
            bank = bbank[n % 2]
            nc.tensor.matmul(bank[:, lo:hi], ks[at:at + rows, g, k * P:(k + 1) * P], qs[at:at + rows, g, lo:hi], start=True, stop=False)
            ins = nc.tensor.matmul(bank[:, lo:hi], c.pick[0:48, h % mg, :], mT[:, h // mg % 2, lo:hi], start=False, stop=not masked)
            if masked:
                ins = nc.tensor.matmul(bank[:, lo:lo + P], c.ident_bf[:, :], mask_b[:, :], start=False, stop=True)
            ins.then_inc(scored_b.sem, scored_b.one())

        def value(i, h, k):
            if h == 0 and k == 0:
                pe.wait_ge(w_emptied.sem, w_emptied.at(i, 0))
                pe.wait_ge(sums_copied.sem, sums_copied.at(i, 0))
            pe.wait_ge(exped.sem, exped.at(i, NT * h + k + 1))
            side, b = h // half, h % half
            col = side * half * (R + E) + b * R
            lo, hi = queries_of(k)
            ins = nc.tensor.matmul(obank[side][0:R, lo:hi], vx_flat[:, k, col:col + R], pT[:, h % 2, k, lo:hi],
                                   start=b == 0 and k == 0, stop=b == half - 1 and k == NT - 1, skip_group_check=True)
            if k == NT - 1:
                ins.then_inc(head_done.sem, head_done.one())

        def turn_sums(side):
            def emit(bank):
                for q in range(NT):
                    ins = nc.tensor.transpose(bank[:, q * R:(q + 1) * R], sums[:, side, q * P:(q + 1) * P], c.ident[0:R, 0:R])
                return ins
            return emit

        def at_place(i, h, k):
            for what in places.get((h, k), []):
                if what[0:3] == "max":
                    group = MG if what == "max_next" else int(what[-1])
                    maxima(i, group, what)
                elif what[0:4] == "sums":
                    side = int(what[-1])
                    pe.wait_ge(sums_copied.sem, sums_copied.at(i, side + 1))
                    fill(i, what, turn_sums(side))
                elif what[0:6] == "turned":
                    s = int(what[-1])
                    if s > 0:
                        pe.wait_ge(step_taken.sem, step_taken.at(i, s))
                    else:
                        pe.wait_ge(ctx_ready.sem, ctx_ready.at(i, 1))
                    fill(i, what, turn(ctxt))
                elif what[0:9] == "projected":
                    s = int(what[-1])
                    pe.wait_ge(w_emptied.sem, w_emptied.at(i, w_n(i, f"turned{s}")))
                    fill(i, what, tokens(stepT, w[out_steps[s]], w.get(out_steps[s] + "_b")))
                else:
                    prepare(i, what)

        ahead = Ahead()
        for what in W_AHEAD[:-1]:
            prepare(ahead, what)
        for h in range(heads, heads + mg + 1):
            for q in range(NT):
                score_a(ahead, h, q)
        maxima(ahead, MG, "max_next")
        for signal in (w_filled, scored_a):
            signal.ahead_done()
        with turns(pe, B) as i:
            for h in range(-1, heads):
                for k in range(NT):
                    at_place(i, h, k)
                    for head, q in units_a(h, k):
                        score_a(i, head, q)
                    if h >= 0:
                        value(i, h, k)
                    if h + 1 < heads:
                        score_b(i, h + 1, k)
            at_place(i, heads, 0)
            turn_done(w_filled, scored_a, scored_b, head_done)

    @block.scalar
    def _(act):
        if future:
            act.wait_ge(prepared.sem, 1)
            nc.scalar.copy(afT[:, :, :], w0[:, :].rearrange("p (f n) -> p f n", f=4)).then_inc(prepared.sem, prepared.one())
            act.wait_ge(prepared.sem, 3)
            nc.scalar.copy(wkf[:, :, :], w1[:, :].rearrange("p (f n) -> p f n", f=4)).then_inc(prepared.sem, prepared.one())
            nc.scalar.copy(wvf[:, :, :], w0[:, :].rearrange("p (f n) -> p f n", f=4)).then_inc(prepared.sem, prepared.one())
        if bias or affine:
            wait_weights(act, c, w)
        if bias:
            act.wait_ge(prepared.sem, 2 if modulated else 1)

        def empty(i, what, *emits):
            n = w_emptied.n
            assert w_n(i, what) == n + 1, what
            act.wait_ge(w_filled.sem, w_filled.at(i, n + 1))
            bank = wbank[(n + (0 if i.ahead else len(W_AHEAD))) % 2]
            for emit in emits:
                ins = emit(bank)
            ins.then_inc(w_emptied.sem, w_emptied.one())

        def tokens_to(dst):
            return lambda bank: nc.scalar.copy(dst, bank[:, :].rearrange("p (j d) -> p j d", j=NT))

        def prepare(i, what):
            kind, g = what[0], int(what[-1]) if what[-1].isdigit() else 0
            if what == "uT":
                if affine:
                    empty(i, what, lambda bank: nc.scalar.activation(uT[:, :], bank[:, :], ACT.Identity, bias=w["shift"], scale=w["gain"]))
                else:
                    empty(i, what, lambda bank: nc.scalar.copy(uT[:, :], bank[:, :]))
            elif kind == "m":
                if not i.ahead:
                    act.wait_ge(mod_scaled.sem, mod_scaled.at(i, G))
                empty(i, what, lambda bank: nc.scalar.activation(modT[:, g, :], bank[:, :], ACT.Sigmoid, bias=mod_bias[:, g:g + 1]))
            elif kind in "qk":
                m = 2 * g + (kind == "k")
                if m >= 2 or not i.ahead:
                    act.wait_ge(stacked.sem, stacked.at(i, 2 * G + m - 1))
                part, isc = (0, scale) if kind == "q" else (1, 1.0)
                low_scale = w["maskq_scaled"] if kind == "q" else w["maskk"][1]
                at = part * G + g
                if modulated and kind == "q":
                    empty(i, what, lambda bank: nc.scalar.activation(scaled, bank[:, :], ACT.Identity, bias=biases[:, g:g + 1], scale=isc))
                    return
                empty(i, what,
                      lambda bank: nc.scalar.activation(high[:, part, :], bank[:, :], ACT.Identity, bias=biases[:, at:at + 1] if bias else 0.0, scale=isc),
                      lambda bank: nc.scalar.activation(lowpart[:, part, :], bank[:, :], ACT.Identity, bias=biases[:, 2 * G + at:2 * G + at + 1] if bias else 0.0, scale=low_scale))
            elif what == "v":
                if not i.ahead:
                    act.wait_ge(head_done.sem, head_done.at(i, heads))
                empty(i, what, lambda bank: nc.scalar.copy(vx[:, :, :, 0:hd], bank[:, :].rearrange("p (j h e) -> p j h e", j=NT, h=heads)))
            elif what == "fq":
                act.wait_ge(fut_used.sem, fut_used.at(i, 1))
                empty(i, what, tokens_to(qtok[:, :, :]))
            else:
                if i.ahead:
                    act.wait_ge(prepared.sem, 5)
                empty(i, what, tokens_to((kf if what[1] == "k" else vf)[:, g, :, :]))

        def modulated_parts(i, g):
            act.wait_ge(mod_scaled.sem, mod_scaled.at(i, G + g + 1))
            nc.scalar.copy(high[:, 0, :], scaled)
            nc.scalar.mul(lowpart[:, 0, :], scaled, w["maskq"][1]).then_inc(parts_ready.sem, parts_ready.one())

        def rows_of_maxima(i, group, what):
            if not i.ahead:
                act.wait_ge(m_copied.sem, m_copied.at(i, 2 * group))
            empty(i, what, lambda bank: nc.scalar.copy(mrow[:, :], bank[0:mg, :]))

        def at_place(i, h, k):
            for what in places.get((h, k), []):
                if what[0:3] == "max":
                    rows_of_maxima(i, MG if what == "max_next" else int(what[-1]), what)
                    if future and what == f"max{MG - 1}":
                        act.wait_ge(fut_asked.sem, fut_asked.at(i, 1))
                        nc.scalar.activation(pf[:, :, :, :], fut[:, :, :, :], ACT.Exp).then_inc(fut_exped.sem, fut_exped.one())
                elif what[0:4] == "sums":
                    side = int(what[-1])
                    empty(i, what, lambda bank: nc.scalar.copy(sums_tok[:, side, :, :, :], bank[:, 0:NT * R].rearrange("p (j b e) -> p j b e", j=NT, e=E)))
                elif what[0:6] == "turned":
                    empty(i, what, lambda bank: nc.scalar.copy(stepT[:, :], bank[:, :]))
                elif what[0:9] == "projected":
                    act.wait_ge(step_taken.sem, step_taken.at(i, int(what[-1])))
                    empty(i, what, tokens_to(stepo[:, :, :]))
                else:
                    prepare(i, what)
                    if modulated and what == f"q{G - 1}":
                        modulated_parts(i, G - 1)

        def copy_sums(i, side):
            act.wait_ge(head_done.sem, head_done.at(i, (side + 1) * half))
            nc.scalar.copy(sums[:, side, :], obank[side][0:R, :]).then_inc(sums_copied.sem, sums_copied.one())

        ahead = Ahead()
        for what in W_AHEAD[:-1]:
            prepare(ahead, what)
            if modulated and what[0] == "q":
                modulated_parts(ahead, int(what[-1]))
        rows_of_maxima(ahead, MG, "max_next")
        w_emptied.ahead_done()
        parts_ready.ahead_done()
        with turns(act, B) as i:
            for h in range(-1, heads):
                if 0 <= h + 1 < heads:
                    act.wait_ge(head_done.sem, head_done.at(i, max(h, 0)))
                for k in range(NT):
                    at_place(i, h, k)
                    if h + 1 < heads:
                        lo, hi = queries_of(k)
                        n = (h + 1) * NT + k
                        act.wait_ge(scored_b.sem, scored_b.at(i, n + 1))
                        nc.scalar.activation(pT[:, (h + 1) % 2, k, lo:hi], bbank[n % 2][:, lo:hi], ACT.Exp).then_inc(exped.sem, exped.one())
                    if modulated and h in stack_at and k == 1:
                        modulated_parts(i, stack_at.index(h))
                    if h == half and k == 1:
                        copy_sums(i, 0)
            copy_sums(i, 1)
            at_place(i, heads, 0)
            turn_done(w_emptied, exped, sums_copied)

    @block.gpsimd
    def _(pool):
        for _ in range(norms_ahead):
            norm.on_gpsimd(nc, pool, c, Ahead())
        for signal in (norm.eps_added, norm.rstd_ready):
            signal.ahead_done()
        with turns(pool, B) as i:
            for _ in range(norms):
                norm.on_gpsimd(nc, pool, c, i)

    @block.vector
    def _(dve):
        wait_weights(dve, c, w)
        nc.vector.memset(vx[:, :, :, :], 0.0)
        dve.drain()
        nc.vector.memset(vx[:, :, :, hd:E], 1.0)
        nc.vector.memset(mT[:, :, :].bitcast(F32), 0.0)
        if bias:
            nc.vector.tensor_scalar(biases[:, 0:G], w["bqk"][:, 0:G], scale, None, ALU.mult)
            nc.vector.tensor_copy(biases[:, G:2 * G], w["bqk"][:, G:2 * G])
            nc.vector.tensor_scalar(biases[:, 2 * G:3 * G], w["bqk"][:, 0:G], w["maskq"][1], scale, ALU.mult, ALU.mult)
            ins = nc.vector.tensor_scalar(biases[:, 3 * G:4 * G], w["bqk"][:, G:2 * G], w["maskk"][1], None, ALU.mult)
            if modulated:
                dve.wait_ge(prepared.sem, 1)
                nc.vector.tensor_tensor(mod_bias[:, :], w0[:, 0:G], w["cg_am_bias"][:, 0:G], ALU.add).then_inc(mod_added.sem, mod_added.one())
                dve.wait_ge(mod_added.sem, 1)
                ins = nc.vector.tensor_tensor(mod_bias[:, :], mod_bias[:, :], w["cg_am_bias"][:, G:2 * G], ALU.add)
            ins.then_inc(prepared.sem, prepared.one())

        def then_in(i):
            def then(ins):
                ins.then_inc(step.sem, step.one())
                dve.wait_ge(step.sem, step.at(i, step.n))
            return then

        def next_statistics(i):
            if source is None:
                norm.statistics(nc, dve, lambda j: i.next_tile(c.x, j))

        def next_source(i):
            dve.wait_ge(w_filled.sem, w_filled.at(i, 0) if not i.ahead else 1)
            if source is None:
                if affine:
                    then_in(i)(norm.scaled(nc, dve, i, lambda j: i.next_tile(c.x, j), lambda j: i.next_tile(c.y, j)))
                    ins = norm.on_vector(nc, dve, i, lambda j: i.next_tile(c.y, j), lambda j: src[:, j, :])
                else:
                    ins = norm.scaled(nc, dve, i, lambda j: i.next_tile(c.x, j), lambda j: src[:, j, :])
            else:
                ins = nc.vector.tensor_copy(src[:, :, :], i.next_tiles(c.ctx))
            ins.then_inc(src_ready.sem, src_ready.one())
            if "mixed" in out_steps:
                dve.wait_ge(src_ready.sem, src_ready.at(i, 2))
                nc.vector.tensor_copy(i.next_tiles(c.y), src[:, :, :])

        def modulate(i, g):
            dve.wait_ge(w_emptied.sem, w_emptied.at(i, w_n(i, f"q{g}")))
            nc.vector.tensor_tensor(scaled, scaled, modT[:, g, :], ALU.mult).then_inc(mod_scaled.sem, mod_scaled.one())

        def stack(i, g, kind):
            if modulated and kind == "q":
                dve.wait_ge(parts_ready.sem, parts_ready.at(i, G + g + 1))
            else:
                dve.wait_ge(w_emptied.sem, w_emptied.at(i, w_n(i, f"{kind}{g}")))
            if not i.ahead:
                dve.wait_ge(scored_b.sem, scored_b.at(i, in_group * (g + 1) * NT))
            part, m, dst = (0, w["maskq"], qs[:, g, :]) if kind == "q" else (1, w["maskk"], ks[:, g, :])
            nc.vector.scalar_tensor_tensor(out=dst, in0=high[:, part, :].bitcast(F32), scalar=m[0], in1=lowpart[:, part, :], op0=ALU.mult, op1=ALU.add).then_inc(stacked.sem, stacked.one())

        def future_scores(i, f):
            then = then_in(i)
            dve.wait_ge(w_emptied.sem, w_emptied.at(i, w_n(i, f"fk{f}")))
            then(nc.vector.tensor_tensor(kf[:, f, :, :], kf[:, f, :, :], qtok[:, :, :], ALU.mult))
            then(nc.vector.tensor_reduce(fut[:, f, :, :], kf[:, f, :, :].rearrange("p j (h e) -> p j h e", h=heads), AX.X, ALU.add))
            if f == 3:
                nc.vector.tensor_reduce(futmax[:, :, :], fut[:, :, :, :].rearrange("p f j h -> p j h f"), AX.X, ALU.max, negate=True)
                dve.drain()

        def reduce_a(i, h, q):
            n = h * NT + q
            group = h // mg
            if q == 0 and h % mg == 0 and not i.ahead:
                dve.wait_ge(w_filled.sem, w_filled.at(i, w_n(i, f"max{group - MG}") if group > MG else 0))
            dve.wait_ge(scored_a.sem, scored_a.at(i, n + 1))
            nc.vector.tensor_reduce(negmax[:, q, h % heads:h % heads + 1], abank[n % 2][:, keys_of(q)[0]:keys_of(q)[1]], AX.X, ALU.max, negate=True).then_inc(maxed.sem, maxed.one())

        def maxima(i, group, what):
            of_group = slice(group % MG * mg, (group % MG + 1) * mg)
            if future:
                dve.wait_ge(maxed.sem, maxed.at(i, (group + 1) * mg * NT))
                nc.vector.tensor_tensor(negmax[:, :, of_group], negmax[:, :, of_group], futmax[:, :, of_group], ALU.min).then_inc(m_final.sem, m_final.one())
                if group == MG - 1:
                    dve.wait_ge(m_final.sem, m_final.at(i, MG))
                    nc.vector.tensor_tensor(fut[:, :, :, :], fut[:, :, :, :], negmax[:, :, :].unsqueeze(1).to_broadcast([P, 4, NT, heads]), ALU.add).then_inc(fut_asked.sem, fut_asked.one())
            dve.wait_ge(w_emptied.sem, w_emptied.at(i, w_n(i, what)))
            if not i.ahead:
                dve.wait_ge(scored_b.sem, scored_b.at(i, (group - 1) * mg * NT))
            part = mT[:, group % 2, :]
            nc.vector.tensor_copy(part[0:mg, :], mrow[:, :]).then_inc(m_copied.sem, m_copied.one())
            dve.wait_ge(m_copied.sem, m_copied.at(i, 2 * group + 1))
            nc.vector.tensor_tensor(part[32:32 + mg, :], mrow[:, :], part[0:mg, :].bitcast(F32), ALU.subtract).then_inc(m_copied.sem, m_copied.one())

        def future_values(i, then):
            dve.wait_ge(fut_exped.sem, fut_exped.at(i, 1))
            for f in range(4):
                ins = nc.vector.tensor_tensor(vf[:, f, :, :].rearrange("p j (h e) -> p (j h) e", h=heads), vf[:, f, :, :].rearrange("p j (h e) -> p (j h) e", h=heads),
                                              pf[:, f, :, :].rearrange("p j h -> p (j h)").unsqueeze(2).to_broadcast([P, NT * heads, hd]), ALU.mult)
            nc.vector.tensor_reduce(futden[:, :, :], pf[:, :, :, :].rearrange("p f j h -> p j h f"), AX.X, ALU.add)
            then(ins)
            then(nc.vector.tensor_tensor(vf[:, 0:2, :, :], vf[:, 0:2, :, :], vf[:, 2:4, :, :], ALU.add))
            nc.vector.tensor_tensor(tmp[:, :, :], vf[:, 0, :, :], vf[:, 1, :, :], ALU.add).then_inc(fut_used.sem, fut_used.one())
            dve.wait_ge(fut_used.sem, fut_used.at(i, 1))

        ahead = Ahead()
        next_statistics(ahead)
        next_source(ahead)
        for g in range(G):
            if modulated:
                modulate(ahead, g)
            stack(ahead, g, "q")
            stack(ahead, g, "k")
        if future:
            for f in range(4):
                future_scores(ahead, f)
        for h in range(heads, heads + mg + 1):
            for q in range(NT):
                reduce_a(ahead, h, q)
        maxima(ahead, MG, "max_next")
        for signal in (step, norm.variance, stacked, maxed, m_copied, m_final, src_ready, mod_scaled):
            signal.ahead_done()
        with turns(dve, B) as i:
            then = then_in(i)
            for h in range(-1, heads):
                if (h, 0) == next_at[0]:
                    next_statistics(i)
                if (h, 0) == next_at[1]:
                    next_source(i)
                if 0 < h + 1 < heads and (h + 1) % mg == 0:
                    maxima(i, (h + 1) // mg, f"max{(h + 1) // mg}")
                if future and h == 12:
                    future_values(i, then)
                for k in range(NT):
                    if (h, k) == next_at[1] and k > 0:
                        next_source(i)
                    if h in stack_at:
                        g = stack_at.index(h)
                        if modulated and k == 1:
                            modulate(i, g)
                        if k == 2 + modulated:
                            stack(i, g, "q")
                    if h - 1 in stack_at and k == (mg > 1):
                        stack(i, stack_at.index(h - 1), "k")
                    if future and (h, k) in ((14, 0), (15, 0), (15, 2)):
                        future_scores(i, ((14, 0), (15, 0), (15, 2)).index((h, k)))
                    for head, q in units_a(h, k):
                        reduce_a(i, head, q)
            if heads - 1 in stack_at:
                stack(i, stack_at.index(heads - 1), "k")
            if future:
                future_scores(i, 3)
            maxima(i, MG, "max_next")
            dve.wait_ge(w_emptied.sem, w_emptied.at(i, w_n(i, "sums1")))
            if future:
                then(nc.vector.tensor_tensor(rden[:, :, :, :], sums_tok[:, :, :, :, hd], futden[:, :, :].rearrange("p j (s b) -> p s j b", s=2), ALU.add))
                then(nc.vector.reciprocal(rden[:, :, :, :], rden[:, :, :, :]))
            else:
                then(nc.vector.reciprocal(rden[:, :, :, :], sums_tok[:, :, :, :, hd]))
            for side in range(2):
                den = rden[:, side, :, :].unsqueeze(3).to_broadcast([P, NT, half, hd])
                part = slice(side * half * hd, (side + 1) * half * hd)
                dst = ctxt[:, :, part].rearrange("p j (b e) -> p j b e", b=half)
                if future:
                    more = tmp[:, :, part].rearrange("p j (b e) -> p j b e", b=half)
                    then(nc.vector.tensor_tensor(more, more, sums_tok[:, side, :, :, 0:hd], ALU.add))
                    ins = nc.vector.tensor_tensor(dst, more, den, ALU.mult)
                else:
                    ins = nc.vector.tensor_tensor(dst, sums_tok[:, side, :, :, 0:hd], den, ALU.mult)
            ins.then_inc(ctx_ready.sem, ctx_ready.one())
            if modulated:
                modulate(i, G - 1)
            stack(i, G - 1, "q")
            stack(i, G - 1, "k")
            dve.wait_ge(ctx_ready.sem, ctx_ready.at(i, 1))
            result = ctxt
            for s in range(len(out_steps)):
                kind = out_steps[s]
                dve.wait_ge(w_emptied.sem, w_emptied.at(i, w_n(i, f"projected{s}")))
                if kind == "mixed":
                    nc.vector.tensor_tensor(tmp[:, :, :], stepo[:, :, :], tiles_of(c.y, i), ALU.add).then_inc(step_taken.sem, step_taken.one())
                    dve.wait_ge(step_taken.sem, step_taken.at(i, s + 1))
                    then(norm.on_vector(nc, dve, i, lambda j: tmp[:, j, :], lambda j: ctxt[:, j, :]))
                    then(nc.vector.tensor_tensor(ctxt[:, :, :], ctxt[:, :, :], wide(w["g1"]), ALU.mult))
                    then(nc.vector.tensor_tensor(tiles_of(c.y, i), ctxt[:, :, :], wide(w["be1"]), ALU.add))
                elif kind == "proj":
                    nc.vector.tensor_tensor(tiles_of(c.y, i), stepo[:, :, :], tiles_of(c.y, i), ALU.add).then_inc(step_taken.sem, step_taken.one())
                elif kind == "causal_out":
                    then(nc.vector.tensor_scalar(stepo[:, :, :], stepo[:, :, :], w["mix"][1], None, ALU.mult))
                    nc.vector.scalar_tensor_tensor(out=tiles_of(c.ctx, i), in0=tiles_of(c.ctx, i), scalar=w["mix"][0], in1=stepo[:, :, :], op0=ALU.mult, op1=ALU.add).then_inc(step_taken.sem, step_taken.one())
                elif kind == "meta_out":
                    then(nc.vector.tensor_scalar(stepo[:, :, :], stepo[:, :, :], w["mix"][1], None, ALU.mult))
                    nc.vector.scalar_tensor_tensor(out=ctxt[:, :, :], in0=tiles_of(c.ctx, i), scalar=w["mix"][0], in1=stepo[:, :, :], op0=ALU.mult, op1=ALU.add).then_inc(step_taken.sem, step_taken.one())
                else:
                    result = stepo
            if finish == "residual_norm":
                then(norm.on_vector(nc, dve, i, lambda j: result[:, j, :], lambda j: tmp[:, j, :]))
                ins = nc.vector.tensor_tensor(tiles_of(c.x, i), tiles_of(c.x, i), tmp[:, :, :], ALU.add)
                if result is stepo:
                    ins.then_inc(step_taken.sem, step_taken.one())
                    dve.wait_ge(step_taken.sem, step_taken.at(i, len(out_steps)))
                else:
                    then(ins)
            elif finish == "context":
                then(nc.vector.tensor_copy(tiles_of(c.ctx, i), ctxt[:, :, :]))
            turn_done(step, norm.variance, stacked, maxed, m_copied, ctx_ready)
    ph.close()



class Layer:

    def __init__(self, kb, mb, W, func, scale=None, bias=None, V=None, v_op=None, v_arg=None):
        self.kb, self.mb, self.W, self.func, self.scale, self.bias = kb, mb, W, func, scale, bias
        self.V, self.v_op, self.v_arg = V, v_op, v_arg


def mlp_phase(nc, c, name, w, layers, final, experts=1, source="x", affine=False, shifted=False, gate=None,
              out_scale=False, tail_gain=False, finish="residual_norm"):
    ph = Phase(nc, name)
    S = ph.flag
    L = layers(0)
    gated = any(l.V is not None for l in L)
    moe = experts > 1
    top1 = gate == "top1"
    NA = 1 + experts * sum(l.mb for l in L) + top1
    NB = shifted + moe + experts * (1 + sum(l.mb for l in L if l.V is not None)) + top1
    widest = max(l.mb for l in L)
    norms_ahead = int(source == "x" or affine or shifted)
    norms = norms_ahead + (finish == "residual_norm") + tail_gain
    src = ph.sb("src", [P, NT, D])
    uT = ph.sb("uT", [P, T])
    hidden = [ph.sb(f"hidden{k}", [P, widest, T]) for k in range(2)]
    gates = ph.sb("gates", [P, 2, T]) if gated else None
    acc = ph.sb("acc", [P, NT, D])
    tmp = ph.sb("tmp", [P, NT, D])
    if moe:
        logit = ph.sb("logit", [P, NT, 8])
        chosen = ph.sb("chosen", [P, NT, 8])
        picked = ph.sb("picked", [P, NT, 8])
        second = ph.sb("second", [P, NT, 8])
        small = ph.sb("small", [P, 4, NT])
        chosenT = ph.sb("chosenT", [8, T])
    ring_a, ring_b = c.bank[0:4], c.bank[4:8]
    a_filled, a_emptied, b_filled, b_emptied = S("a_filled", NA, 1), S("a_emptied", NA, 1), S("b_filled", NB, shifted + moe), S("b_emptied", NB, shifted + moe)
    src_ready, expected, exped = S("src_ready"), S("exp_asked"), S("gate_exped")
    chosen_ready = S("chosen_ready")
    steps = {"residual_norm": 2}.get(finish, 0) + 3 * tail_gain + {None: 0, "top1": 5, "top2": 18}[gate]
    step = S("dve_step", steps, {None: 0, "top1": 5, "top2": 18}[gate])
    norm = Norm(ph, max(norms, 1), norms_ahead)
    block = ph.block()

    @block.sync
    def _(sp):
        load_next(sp, c)

    def order():
        out = []
        for e in range(experts):
            out.append(("up", e))
            if e == 0 and top1:
                out.append(("chosen", 0))
            if e > 0:
                out.append(("down", e - 1))
        return out + [("down", experts - 1)]

    @block.tensor
    def _(pe):
        wait_weights(pe, c, w)

        def fill(i, ring, n, filled, emptied, emit):
            if n[0] > 3 or not i.ahead:
                pe.wait_ge(emptied.sem, emptied.at(i, max(n[0] - 3, 0)))
            emit(ring[n[0] % 4]).then_inc(filled.sem, filled.one())
            n[0] += 1

        def next_shifted(i, nb):
            def emit(bank):
                for j in range(NT):
                    dst = bank[:, j * H2:(j + 1) * H2]
                    ins = nc.tensor.matmul(dst, c.shift[:, 0, :], i.next_tile(c.y, j)[:, :, H2:D], start=True, stop=j == 0)
                    if j > 0:
                        ins = nc.tensor.matmul(dst, c.shift[:, 1, :], i.next_tile(c.y, j - 1)[:, :, H2:D], start=False, stop=True)
                return ins
            fill(i, ring_b, nb, b_filled, b_emptied, emit)

        def next_turned(i, na):
            pe.wait_ge(src_ready.sem, src_ready.at(i, 2))

            def turn(bank):
                for j in range(NT):
                    ins = nc.tensor.transpose(bank[:, j * P:(j + 1) * P], src[:, j, :], c.ident[:, :])
                return ins
            fill(i, ring_a, na, a_filled, a_emptied, turn)

        def next_logits(i, na, nb):
            pe.wait_ge(a_emptied.sem, a_emptied.at(i, na[0]))

            def emit(bank):
                for j in range(NT):
                    ins = nc.tensor.matmul(bank[:, j * 8:(j + 1) * 8], uT[:, j * P:(j + 1) * P], w["gate"], start=True, stop=True)
                return ins
            fill(i, ring_b, nb, b_filled, b_emptied, emit)

        ahead, na, nb = Ahead(), [0], [0]
        if shifted:
            next_shifted(ahead, nb)
        next_turned(ahead, na)
        if moe:
            next_logits(ahead, na, nb)
        a_filled.ahead_done()
        b_filled.ahead_done()
        with turns(pe, B) as i:
            na, nb = [0], [0]
            fill_a = lambda emit: fill(i, ring_a, na, a_filled, a_emptied, emit)
            fill_b = lambda emit: fill(i, ring_b, nb, b_filled, b_emptied, emit)
            if shifted:
                next_shifted(i, nb)
            pe.wait_ge(a_emptied.sem, a_emptied.at(i, 0))
            ready = {}

            def product(bank, W, m, kb, src_of, blocks):
                for k in range(kb):
                    if m == 0 and blocks:
                        signal, n = blocks[k]
                        pe.wait_ge(signal.sem, signal.at(i, n))
                    ins = nc.tensor.matmul(bank[:, :], W(k, m), src_of(k), start=k == 0, stop=k == kb - 1)
                return ins

            for what, e in order():
                if what == "up":
                    src_of = lambda k: uT[:, :]
                    blocks = []
                    for l, layer in enumerate(layers(e)):
                        made = []
                        for m in range(layer.mb):
                            fill_a(lambda bank: product(bank, layer.W, m, layer.kb, src_of, blocks))
                            if layer.V is not None:
                                fill_b(lambda bank: product(bank, layer.V, m, layer.kb, src_of, []))
                            made.append((b_emptied, nb[0]) if layer.V is not None else (a_emptied, na[0]))
                        buf = hidden[(e + l) % 2]
                        ready[e] = blocks = made
                        src_of = (lambda b: lambda k: b[:, k, :])(buf)
                elif what == "chosen":
                    pe.wait_ge(chosen_ready.sem, chosen_ready.at(i, 1))

                    def turn_chosen(bank):
                        for j in range(NT):
                            ins = nc.tensor.transpose(bank[0:8, j * P:(j + 1) * P], chosen[:, j, :], c.ident[:, :])
                        return ins
                    fill_a(turn_chosen)
                    pe.wait_ge(a_emptied.sem, a_emptied.at(i, na[0]))

                    def chosen_bias(bank):
                        for j in range(NT):
                            ins = nc.tensor.matmul(bank[:, j * P:(j + 1) * P], chosenT[:, j * P:(j + 1) * P], w["expert_bias"], start=True, stop=True)
                        return ins
                    fill_b(chosen_bias)
                else:
                    if moe and e == experts - 2:
                        next_turned(i, na)
                    if moe and e == experts - 1:
                        next_logits(i, na, nb)
                    kb, W = final(e)
                    buf = hidden[(e + len(L) - 1) % 2]

                    def down(bank):
                        for j in range(NT):
                            for k in range(kb):
                                if j == 0:
                                    signal, n = ready[e][k]
                                    pe.wait_ge(signal.sem, signal.at(i, n))
                                ins = nc.tensor.matmul(bank[:, j * P:(j + 1) * P], buf[:, k, j * P:(j + 1) * P], W(k), start=k == 0, stop=k == kb - 1 and "final_b" not in w)
                            if "final_b" in w:
                                ins = nc.tensor.matmul(bank[:, j * P:(j + 1) * P], c.ones[0:1, :], w["final_b"], start=False, stop=True)
                        return ins
                    fill_b(down)
            if not moe:
                next_turned(i, na)
            turn_done(a_filled, b_filled)

    @block.scalar
    def _(act):
        wait_weights(act, c, w)

        def empty(i, na, emit):
            act.wait_ge(a_filled.sem, a_filled.at(i, na[0] + 1))
            emit(ring_a[na[0] % 4]).then_inc(a_emptied.sem, a_emptied.one())
            na[0] += 1

        def next_turned(i, na):
            if affine:
                empty(i, na, lambda bank: nc.scalar.activation(uT[:, :], bank[:, :], ACT.Identity, bias=w["shift"], scale=w["gain"]))
            else:
                empty(i, na, lambda bank: nc.scalar.copy(uT[:, :], bank[:, :]))

        def next_gate(i):
            if gate == "top2":
                act.wait_ge(expected.sem, expected.at(i, 2))
                nc.scalar.activation(logit[:, :, :], logit[:, :, :], ACT.Exp).then_inc(exped.sem, exped.one())

        next_turned(Ahead(), [0])
        next_gate(Ahead())
        a_emptied.ahead_done()
        with turns(act, B) as i:
            na, nb = [0], [int(shifted)]
            for what, e in order():
                if what == "up":
                    for l, layer in enumerate(layers(e)):
                        for m in range(layer.mb):
                            if layer.V is not None:
                                k = nb[0]
                                act.wait_ge(b_emptied.sem, b_emptied.at(i, max(k - 1, 0)))
                                dst = gates[:, nb[0] % 2, :]
                                nb[0] += 1
                            else:
                                dst = hidden[(e + l) % 2][:, m, :]
                            kw = {}
                            if layer.scale is not None:
                                kw["scale"] = layer.scale(m)
                            if layer.bias is not None:
                                kw["bias"] = layer.bias(m)
                            empty(i, na, lambda bank: nc.scalar.activation(dst, bank[:, :], layer.func, **kw))
                elif what == "chosen":
                    empty(i, na, lambda bank: nc.scalar.copy(chosenT[:, :], bank[0:8, :]))
                    nb[0] += 1
                else:
                    if e == max(experts - 2, 0):
                        next_turned(i, na)
                    nb[0] += 1
            next_gate(i)
            turn_done(a_emptied)

    @block.gpsimd
    def _(pool):
        for _ in range(norms_ahead):
            norm.on_gpsimd(nc, pool, c, Ahead())
        for signal in (norm.eps_added, norm.rstd_ready):
            signal.ahead_done()
        with turns(pool, B) as i:
            for _ in range(norms):
                norm.on_gpsimd(nc, pool, c, i)

    @block.vector
    def _(dve):
        wait_weights(dve, c, w)
        whole = c.x if source == "x" else c.y

        def then_in(i):
            def then(ins):
                ins.then_inc(step.sem, step.one())
                dve.wait_ge(step.sem, step.at(i, step.n))
            return then

        def empty_b(i, nb, emit):
            dve.wait_ge(b_filled.sem, b_filled.at(i, nb[0] + 1))
            emit(ring_b[nb[0] % 4]).then_inc(b_emptied.sem, b_emptied.one())
            nb[0] += 1
            return nb[0]

        def next_begun(i, nb):
            if shifted:
                if not i.ahead:
                    dve.wait_ge(a_filled.sem, a_filled.at(i, 0))

                def take_shifted(bank):
                    nc.vector.tensor_copy(src[:, :, 0:H2], i.next_tiles(c.y)[:, :, 0:H2])
                    return nc.vector.tensor_copy(src[:, :, H2:D], bank[:, 0:NT * H2].rearrange("p (j d) -> p j d", j=NT))
                n = empty_b(i, nb, take_shifted)
                dve.wait_ge(b_emptied.sem, b_emptied.at(i, n))
                norm.statistics(nc, dve, lambda j: src[:, j, :])
            elif source == "x" or affine:
                norm.statistics(nc, dve, lambda j: i.next_tile(whole, j))

        def next_scaled(i):
            if not i.ahead:
                dve.wait_ge(a_filled.sem, a_filled.at(i, 0))
            if shifted:
                ins = norm.scaled(nc, dve, i, lambda j: src[:, j, :], lambda j: src[:, j, :])
            elif source == "x" or affine:
                ins = norm.scaled(nc, dve, i, lambda j: i.next_tile(whole, j), lambda j: src[:, j, :])
            else:
                ins = nc.vector.tensor_copy(src[:, :, :], i.next_tiles(whole))
            ins.then_inc(src_ready.sem, src_ready.one())

        def next_gate(i, nb):
            then = then_in(i)
            bc = lambda a: a.unsqueeze(2).to_broadcast([P, NT, 8])
            down8 = c.down8[:, :].unsqueeze(1).to_broadcast([P, NT, 8])
            n = empty_b(i, nb, lambda bank: nc.vector.tensor_copy(logit[:, :, :], bank[:, 0:8 * NT].rearrange("p (j e) -> p j e", e=8)))
            dve.wait_ge(b_emptied.sem, b_emptied.at(i, n))

            def first_of(values, largest, dst):
                then(nc.vector.tensor_tensor(dst, values, bc(largest), ALU.is_ge))
                then(nc.vector.tensor_tensor(dst, dst, down8, ALU.mult))
                then(nc.vector.tensor_reduce(small[:, 3, :], dst, AX.X, ALU.max))
                return nc.vector.tensor_tensor(dst, dst, bc(small[:, 3, :]), ALU.is_equal)

            then(nc.vector.tensor_reduce(small[:, 0, :], logit[:, :, :], AX.X, ALU.max))
            if gate == "top1":
                then(first_of(logit[:, :, :], small[:, 0, :], picked[:, :, :]))
                return
            nc.vector.tensor_tensor(logit[:, :, :], logit[:, :, :], bc(small[:, 0, :]), ALU.subtract).then_inc(expected.sem, expected.one())
            dve.wait_ge(exped.sem, exped.at(i, 2))
            then(nc.vector.tensor_reduce(small[:, 0, :], logit[:, :, :], AX.X, ALU.add))
            then(nc.vector.reciprocal(small[:, 0, :], small[:, 0, :]))
            then(nc.vector.tensor_tensor(logit[:, :, :], logit[:, :, :], bc(small[:, 0, :]), ALU.mult))
            then(nc.vector.tensor_reduce(small[:, 0, :], logit[:, :, :], AX.X, ALU.max))
            then(first_of(logit[:, :, :], small[:, 0, :], picked[:, :, :]))
            then(nc.vector.scalar_tensor_tensor(out=second[:, :, :], in0=picked[:, :, :], scalar=-2.0, in1=logit[:, :, :], op0=ALU.mult, op1=ALU.add))
            then(nc.vector.tensor_reduce(small[:, 1, :], second[:, :, :], AX.X, ALU.max))
            nc.vector.tensor_tensor(small[:, 2, :], small[:, 0, :], small[:, 1, :], ALU.add)
            then(first_of(second[:, :, :], small[:, 1, :], second[:, :, :]))
            nc.vector.tensor_tensor(picked[:, :, :], picked[:, :, :], second[:, :, :], ALU.add)
            then(nc.vector.tensor_scalar(small[:, 2, :], small[:, 2, :], 1e-8, None, ALU.add))
            nc.vector.tensor_tensor(picked[:, :, :], picked[:, :, :], logit[:, :, :], ALU.mult)
            then(nc.vector.reciprocal(small[:, 2, :], small[:, 2, :]))
            then(nc.vector.tensor_tensor(picked[:, :, :], picked[:, :, :], bc(small[:, 2, :]), ALU.mult))

        def next_chosen(i):
            nc.vector.tensor_copy(chosen[:, :, :], picked[:, :, :]).then_inc(chosen_ready.sem, chosen_ready.one())
            dve.wait_ge(chosen_ready.sem, chosen_ready.at(i, 2))

        ahead, nb = Ahead(), [0]
        next_begun(ahead, nb)
        next_scaled(ahead)
        if moe:
            next_gate(ahead, nb)
            next_chosen(ahead)
        for signal in (step, b_emptied, norm.variance, src_ready, chosen_ready):
            signal.ahead_done()
        with turns(dve, B) as i:
            na, nb = [0], [0]
            then = then_in(i)
            emptyb = lambda emit: empty_b(i, nb, emit)
            if not moe:
                next_begun(i, nb)
            for what, e in order():
                if moe and (what, e) == ("up", experts - 2):
                    next_begun(i, nb)
                if (what, e) == (("up", experts - 1) if moe else ("down", 0)):
                    next_scaled(i)
                if moe and (what, e) == ("down", experts - 1):
                    next_gate(i, nb)
                if what == "up":
                    for l, layer in enumerate(layers(e)):
                        for m in range(layer.mb):
                            na[0] += 1
                            if layer.V is not None:
                                dve.wait_ge(a_emptied.sem, a_emptied.at(i, na[0]))
                                g = gates[:, nb[0] % 2, :]
                                arg = layer.v_arg(m) if layer.v_arg is not None else 1.0
                                emptyb(lambda bank: nc.vector.scalar_tensor_tensor(out=hidden[(e + l) % 2][:, m, :], in0=bank[:, :], scalar=arg, in1=g, op0=layer.v_op or ALU.mult, op1=ALU.mult))
                elif what == "chosen":
                    na[0] += 1
                    n = emptyb(lambda bank: nc.vector.tensor_tensor(acc[:, :, :], bank[:, :].rearrange("p (j d) -> p j d", j=NT), src[:, :, :], ALU.add))
                    dve.wait_ge(b_emptied.sem, b_emptied.at(i, n))
                elif moe:
                    def add(bank):
                        for j in range(NT):
                            part = bank[:, j * P:(j + 1) * P]
                            if e == 0 and not top1:
                                ins = nc.vector.tensor_scalar(acc[:, j, :], part, chosen[:, j, e:e + 1], None, ALU.mult)
                            else:
                                ins = nc.vector.scalar_tensor_tensor(out=acc[:, j, :], in0=part, scalar=chosen[:, j, e:e + 1], in1=acc[:, j, :], op0=ALU.mult, op1=ALU.add)
                        return ins
                    n = emptyb(add)
                    dve.wait_ge(b_emptied.sem, b_emptied.at(i, n))
                else:
                    def take(bank):
                        part = bank[:, :].rearrange("p (j d) -> p j d", j=NT)
                        if out_scale:
                            return nc.vector.tensor_tensor(acc[:, :, :], part, wide(w["out_scale"]), ALU.mult)
                        dst = tiles_of(c.y, i) if finish == "y" else acc[:, :, :]
                        return nc.vector.tensor_tensor(dst, part, tiles_of(c.y, i), ALU.add)
                    n = emptyb(take)
                    dve.wait_ge(b_emptied.sem, b_emptied.at(i, n))
            if moe:
                next_chosen(i)
            if tail_gain:
                then(norm.on_vector(nc, dve, i, lambda j: acc[:, j, :], lambda j: tmp[:, j, :]))
                then(nc.vector.tensor_tensor(tmp[:, :, :], tmp[:, :, :], wide(w["g2"]), ALU.mult))
                then(nc.vector.tensor_tensor(acc[:, :, :], tmp[:, :, :], wide(w["be2"]), ALU.add))
            if finish == "residual_norm":
                then(norm.on_vector(nc, dve, i, lambda j: acc[:, j, :], lambda j: tmp[:, j, :]))
                then(nc.vector.tensor_tensor(tiles_of(c.x, i), tiles_of(c.x, i), tmp[:, :, :], ALU.add))
            turn_done(b_emptied, step)
    ph.close()



def local_attention_phase(nc, c, name, w, first):
    heads, hd = 8, 64
    E = hd + 1
    inner = heads * hd
    BLK = inner // P
    SPAN = P + hd
    PAIRS = [(4 * (u // 2) + u % 2, 4 * (u // 2) + u % 2 + 2) for u in range(heads // 2)]
    both = [slice(h0, h1 + 1, 2) for h0, h1 in PAIRS]
    units = NT * len(PAIRS)
    ph = Phase(nc, name)
    S = ph.flag
    TURN = ["A0", "uT", "q0", "k0", "A1", "q1", "k1", "A2", "A3", "max", "q2", "k2",
            "B0", "tq0", "tk0", "B1", "tq1", "tk1", "q3", "k3", "v0", "c0",
            "B2", "tq2", "tk2", "v1", "c1", "B3", "tq3", "tk3", "v2", "v3", "c2", "c3", "out"]
    AHEAD = ["uT", "q0", "k0", "q1", "k1", "tq0", "tk0", "q2", "k2", "tq1", "tk1", "q3", "k3",
             "v0", "v1", "v2", "v3", "tq2", "tk2", "tq3", "tk3"]
    W_TURN = [what for what in TURN if what[0] not in "AB"]

    def w_n(i, what):
        return (AHEAD if i.ahead else W_TURN).index(what) + 1

    src = ph.sb("src", [P, NT, D])
    uT = ph.sb("uT", [P, T])
    raw = ph.sb("raw", [P, 2, 2, heads, hd])
    square = ph.sb("square", [P, 2, heads, hd])
    turned = ph.sb("turned", [P, 2, 2, heads, hd])
    inv = ph.sb("inv", [P, 2, 2 * heads])
    cosines = ph.sb("cosines", [P, NT, 2, hd])
    sines = ph.sb("sines", [P, NT, 2, hd])
    qT = ph.sb("qT", [P, BLK, T])
    kT = ph.sb("kT", [P, BLK, T])
    vx = ph.sb("vx", [P, NT, heads, E])
    negmax = ph.sb("negmax", [P, NT, heads])
    mrow = ph.sb("mrow", [heads, T])
    mT = ph.sb("mT", [P, T], F32R)
    pT = ph.sb("pT", [P, 2, heads, SPAN])
    rden = ph.sb("rden", [P, 2, heads])
    stepo = ph.sb("stepo", [P, NT, D])
    ctxt = c.ctx[:, 0:NT * BLK, :].rearrange("p (j b) d -> p j (b d)", j=NT)
    ctxT = c.ctx[:, NT * BLK:2 * NT * BLK, :].rearrange("p (b j) d -> p b (j d)", b=BLK)

    wbank = (c.bank[0], c.bank[1])
    sbank = (c.bank[2], c.bank[3])
    obank = ((c.bank[4], c.bank[5]), (c.bank[6], c.bank[7]))
    tables = S("tables", 0)
    src_ready = S("src_ready")
    w_filled, w_emptied = S("w_filled", len(W_TURN), len(AHEAD)), S("w_emptied", len(W_TURN), len(AHEAD))
    summed, inverted = S("summed", 2 * NT), S("inverted", NT)
    floored = S("floored", NT)
    sines_done, rotated = S("sines_done", NT), S("rotated", NT)
    scored_a, maxed = S("scored_a", units), S("maxed", units)
    m_copied = S("m_copied", 2)
    scored_b, exped = S("scored_b", units), S("exped", units)
    tile_done, o_taken = S("tile_done", NT), S("o_taken", NT)
    step = S("dve_step", 3 * NT, 2 * NT)
    stored = S("stored")
    norm = Norm(ph, 1, int(first))
    block = ph.block()

    def keys_of(q):
        return max(q * P - hd, 0), (q + 1) * P

    def queries_of(k):
        return k * P, min(k * P + SPAN, T)

    @block.sync
    def _(sp):
        load_next(sp, c)

    @block.tensor
    def _(pe):
        wait_weights(pe, c, w)

        def fill(i, what, emit):
            n = w_filled.n
            assert w_n(i, what) == n + 1, what
            if n > 1 or not i.ahead:
                pe.wait_ge(w_emptied.sem, w_emptied.at(i, n - 1))
            bank = wbank[(n + (0 if i.ahead else len(AHEAD))) % 2]
            emit(bank).then_inc(w_filled.sem, w_filled.one())

        def turn(tiles, width=P):
            def emit(bank):
                for k, t in enumerate(tiles):
                    ins = nc.tensor.transpose(bank[0:width, k * P:(k + 1) * P], t, c.ident[:, :])
                return ins
            return emit

        def out(bank):
            for j in range(NT):
                for b in range(BLK):
                    ins = nc.tensor.matmul(bank[:, j * P:(j + 1) * P], ctxT[:, b, j * P:(j + 1) * P], w["wo"][:, b * P:(b + 1) * P], start=b == 0, stop=b == BLK - 1)
            return ins

        def scores_a(i, q):
            lo, hi = keys_of(q)
            if q == 0:
                pe.wait_ge(w_emptied.sem, w_emptied.at(i, 0))
                pe.wait_ge(exped.sem, exped.at(i, 0))
            for u, pair in enumerate(PAIRS):
                n = q * len(PAIRS) + u
                pe.wait_ge(maxed.sem, maxed.at(i, max(n - 1, 0)))
                for side, h in enumerate(pair):
                    at = h % 2 * hd
                    dst = sbank[n % 2][:, side * (hi - lo):(side + 1) * (hi - lo)]
                    nc.tensor.matmul(dst, qT[at:at + hd, h // 2, q * P:(q + 1) * P], kT[at:at + hd, h // 2, lo:hi], start=True, stop=False)
                    ins = nc.tensor.matmul(dst, c.ident_bf[:, :], c.far_keys[:, SPAN - (hi - lo):SPAN], start=False, stop=True)
                ins.then_inc(scored_a.sem, scored_a.one())

        def scores_b(i, k, u):
            n = k * len(PAIRS) + u
            lo, hi = queries_of(k)
            pe.wait_ge(exped.sem, exped.at(i, max(n - 1, 0)))
            for side, h in enumerate(PAIRS[u]):
                at = h % 2 * hd
                dst = sbank[n % 2][:, side * (hi - lo):(side + 1) * (hi - lo)]
                nc.tensor.matmul(dst, kT[at:at + hd, h // 2, k * P:(k + 1) * P], qT[at:at + hd, h // 2, lo:hi], start=True, stop=False)
                nc.tensor.matmul(dst, c.pick[:, h, :], mT[:, lo:hi], start=False, stop=False)
                ins = nc.tensor.matmul(dst, c.ident_bf[:, :], c.far_queries[:, 0:hi - lo], start=False, stop=True)
            ins.then_inc(scored_b.sem, scored_b.one())

        def values(i, q, u):
            pe.wait_ge(exped.sem, exped.at(i, q * len(PAIRS) + u + 1))
            if u == 0:
                pe.wait_ge(o_taken.sem, o_taken.at(i, max(q - 1, 0)))
            for h in PAIRS[u]:
                dst = obank[q % 2][h // 4][:, h % 4 * E:(h % 4 + 1) * E]
                ins = nc.tensor.matmul(dst, pT[:, q % 2, h, 0:P], vx[:, q, h, :], start=True, stop=True)
                if q > 0:
                    ins = nc.tensor.matmul(dst[0:hd, :], pT[:, (q - 1) % 2, h, P:SPAN], vx[:, q - 1, h, :], start=False, stop=True, skip_group_check=True)
            if u == len(PAIRS) - 1:
                ins.then_inc(tile_done.sem, tile_done.one())

        def do(i, what):
            kind, j = what[:-1], int(what[-1]) if what[-1].isdigit() else 0
            if kind == "A":
                scores_a(i, j)
            elif kind == "B":
                if j == 0:
                    pe.wait_ge(m_copied.sem, m_copied.at(i, 2))
                for u in range(len(PAIRS)):
                    scores_b(i, j, u)
                    if u >= 1:
                        values(i, j, u - 1)
                values(i, j, len(PAIRS) - 1)
            elif what == "uT":
                pe.wait_ge(src_ready.sem, src_ready.at(i, 2))
                fill(i, what, turn([src[:, j, :] for j in range(NT)]))
            elif kind in ("q", "k", "v"):
                pe.wait_ge(w_emptied.sem, w_emptied.at(i, w_n(i, "uT")))
                part = "qkv".index(kind)
                fill(i, what, lambda bank: nc.tensor.matmul(bank[:, :], uT[:, j * P:(j + 1) * P], w["qkv"][:, part * inner:(part + 1) * inner], start=True, stop=True))
            elif kind in ("tq", "tk"):
                pe.wait_ge(rotated.sem, rotated.at(i, NT + j + 1))
                flat = turned[:, j % 2, int(kind == "tk"), :, :].rearrange("p h d -> p (h d)")
                fill(i, what, turn([flat[:, b * P:(b + 1) * P] for b in range(BLK)]))
            elif what == "max":
                pe.wait_ge(maxed.sem, maxed.at(i, units))
                fill(i, what, turn([negmax[:, q, :] for q in range(NT)], heads))
            elif kind == "c":
                pe.wait_ge(o_taken.sem, o_taken.at(i, j + 1))
                fill(i, what, turn([ctxt[:, j, b * P:(b + 1) * P] for b in range(BLK)]))
            else:
                pe.wait_ge(w_emptied.sem, w_emptied.at(i, w_n(i, "c3")))
                fill(i, what, out)

        ahead = Ahead()
        for what in AHEAD:
            do(ahead, what)
        w_filled.ahead_done()
        with turns(pe, B) as i:
            for what in TURN:
                do(i, what)
            turn_done(w_filled, scored_a, scored_b, tile_done)

    @block.scalar
    def _(act):

        def empty(i, what, *emits):
            n = w_emptied.n
            assert w_n(i, what) == n + 1, what
            act.wait_ge(w_filled.sem, w_filled.at(i, n + 1))
            bank = wbank[(n + (0 if i.ahead else len(AHEAD))) % 2]
            for emit in emits:
                ins = emit(bank)
            ins.then_inc(w_emptied.sem, w_emptied.one())

        def by_head(bank):
            return bank[:, :].rearrange("p (h d) -> p h d", h=heads)

        def do(i, what):
            kind, j = what[:-1], int(what[-1]) if what[-1].isdigit() else 0
            if what == "uT":
                empty(i, what, lambda bank: nc.scalar.copy(uT[0:H2, :], bank[0:H2, :]),
                      lambda bank: nc.scalar.copy(uT[H2:P, 1:T], bank[H2:P, 0:T - 1]))
            elif kind in ("q", "k"):
                side = int(kind == "k")
                if side == 0 and not (i.ahead and j < 2):
                    act.wait_ge(rotated.sem, rotated.at(i, NT + j - 1))
                if not (i.ahead and j == 0):
                    act.wait_ge(summed.sem, summed.at(i, 2 * (NT + j - 1) + side + 1))
                empty(i, what, lambda bank: nc.scalar.copy(raw[:, j % 2, side, :, :], by_head(bank)),
                      lambda bank: nc.scalar.activation(square[:, side, :, :], by_head(bank), ACT.Square))
            elif kind == "v":
                if not i.ahead:
                    act.wait_ge(tile_done.sem, tile_done.at(i, min(j + 2, NT)))
                empty(i, what, lambda bank: nc.scalar.copy(vx[:, j, :, 0:hd], by_head(bank)))
            elif kind in ("tq", "tk"):
                dst = qT if kind == "tq" else kT
                empty(i, what, lambda bank: nc.scalar.copy(dst[:, :, j * P:(j + 1) * P], bank[:, :].rearrange("p (b n) -> p b n", b=BLK)))
            elif what == "max":
                act.wait_ge(m_copied.sem, m_copied.at(i, 0))
                empty(i, what, lambda bank: nc.scalar.copy(mrow[:, :], bank[0:heads, :]))
            elif kind == "B":
                for u in range(len(PAIRS)):
                    n = j * len(PAIRS) + u
                    lo, hi = queries_of(j)
                    if u == 0:
                        act.wait_ge(tile_done.sem, tile_done.at(i, max(j - 1, 0)))
                    act.wait_ge(scored_b.sem, scored_b.at(i, n + 1))
                    nc.scalar.activation(pT[:, j % 2, both[u], 0:hi - lo], sbank[n % 2][:, 0:2 * (hi - lo)].rearrange("p (s n) -> p s n", s=2), ACT.Exp).then_inc(exped.sem, exped.one())
            elif kind == "c":
                empty(i, what, lambda bank: nc.scalar.copy(ctxT[:, :, j * P:(j + 1) * P], bank[:, :].rearrange("p (b n) -> p b n", b=BLK)))
            elif what == "out":
                act.wait_ge(stored.sem, stored.at(i, 0))
                empty(i, what, lambda bank: nc.scalar.copy(stepo[:, :, :], bank[:, :].rearrange("p (j d) -> p j d", j=NT)))

        act.wait_ge(tables.sem, 3)
        for what in AHEAD:
            do(Ahead(), what)
        w_emptied.ahead_done()
        with turns(act, B) as i:
            for what in TURN:
                do(i, what)
            turn_done(w_emptied, exped)

    @block.gpsimd
    def _(pool):
        pool.wait_ge(tables.sem, 3)

        def rotate(i):
            if first:
                norm.on_gpsimd(nc, pool, c, i)
            for j in range(NT):
                pool.wait_ge(floored.sem, floored.at(i, NT + j + 1))
                nc.gpsimd.tensor_tensor(inv[:, j % 2, :], inv[:, j % 2, :], c.minus_half16[:, :], ALU.pow).then_inc(inverted.sem, inverted.one())
                sin = sines[:, j, :, :].unsqueeze(2).to_broadcast([P, 2, heads, hd])
                nc.gpsimd.tensor_tensor(turned[:, j % 2, :, :, 0:hd // 2], raw[:, j % 2, :, :, hd // 2:hd], sin[:, :, :, 0:hd // 2], ALU.mult)
                nc.gpsimd.tensor_tensor(turned[:, j % 2, :, :, hd // 2:hd], raw[:, j % 2, :, :, 0:hd // 2], sin[:, :, :, hd // 2:hd], ALU.mult).then_inc(sines_done.sem, sines_done.one())

        rotate(Ahead())
        for signal in (norm.eps_added, norm.rstd_ready, inverted, sines_done):
            signal.ahead_done()
        with turns(pool, B) as i:
            rotate(i)
            turn_done(inverted, sines_done)

    @block.vector
    def _(dve):
        wait_weights(dve, c, w)
        nc.vector.memset(vx[:, :, :, hd:E], 1.0)
        nc.vector.memset(mT[:, :].bitcast(F32), 0.0)
        nc.vector.memset(inv[:, :, :], 1.0)
        nc.vector.memset(uT[H2:P, 0:1], 0.0).then_inc(tables.sem, tables.one())
        rows = lambda t: t.rearrange("p (j s d) -> p j s d", j=NT, s=2)
        gains = lambda t: t.rearrange("p (s d) -> p s d", s=2).unsqueeze(1).to_broadcast([P, NT, 2, hd])
        nc.vector.tensor_tensor(cosines[:, :, :, :], rows(w["cosines"]), gains(w["gains"]), ALU.mult).then_inc(tables.sem, tables.one())
        nc.vector.tensor_tensor(sines[:, :, :, :], rows(w["sines"]), gains(w["gains_turned"]), ALU.mult).then_inc(tables.sem, tables.one())
        dve.wait_ge(tables.sem, 3)

        def then_in(i):
            def then(ins):
                ins.then_inc(step.sem, step.one())
                dve.wait_ge(step.sem, step.at(i, step.n))
            return then

        def next_source(i):
            if not i.ahead:
                dve.wait_ge(w_filled.sem, w_filled.at(i, 0))
            if first:
                norm.scaled(nc, dve, i, lambda j: i.next_tile(c.x, j), lambda j: src[:, j, :]).then_inc(src_ready.sem, src_ready.one())
                dve.wait_ge(src_ready.sem, src_ready.at(i, 2))
                nc.vector.tensor_copy(i.next_tiles(c.y), src[:, :, :])
            else:
                nc.vector.tensor_copy(src[:, :, :], i.next_tiles(c.y)).then_inc(src_ready.sem, src_ready.one())

        def sum_squares(i, j):
            if j > 1 and not i.ahead:
                dve.wait_ge(w_filled.sem, w_filled.at(i, w_n(i, f"tk{j - 2}")))
            for side, what in enumerate((f"q{j}", f"k{j}")):
                dve.wait_ge(w_emptied.sem, w_emptied.at(i, w_n(i, what)))
                nc.vector.tensor_reduce(inv[:, j % 2, side * heads:(side + 1) * heads], square[:, side, :, :], AX.X, ALU.add).then_inc(summed.sem, summed.one())
            dve.wait_ge(summed.sem, summed.at(i, 2 * (NT + j + 1)))
            nc.vector.tensor_scalar(inv[:, j % 2, :], inv[:, j % 2, :], 1e-24, None, ALU.max).then_inc(floored.sem, floored.one())

        def rotate(i, j, parts=(0, 1, 2)):
            then = then_in(i)
            cos = cosines[:, j, :, :].unsqueeze(2).to_broadcast([P, 2, heads, hd])
            r = raw[:, j % 2, :, :, :]
            t = turned[:, j % 2, :, :, :]
            if 0 in parts:
                dve.wait_ge(sines_done.sem, sines_done.at(i, NT + j + 1))
                then(nc.vector.tensor_tensor(r, r, cos, ALU.mult))
            if 1 in parts:
                then(nc.vector.tensor_tensor(t, t, r, ALU.add))
            if 2 in parts:
                t = t.rearrange("p s h d -> p (s h) d")
                nc.vector.tensor_tensor(t, t, inv[:, j % 2, :].unsqueeze(2).to_broadcast([P, 2 * heads, hd]), ALU.mult).then_inc(rotated.sem, rotated.one())

        def reduce_a(i, n):
            q, u = n // len(PAIRS), n % len(PAIRS)
            lo, hi = keys_of(q)
            dve.wait_ge(scored_a.sem, scored_a.at(i, n + 1))
            nc.vector.tensor_reduce(negmax[:, q, both[u]], sbank[n % 2][:, 0:2 * (hi - lo)].rearrange("p (s n) -> p s n", s=2), AX.X, ALU.max, negate=True).then_inc(maxed.sem, maxed.one())

        def take(i, q):
            dve.wait_ge(tile_done.sem, tile_done.at(i, q + 1))
            for b in range(2):
                o = obank[q % 2][b][:, 0:4 * E].rearrange("p (h e) -> p h e", e=E)
                ins = nc.vector.reciprocal(rden[:, q % 2, 4 * b:4 * b + 4], o[:, :, hd])
            then_in(i)(ins)
            for b in range(2):
                o = obank[q % 2][b][:, 0:4 * E].rearrange("p (h e) -> p h e", e=E)
                dst = ctxt[:, q, b * 4 * hd:(b + 1) * 4 * hd].rearrange("p (h e) -> p h e", e=hd)
                ins = nc.vector.tensor_tensor(dst, o[:, :, 0:hd], rden[:, q % 2, 4 * b:4 * b + 4].unsqueeze(2).to_broadcast([P, 4, hd]), ALU.mult)
            ins.then_inc(o_taken.sem, o_taken.one())

        ahead = Ahead()
        if first:
            norm.statistics(nc, dve, lambda j: ahead.next_tile(c.x, j))
        next_source(ahead)
        for j in range(NT):
            sum_squares(ahead, j)
            rotate(ahead, j)
        for signal in (step, norm.variance, src_ready, summed, floored, rotated):
            signal.ahead_done()
        with turns(dve, B) as i:
            if first:
                norm.statistics(nc, dve, lambda j: i.next_tile(c.x, j))
            for n in range(units):
                if n == 2:
                    next_source(i)
                if n in (len(PAIRS) + 2, 2 * len(PAIRS) + 2):
                    sum_squares(i, n // len(PAIRS) - 1)
                if n - 3 * len(PAIRS) in (1, 2, 3):
                    rotate(i, 0, (n - 3 * len(PAIRS) - 1,))
                reduce_a(i, n)
            dve.wait_ge(w_emptied.sem, w_emptied.at(i, w_n(i, "max")))
            nc.vector.tensor_copy(mT[0:heads, :], mrow[:, :]).then_inc(m_copied.sem, m_copied.one())
            dve.wait_ge(m_copied.sem, m_copied.at(i, 1))
            nc.vector.tensor_tensor(mT[32:32 + heads, :], mrow[:, :], mT[0:heads, :].bitcast(F32), ALU.subtract).then_inc(m_copied.sem, m_copied.one())
            rotate(i, 1)
            take(i, 0)
            sum_squares(i, 2)
            take(i, 1)
            rotate(i, 2)
            sum_squares(i, 3)
            take(i, 2)
            rotate(i, 3)
            take(i, 3)
            dve.wait_ge(w_emptied.sem, w_emptied.at(i, w_n(i, "out")))
            nc.vector.tensor_tensor(tiles_of(c.y, i), stepo[:, :, :], tiles_of(c.y, i), ALU.add).then_inc(stored.sem, stored.one())
            turn_done(step, maxed, m_copied, o_taken, summed, rotated, floored)
    ph.close()



def linear_attention_phase(nc, c, name, w):
    heads, hd = 16, 8
    F = D + heads
    W_USES = 4
    ph = Phase(nc, name)
    S = ph.flag
    src = ph.sb("src", [P, NT, D])
    uT, qT = ph.sb("uT", [P, T]), ph.sb("qT", [P, T])
    ktok = ph.sb("ktok", [P, NT, D])
    vtok = ph.sb("vtok", [P, NT, D + 1])
    kv = ph.sb("kv", [P, F])
    kv_sum = ph.sb("kv_sum", [P, 1])
    den = ph.sb("den", [P, NT, heads])
    acc, tmp = ph.sb("acc", [P, NT, D]), ph.sb("tmp", [P, NT, D])
    wbank = (c.bank[0], c.bank[1])
    kvbank, obank = c.bank[2], (c.bank[3], c.bank[4])
    src_ready = S("src_ready")
    w_filled, w_emptied = S("w_filled", W_USES, 1), S("w_emptied", W_USES, 1)
    kv_summed, kv_ready = S("kv_summed"), S("kv_ready", 2)
    context, o_taken = S("context"), S("o_taken")
    ready = S("ready", 0)
    step = S("dve_step", 9)
    norm = Norm(ph, 3, 1)
    block = ph.block()

    @block.sync
    def _(sp):
        load_next(sp, c)

    @block.tensor
    def _(pe):
        wait_weights(pe, c, w)
        pe.wait_ge(ready.sem, 1)

        def fill(i, emit):
            n = w_filled.n
            if not i.ahead:
                pe.wait_ge(w_emptied.sem, w_emptied.at(i, max(n - 1, 0)))
            emit(wbank[(n + (not i.ahead)) % 2]).then_inc(w_filled.sem, w_filled.one())

        def next_turned(i):
            pe.wait_ge(src_ready.sem, src_ready.at(i, 2))

            def turn(bank):
                for j in range(NT):
                    ins = nc.tensor.transpose(bank[:, j * P:(j + 1) * P], src[:, j, :], c.ident[:, :])
                return ins
            fill(i, turn)

        def tokens(weights, b):
            def emit(bank):
                for j in range(NT):
                    dst = bank[:, j * P:(j + 1) * P]
                    nc.tensor.matmul(dst, uT[:, j * P:(j + 1) * P], weights, start=True, stop=False)
                    ins = nc.tensor.matmul(dst, c.ones[0:1, :], b, start=False, stop=True)
                return ins
            return emit

        next_turned(Ahead())
        w_filled.ahead_done()
        with turns(pe, B) as i:
            pe.wait_ge(w_emptied.sem, w_emptied.at(i, 0))
            fill(i, tokens(w["wk"], w["bk_b"]))
            fill(i, tokens(w["wv"], w["bv"]))
            fill(i, lambda bank: nc.tensor.matmul(bank[:, :], w["wq"], uT[:, :], start=True, stop=True))
            pe.wait_ge(w_emptied.sem, w_emptied.at(i, 2))
            pe.wait_ge(kv_ready.sem, kv_ready.at(i, 0))
            for j in range(NT):
                ins = nc.tensor.matmul(kvbank[:, 0:D + 1], ktok[:, j, :], vtok[:, j, :], start=j == 0, stop=j == NT - 1)
            ins.then_inc(kv_summed.sem, kv_summed.one())
            pe.wait_ge(kv_ready.sem, kv_ready.at(i, 2))
            pe.wait_ge(w_emptied.sem, w_emptied.at(i, 3))
            pe.wait_ge(o_taken.sem, o_taken.at(i, 0))
            for j in range(NT):
                ins = nc.tensor.matmul(obank[j // 2][:, j % 2 * F:(j % 2 + 1) * F], qT[:, j * P:(j + 1) * P], kv[:, :], start=True, stop=True)
            ins.then_inc(context.sem, context.one())
            next_turned(i)
            turn_done(w_filled, kv_summed, context)

    @block.scalar
    def _(act):
        wait_weights(act, c, w)

        def empty(i, emit):
            n = w_emptied.n
            act.wait_ge(w_filled.sem, w_filled.at(i, n + 1))
            emit(wbank[(n + (not i.ahead)) % 2]).then_inc(w_emptied.sem, w_emptied.one())

        empty(Ahead(), lambda bank: nc.scalar.copy(uT[:, :], bank[:, :]))
        w_emptied.ahead_done()
        with turns(act, B) as i:
            empty(i, lambda bank: nc.scalar.activation(ktok[:, :, :], bank[:, :].rearrange("p (j d) -> p j d", j=NT), ACT.Relu))
            empty(i, lambda bank: nc.scalar.copy(vtok[:, :, 0:D], bank[:, :].rearrange("p (j d) -> p j d", j=NT)))
            empty(i, lambda bank: nc.scalar.activation(qT[:, :], bank[:, :], ACT.Relu, bias=w["bq"]))
            empty(i, lambda bank: nc.scalar.copy(uT[:, :], bank[:, :]))
            turn_done(w_emptied)

    @block.gpsimd
    def _(pool):
        norm.on_gpsimd(nc, pool, c, Ahead())
        for signal in (norm.eps_added, norm.rstd_ready):
            signal.ahead_done()
        with turns(pool, B) as i:
            for _ in range(3):
                norm.on_gpsimd(nc, pool, c, i)

    @block.vector
    def _(dve):
        wait_weights(dve, c, w)
        nc.vector.memset(vtok[:, :, D:D + 1], 1.0).then_inc(ready.sem, ready.one())

        def next_source(i):
            if not i.ahead:
                dve.wait_ge(w_filled.sem, w_filled.at(i, 0))
            norm.on_vector(nc, dve, i, lambda j: i.next_tile(c.x, j), lambda j: src[:, j, :]).then_inc(src_ready.sem, src_ready.one())
            dve.wait_ge(src_ready.sem, src_ready.at(i, 2))
            nc.vector.tensor_copy(i.next_tiles(c.y), src[:, :, :])

        next_source(Ahead())
        for signal in (norm.variance, src_ready):
            signal.ahead_done()
        with turns(dve, B) as i:
            def then(ins):
                ins.then_inc(step.sem, step.one())
                dve.wait_ge(step.sem, step.at(i, step.n))

            dve.wait_ge(kv_summed.sem, kv_summed.at(i, 1))
            dve.wait_ge(context.sem, context.at(i, 0))
            nc.vector.tensor_tensor(kv[:, 0:D], kvbank[:, 0:D], w["same_head"], ALU.mult).then_inc(kv_ready.sem, kv_ready.one())
            then(nc.vector.tensor_copy(kv_sum[:, :], kvbank[:, D:D + 1]))
            nc.vector.tensor_scalar(kv[:, D:F], w["head_of"], kv_sum[:, 0:1], None, ALU.mult).then_inc(kv_ready.sem, kv_ready.one())
            dve.wait_ge(context.sem, context.at(i, 1))
            for b in range(2):
                o = obank[b][:, 0:2 * F].rearrange("p (j f) -> p j f", j=2)
                ins = nc.vector.tensor_scalar(den[:, 2 * b:2 * b + 2, :], o[:, :, D:F], 1e-6, None, ALU.max)
            then(ins)
            then(nc.vector.reciprocal(den[:, :, :], den[:, :, :]))
            for b in range(2):
                o = obank[b][:, 0:2 * F].rearrange("p (j f) -> p j f", j=2)[:, :, 0:D].rearrange("p j (h e) -> p j h e", h=heads)
                ins = nc.vector.tensor_tensor(acc[:, 2 * b:2 * b + 2, :].rearrange("p j (h e) -> p j h e", h=heads), o,
                                              den[:, 2 * b:2 * b + 2, :].unsqueeze(3).to_broadcast([P, 2, heads, hd]), ALU.mult)
            ins.then_inc(o_taken.sem, o_taken.one())
            dve.wait_ge(o_taken.sem, o_taken.at(i, 1))
            next_source(i)
            then(nc.vector.tensor_tensor(acc[:, :, :], acc[:, :, :], tiles_of(c.y, i), ALU.add))
            then(norm.on_vector(nc, dve, i, lambda j: acc[:, j, :], lambda j: tmp[:, j, :]))
            then(nc.vector.tensor_tensor(tmp[:, :, :], tmp[:, :, :], wide(w["gamma"]), ALU.mult))
            then(nc.vector.tensor_tensor(acc[:, :, :], tmp[:, :, :], wide(w["beta"]), ALU.add))
            then(norm.on_vector(nc, dve, i, lambda j: acc[:, j, :], lambda j: tmp[:, j, :]))
            then(nc.vector.tensor_tensor(tiles_of(c.x, i), tiles_of(c.x, i), tmp[:, :, :], ALU.add))
            turn_done(step, src_ready, kv_ready, o_taken, norm.variance)
    ph.close()


def reorder_phase(nc, c, name, by_position):
    ph = Phase(nc, name)
    written, read = ph.flag("written", 0), ph.flag("read", 0)
    block = ph.block()
    natural = c.scratch.rearrange("b (j p) d -> p (b j) d", p=P)

    @block.sync
    def _(sp):
        parts = [(c.x[:, k:k + 2 * NT, :], natural[:, k:k + 2 * NT, :]) for k in range(0, TILES, 2 * NT)]
        grouped = [(c.x[b::B, 0:TILES, :], c.scratch[b].rearrange("(g t) d -> t g d", t=P // B)) for b in range(B)]
        first, then = (parts, grouped) if by_position else (grouped, parts)
        for tile, dram in first:
            sp.dma_start(dram, tile).then_inc(written.sem, 16)
        sp.wait_ge(written.sem, 16 * len(first))
        for tile, dram in then:
            sp.dma_start(tile, dram).then_inc(read.sem, 16)
        sp.wait_ge(read.sem, 16 * len(then))
    ph.close()



class Pack:

    def __init__(self):
        self.names, self.cols, self.host = {}, 0, []

    def add(self, name, n, lay):
        self.names[name] = (self.cols, n)
        self.cols += n
        self.host.append((n, lay))


def rows_to(a, n=P):
    a = np.asarray(a)
    if a.ndim == 1:
        a = a[None, :]
    out = np.zeros((n, a.shape[1]), a.dtype)
    out[:a.shape[0]] = a
    return out


def blocks(a):
    a = np.asarray(a)
    k = a.shape[0] // P
    return a.reshape(k, P, -1).transpose(1, 0, 2).reshape(P, -1)


def column(v):
    return np.asarray(v).reshape(-1, P).T


def stack_index(heads):
    hd = D // heads
    r = np.arange(NQ * D)
    return r // (NQ * hd) * hd + r % hd


def stack_masks(heads):
    part = np.arange(P) % (NQ * D // heads) // (D // heads)
    qlow, klow = part // 2, part % 2
    out = np.stack([1 - 2 * qlow, qlow, 1 - 2 * klow, klow], 1)
    return out.astype(np.float32)


def attention_pack(heads, scale, wq, wk, wv, bq=None, bk=None, bv=None):
    hd = D // heads
    pk = Pack()
    idx = stack_index(heads)
    pk.add("qk", 2 * NQ * P, lambda a: np.concatenate([wq(a)[:, idx], wk(a)[:, idx]], 1))
    pk.add("v", P, wv)
    pk.add("masks", 4, lambda a: stack_masks(heads))
    pk.add("maskq_scaled", 1, lambda a: stack_masks(heads)[:, 1:2] * np.float32(scale))
    if bq is not None:
        pk.add("bqk", 2 * NQ, lambda a: np.concatenate([column(bq(a)[idx]), column(bk(a)[idx])], 1))
        pk.add("bv", P, lambda a: rows_to(bv(a)))
    return pk


def views(pk, region, need):
    w = {n: region[:, o:o + m] for n, (o, m) in pk.names.items()}
    w["need"] = need
    for n in ("mod", "am", "bd"):
        if n in pk.names:
            w[n] = (lambda o, rows: lambda g: region[0:rows, o + g * P:o + (g + 1) * P])(pk.names[n][0], 16 if n == "am" else P)
    if "cons" in w:
        w["cons"] = w["cons"][0:16, :]
    if "qk" in w:
        o = pk.names["qk"][0]
        w["qk"] = lambda g: region[:, o + g * P:o + (g + 1) * P]
        m = pk.names["masks"][0]
        w["maskq"] = (region[:, m:m + 1], region[:, m + 1:m + 2])
        w["maskk"] = (region[:, m + 2:m + 3], region[:, m + 3:m + 4])
    for n in list(w):
        if n == "bv" or n.endswith("_b"):
            w[n] = w[n][0:1, :]
    return w


def wait_weights(eng, c, w):
    eng.wait_ge(c.loaded[w["need"]], 16)


CONSTS = Pack()
CONSTS.add("ident", P, lambda a: np.eye(P, dtype=np.float32))
CONSTS.add("later_keys", P, lambda a: np.triu(np.full((P, P), MASKED, np.float32), 1))
CONSTS.add("earlier_queries", P, lambda a: np.tril(np.full((P, P), MASKED, np.float32), -1))


def pick_rows():
    out = np.zeros((P, 8, P), np.float32)
    for h in range(8):
        out[h, h] = out[32 + h, h] = 1
    return out.reshape(P, -1)


CONSTS.add("other_groups", P, lambda a: np.where(np.arange(P)[:, None] // B == np.arange(P)[None, :] // B, 0, MASKED).astype(np.float32))
_q, _k = np.arange(P)[:, None], np.arange(P + 64)[None, :]
CONSTS.add("far_keys", P + 64, lambda a: np.where((_k >= _q) & (_k <= _q + 64), 0, MASKED).astype(np.float32))
CONSTS.add("far_queries", P + 64, lambda a: np.where((_k >= _q) & (_k <= _q + 64), 0, MASKED).astype(np.float32))
CONSTS.add("down8", 8, lambda a: np.tile(np.arange(8, 0, -1, dtype=np.float32), (P, 1)))
CONSTS.add("shift", 2 * P, lambda a: np.concatenate([np.eye(P, k=1, dtype=np.float32), np.eye(P, k=1 - P, dtype=np.float32)], 1))
CONSTS.add("pick", 8 * P, lambda a: pick_rows())


def setup_phase(nc, c, consts, x, pk0, w0):
    ph = Phase(nc, "setup")
    raw = ph.sb("raw", [P, CONSTS.cols])
    came, cast = ph.flag("came", 0), ph.flag("cast", 0)
    block = ph.block()

    def part(n):
        o, m = CONSTS.names[n]
        return raw[:, o:o + m]

    @block.sync
    def _(sp):
        sp.dma_start(raw[:, :], consts).then_inc(came.sem, 16)
        for b in range(0, TILES, NT * 2):
            sp.dma_start(c.x[:, b:b + NT * 2, :], x[:, b:b + NT * 2, :]).then_inc(came.sem, 16)
        load_weights(sp, c, pk0, w0)
        sp.wait_ge(came.sem, 80)

    @block.vector
    def _(dve):
        nc.vector.memset(c.ones[:, :], 1.0)
        nc.vector.memset(c.x[:, TILES:, :], 0.0)
        nc.vector.memset(c.ctx[:, TILES:, :], 0.0)
        nc.vector.memset(c.y[:, TILES:, :], 0.0)
        nc.vector.memset(c.minus_half[:, :], -0.5)
        nc.vector.memset(c.eps[:, :], EPS)
        dve.wait_ge(came.sem, 80)
        nc.vector.tensor_copy(c.ident[:, :], part("ident"))
        nc.vector.tensor_copy(c.ident_bf[:, :], part("ident"))
        nc.vector.tensor_copy(c.later_keys[:, :], part("later_keys"))
        nc.vector.tensor_copy(c.earlier_queries[:, :], part("earlier_queries"))
        nc.vector.tensor_copy(c.other_groups[:, :], part("other_groups"))
        nc.vector.memset(c.minus_half16[:, :], -0.5)
        nc.vector.tensor_copy(c.far_keys[:, :], part("far_keys"))
        nc.vector.tensor_copy(c.far_queries[:, :], part("far_queries"))
        nc.vector.tensor_copy(c.down8[:, :], part("down8"))
        nc.vector.tensor_copy(c.shift[:, :, :], part("shift").rearrange("p (a n) -> p a n", a=2))
        nc.vector.tensor_copy(c.pick[:, :, :], part("pick").rearrange("p (h n) -> p h n", h=8)).then_inc(cast.sem, 1)
        dve.wait_ge(cast.sem, 1)
    ph.close()


def load_weights(sp, c, pk, src):
    n_load = c.region_turn
    n = n_load % 2
    c.region_turn += 1
    sp.dma_start(c.region[n][:, 0:pk.cols], src).then_inc(c.loaded[n_load], 16)


def load_next(sp, c):
    if c.next is not None:
        load_weights(sp, c, *c.next)


def store_phase(nc, c, out):
    ph = Phase(nc, "store")
    stored = ph.flag("stored", 0)
    block = ph.block()

    @block.sync
    def _(sp):
        for b in range(0, TILES, NT * 2):
            sp.dma_start(out[:, b:b + NT * 2, :], c.x[:, b:b + NT * 2, :]).then_inc(stored.sem, 16)
        sp.wait_ge(stored.sem, 64)
    ph.close()


def rotary_tables():
    hd, window = 64, 64
    half = np.arange(0, hd, 2, dtype=np.float32)
    t = np.arange(T, dtype=np.float32)
    freqs = t[:, None] * (np.float32(1) / np.float32(10000) ** (half / np.float32(hd)))[None]
    base = (half + np.float32(0.4 * hd)) / np.float32(1.4 * hd)
    power = (t - T // 2) / np.float32(window // 2)
    scale = base[None, :] ** power[:, None]
    out = []
    for f, sign in ((np.cos(freqs), 1.0), (np.sin(freqs), -1.0)):
        q = np.concatenate([sign * f * scale, f * scale], 1) * 8.0
        k = np.concatenate([sign * f / scale, f / scale], 1)
        tab = np.stack([q, k], 1).astype(np.float32)
        out.append(tab.reshape(NT, P, 2, hd).transpose(1, 0, 2, 3).reshape(P, -1))
    return out


def phase_list():
    T_ = lambda n: (lambda a: np.asarray(a[n]).T)
    V_ = lambda n: (lambda a: np.asarray(a[n]))
    out = []
    f32 = lambda v: float(np.float32(v))
    W4 = lambda k: (lambda a: np.asarray(a["L0_attn_W_qkvf"])[k * D:(k + 1) * D].T)

    def conv_blocks(a):
        conv = np.asarray(a["L0_attn_W_conv"])
        o = np.zeros((16, 8, 4, 16, 8), np.float32)
        for h in range(16):
            o[h, :, :, h, :] = conv.transpose(0, 2, 1)
        return o.reshape(D, 4 * D)
    sc0 = f32(8 ** -0.5)
    pk = attention_pack(16, sc0, W4(0), W4(1), W4(2))
    pk.add("q", P, W4(0))
    pk.add("wf", P, lambda a: np.asarray(a["L0_attn_W_qkvf"])[3 * D:])
    pk.add("wkT", P, W4(1))
    pk.add("wvT", P, W4(2))
    pk.add("bd", 4 * P, conv_blocks)
    pk.add("gain", 1, lambda a: column(a["L0_attn_ln1_g"]))
    pk.add("shift", 1, lambda a: column(a["L0_attn_ln1_b"]))
    pk.add("proj", P, T_("L0_attn_W_proj"))
    out.append(("L0a", pk, lambda nc, c, w: attention_phase(nc, c, "l0a", w, 16, sc0, causal=True, affine=True, future=True, out_steps=("proj",), finish="y")))
    pk = Pack()
    pk.add("ff1", 4 * P, V_("L0_attn_W_ff1"))
    pk.add("ff2", 4 * P, lambda a: blocks(a["L0_attn_W_ff2"]))
    pk.add("gain", 1, lambda a: column(a["L0_attn_ln2_g"]))
    pk.add("shift", 1, lambda a: column(a["L0_attn_ln2_b"]))

    def l0g(nc, c, w):
        blk = lambda t, k: t[:, k * P:(k + 1) * P]
        L = [Layer(1, 4, lambda k, m: blk(w["ff1"], m), ACT.Gelu)]
        mlp_phase(nc, c, "l0g", w, lambda e: L, lambda e: (4, lambda k: blk(w["ff2"], k)), source="y", affine=True)
    out.append(("L0g", pk, l0g))
    for d in range(2):
        G = lambda n, d=d: (lambda a: np.asarray(a["L0_ffn_" + n])[d])
        pk = Pack()
        pk.add("qkv", 1536, G("wqkv"))
        pk.add("wo", 4 * P, (lambda g: lambda a: blocks(g(a)))(G("wo")))
        pk.add("cosines", 4 * P, lambda a: rotary_tables()[0])
        pk.add("sines", 4 * P, lambda a: rotary_tables()[1])
        pk.add("gains", P, (lambda d: lambda a: np.broadcast_to(np.concatenate([a["L0_ffn_q_scale"][d], a["L0_ffn_k_scale"][d]]), (P, P)))(d))
        pk.add("gains_turned", P, (lambda d: lambda a: np.broadcast_to(np.concatenate([np.roll(a["L0_ffn_q_scale"][d], 32), np.roll(a["L0_ffn_k_scale"][d], 32)]), (P, P)))(d))
        out.append((f"L0w{d}", pk, (lambda d: lambda nc, c, w: local_attention_phase(nc, c, f"l0w{d}", w, first=d == 0))(d)))
        pk = Pack()
        HID, HB = 341, 3

        def padded(v, n=HB * P):
            return np.concatenate([v, np.zeros(v.shape[:-1] + (n - v.shape[-1],), v.dtype)], -1)
        pk.add("wa", HB * P, (lambda g: lambda a: padded(g(a)[:, :HID]))(G("w1")))
        pk.add("wg", HB * P, (lambda g: lambda a: padded(g(a)[:, HID:]))(G("w1")))
        pk.add("ba", HB, (lambda g: lambda a: column(padded(g(a)[:HID])))(G("b1")))
        pk.add("bg", HB, (lambda g: lambda a: column(padded(g(a)[HID:])))(G("b1")))
        pk.add("w2", HB * P, (lambda g: lambda a: blocks(padded(g(a).T).T))(G("w2")))
        pk.add("final_b", P, (lambda g: lambda a: rows_to(g(a)))(G("b2")))
        pk.add("gain", 1, (lambda g: lambda a: column(g(a)))(G("ln_g")))
        pk.add("shift", 1, (lambda g: lambda a: column(g(a)))(G("ln_b")))

        def l0h(nc, c, w, d=d):
            blk = lambda t, k: t[:, k * P:(k + 1) * P]
            L = [Layer(1, 3, lambda k, m: blk(w["wg"], m), ACT.Gelu, bias=lambda m: w["bg"][:, m:m + 1],
                       V=lambda k, m: blk(w["wa"], m), v_op=ALU.add, v_arg=lambda m: w["ba"][:, m:m + 1])]
            mlp_phase(nc, c, f"l0h{d}", w, lambda e: L, lambda e: (3, lambda k: blk(w["w2"], k)), source="y", affine=True,
                      shifted=True, finish="residual_norm" if d else "y")
        out.append((f"L0h{d}", pk, l0h))
    fl = lambda n: (lambda a: np.asarray(a[n]).reshape(D, D).T)
    fb = lambda n: (lambda a: np.asarray(a[n]).reshape(D))
    sc = float(np.float32(1 / np.sqrt(8.0)))
    pk = attention_pack(16, sc, fl("L1_attn_Wq"), fl("L1_attn_Wk"), fl("L1_attn_Wv"), fb("L1_attn_bq"), fb("L1_attn_bk"), fb("L1_attn_bv"))
    out.append(("L1a", pk, lambda nc, c, w: attention_phase(nc, c, "l1a", w, 16, sc, causal=True, bias=True)))
    pk = Pack()
    for n in ("w1", "w2"):
        pk.add(n, 4 * P, T_(f"L1_ffn_{n}_w"))
        pk.add(n + "s", 4, (lambda n: lambda a: column(a[f"L1_ffn_{n}_s"]))(n))
    for n in ("h1", "h2"):
        pk.add(n, 16 * P, (lambda n: lambda a: blocks(np.asarray(a[f"L1_ffn_{n}_w"]).T))(n))
        pk.add(n + "s", 4, (lambda n: lambda a: column(a[f"L1_ffn_{n}_s"]))(n))
    pk.add("w3", 4 * P, lambda a: blocks(np.asarray(a["L1_ffn_w3_w"]).T))
    pk.add("out_scale", P, lambda a: np.broadcast_to(np.asarray(a["L1_ffn_w3_s"]), (P, P)))

    def l1f(nc, c, w):
        m1 = lambda t: (lambda k, m: t[:, (k * 4 + m) * P:(k * 4 + m + 1) * P])
        s1 = lambda t: (lambda m: t[:, m:m + 1])
        L = [Layer(1, 4, m1(w["w1"]), ACT.Silu, scale=s1(w["w1s"]), V=m1(w["w2"]), v_arg=s1(w["w2s"])),
             Layer(4, 4, m1(w["h1"]), ACT.Gelu, scale=s1(w["h1s"])),
             Layer(4, 4, m1(w["h2"]), ACT.Gelu, scale=s1(w["h2s"]))]
        mlp_phase(nc, c, "l1f", w, lambda e: L, lambda e: (4, lambda k: w["w3"][:, k * P:(k + 1) * P]), out_scale=True)
    out.append(("L1f", pk, l1f))
    h16 = stack_index(16) // 8
    col = lambda n, k: (lambda a: np.asarray(a[n])[:, k * D:(k + 1) * D])
    row = lambda n, k: (lambda a: np.asarray(a[n])[k * D:(k + 1) * D])
    pk = attention_pack(16, sc, V_("L2_attn_Wq"), V_("L2_attn_Wk"), V_("L2_attn_Wv"), V_("L2_attn_bq"), V_("L2_attn_bk"), V_("L2_attn_bv"))
    pk.add("mod", 4 * P, lambda a: np.asarray(a["L2_attn_cg_W"])[:, h16])
    pk.add("am", 4 * P, lambda a: rows_to(np.asarray(a["L2_attn_am_W"])[:, h16]))
    pk.add("cons", 1, lambda a: rows_to(np.asarray(a["L2_attn_cons_vec"])[:, None]))
    pk.add("cg_am_bias", 8, lambda a: np.concatenate([column(np.asarray(a["L2_attn_cg_b"])[h16]), column(np.asarray(a["L2_attn_am_b"])[h16])], 1))
    out.append(("L2m", pk, lambda nc, c, w: attention_phase(nc, c, "l2m", w, 16, sc, bias=True, modulated=True, finish="context")))
    s32 = f32(1 / np.sqrt(32.0))
    pk = attention_pack(4, s32, col("L2_attn_ca_Win", 0), col("L2_attn_ca_Win", 1), col("L2_attn_ca_Win", 2), row("L2_attn_ca_bin", 0), row("L2_attn_ca_bin", 1), row("L2_attn_ca_bin", 2))
    pk.add("causal_out", P, V_("L2_attn_ca_Wout"))
    pk.add("causal_out_b", P, lambda a: rows_to(a["L2_attn_ca_bout"]))
    out.append(("L2c", pk, lambda nc, c, w: attention_phase(nc, c, "l2c", w | {"mix": (1.0 - 0.7, 0.7)}, 4, s32, bias=True, out_steps=("causal_out",), finish="y")))
    meta = (0.9 - 0.8) / 0.2 * 0.3
    pk = attention_pack(4, s32, col("L2_attn_mc_Win", 0), col("L2_attn_mc_Win", 1), col("L2_attn_mc_Win", 2), row("L2_attn_mc_bin", 0), row("L2_attn_mc_bin", 1), row("L2_attn_mc_bin", 2))
    pk.add("meta_out", P, V_("L2_attn_mc_Wout"))
    pk.add("meta_out_b", P, lambda a: rows_to(a["L2_attn_mc_bout"]))
    pk.add("out", P, V_("L2_attn_Wo"))
    pk.add("out_b", P, lambda a: rows_to(a["L2_attn_bo"]))
    out.append(("L2t", pk, lambda nc, c, w: attention_phase(nc, c, "l2t", w | {"mix": (1.0 - meta, meta)}, 4, s32, bias=True, source="given", out_steps=("meta_out", "out"))))
    pk = Pack()
    out.append(("R1", None, lambda nc, c, w: reorder_phase(nc, c, "to_positions", True)))
    wq = lambda k: (lambda a: np.asarray(a["L2_ffn_Wqkv"])[k * D:(k + 1) * D].T)
    bq = lambda k: (lambda a: np.asarray(a["L2_ffn_bqkv"])[k * D:(k + 1) * D])
    pk = attention_pack(4, s32, wq(0), wq(1), wq(2), bq(0), bq(1), bq(2))
    pk.add("mixed", P, T_("L2_ffn_Wo"))
    pk.add("mixed_b", P, lambda a: rows_to(a["L2_ffn_bo"]))
    bcast = lambda n: (lambda a: np.broadcast_to(np.asarray(a[n]), (P, P)))
    pk.add("g1", P, bcast("L2_ffn_g1"))
    pk.add("be1", P, bcast("L2_ffn_be1"))
    out.append(("L2p", pk, lambda nc, c, w: attention_phase(nc, c, "l2p", w, 4, s32, bias=True, grouped=True, out_steps=("mixed",), finish="y")))
    pk = Pack()
    pk.add("W1", 32 * P, lambda a: np.asarray(a["L2_ffn_W1"]).transpose(1, 0, 2).reshape(P, -1))
    pk.add("W2", 32 * P, lambda a: np.asarray(a["L2_ffn_W2"]).reshape(32, P, D).transpose(1, 0, 2).reshape(P, -1))
    pk.add("b1", 32, lambda a: np.asarray(a["L2_ffn_b1"]).reshape(32, P).T)
    pk.add("gate", 8, T_("L2_ffn_Wg"))
    pk.add("expert_bias", P, lambda a: rows_to(a["L2_ffn_b2"]))
    pk.add("g2", P, bcast("L2_ffn_g2"))
    pk.add("be2", P, bcast("L2_ffn_be2"))

    def l2e(nc, c, w):
        w = w | {"expert_bias": w["expert_bias"][0:8, :]}
        blk = lambda t, k: t[:, k * P:(k + 1) * P]
        L = lambda e: [Layer(1, 4, lambda k, m: blk(w["W1"], 4 * e + m), ACT.Relu, bias=lambda m: w["b1"][:, 4 * e + m:4 * e + m + 1])]
        mlp_phase(nc, c, "l2e", w, L, lambda e: (4, lambda k: blk(w["W2"], 4 * e + k)), experts=8, source="y", gate="top1", tail_gain=True)
    out.append(("L2e", pk, l2e))
    out.append(("R2", None, lambda nc, c, w: reorder_phase(nc, c, "to_batches", False)))
    pk = Pack()
    pk.add("wq", P, T_("L3_attn_Wq"))
    pk.add("wk", P, T_("L3_attn_Wk"))
    pk.add("wv", P, T_("L3_attn_Wv"))
    pk.add("bq", 1, lambda a: column(a["L3_attn_bq"]))
    pk.add("bk_b", P, lambda a: rows_to(a["L3_attn_bk"]))
    pk.add("bv", P, lambda a: rows_to(a["L3_attn_bv"]))
    pk.add("gamma", P, bcast("L3_attn_gamma"))
    pk.add("beta", P, bcast("L3_attn_beta"))
    pk.add("same_head", P, lambda a: np.kron(np.eye(16), np.ones((8, 8))).astype(np.float32))
    pk.add("head_of", 16, lambda a: np.kron(np.eye(16), np.ones((8, 1))).astype(np.float32))
    out.append(("L3a", pk, lambda nc, c, w: linear_attention_phase(nc, c, "l3a", w)))
    pk = Pack()
    pk.add("Wg", P // 16, V_("L3_ffn_Wg"))
    for n in ("W11", "W12"):
        pk.add(n, 16 * P, (lambda n: lambda a: np.asarray(a[f"L3_ffn_{n}"]).transpose(1, 0, 2).reshape(P, -1))(n))
    pk.add("W2", 16 * P, lambda a: np.asarray(a["L3_ffn_W2"]).reshape(16, P, D).transpose(1, 0, 2).reshape(P, -1))

    def l3e(nc, c, w):
        w = w | {"gate": w["Wg"]}
        blk = lambda t, k: t[:, k * P:(k + 1) * P]
        L = lambda e: [Layer(1, 2, lambda k, m: blk(w["W11"], 2 * e + m), ACT.Silu, V=lambda k, m: blk(w["W12"], 2 * e + m))]
        mlp_phase(nc, c, "l3e", w, L, lambda e: (2, lambda k: blk(w["W2"], 2 * e + k)), experts=8, gate="top2")
    out.append(("L3e", pk, l3e))
    return out


def program(nc, consts, x, packs, out, phases):
    c = Chip()
    with ExitStack() as ctx:
        sb = lambda n, s, d=F32: ctx.enter_context(nc.sbuf_tensor(n, s, d))
        c.x = sb("x", [P, TILES + NT, D])
        c.y = sb("y", [P, TILES + NT, D])
        c.ctx = sb("ctx", [P, TILES + NT, D])
        c.ident = sb("ident", [P, P])
        c.ident_bf = sb("ident_bf", [P, P], BF16)
        c.later_keys = sb("later_keys", [P, P], BF16)
        c.earlier_queries = sb("earlier_queries", [P, P], BF16)
        c.other_groups = sb("other_groups", [P, P], BF16)
        c.far_keys = sb("far_keys", [P, P + 64], BF16)
        c.far_queries = sb("far_queries", [P, P + 64], BF16)
        c.minus_half16 = sb("minus_half16", [P, 16])
        c.down8 = sb("down8", [P, 8])
        c.shift = sb("shift", [P, 2, P])
        c.pick = sb("pick", [P, 8, P], F32R)
        c.ones = sb("ones", [1, P])
        c.minus_half = sb("minus_half", [P, NT])
        c.eps = sb("eps", [P, NT])
        c.bank = [ctx.enter_context(nc.psum_tensor(f"bank{k}", [P, 512], F32)) for k in range(8)]
        c.scratch = nc.dram_tensor("scratch", (B, T, D), F32, kind="Internal").ap()
        loads = [(pk, packs[name]) for name, pk, _ in phases if pk is not None]
        cols = [max([pk.cols for pk, _ in loads[k::2]] + [1]) for k in range(2)]
        tiles = lambda a: a.rearrange("b (j p) d -> p (b j) d", p=P)
        c.loaded = [ctx.enter_context(nc.semaphore(f"weights_loaded{k}")) for k in range(len(loads))]
        c.region_turn = 0
        with nc.sbuf_tensor("weights0", [P, cols[0]], F32) as r0, nc.sbuf_tensor("weights1", [P, cols[1]], F32) as r1:
            c.region = [r0, r1]
            setup_phase(nc, c, consts, tiles(x), *loads[0])
            n = 0
            for name, pk, build in phases:
                if pk is None:
                    build(nc, c, None)
                    continue
                c.next = loads[n + 1] if n + 1 < len(loads) else None
                build(nc, c, views(pk, c.region[n % 2], n))
                n += 1
        store_phase(nc, c, tiles(out))


def lay_out(pk, inputs):
    cols = []
    for n, lay in pk.host:
        a = np.asarray(lay(inputs))
        assert a.shape == (P, n), (a.shape, n)
        cols.append(a)
    return np.ascontiguousarray(np.concatenate(cols, 1))


def kernel(**inputs):
    from concourse import bacc
    from concourse.bass_utils import run_bass_kernel_spmd

    nc = bacc.Bacc("TRN2", target_bir_lowering=False, num_devices=1)
    nc.disable_value_cache = True
    phases = phase_list()
    arrays = {"x_in": np.ascontiguousarray(inputs["L0_attn_x"]), "consts": lay_out(CONSTS, inputs)}
    for name, pk, _ in phases:
        if pk is not None:
            arrays[f"w_{name}"] = lay_out(pk, inputs)
    aps = {n: nc.dram_tensor(n, a.shape, F32, kind="ExternalInput").ap() for n, a in arrays.items()}
    out = nc.dram_tensor("x_out", (B, T, D), F32, kind="ExternalOutput").ap()
    program(nc, aps["consts"], aps["x_in"], {p[0]: aps[f"w_{p[0]}"] for p in phases if p[1] is not None}, out, phases)
    return run_bass_kernel_spmd(nc, [arrays], core_ids=[0]).results[0]["x_out"]
```
